# Optimizing a Trainium2 kernel written in Bass

```python
import numpy as np
import jax
import jax.numpy as jnp

def _softmax(x, axis=-1):
    return jax.nn.softmax(x, axis=axis)

def _gelu(x):
    return jax.nn.gelu(x, approximate=True)

def _silu(x):
    return jax.nn.silu(x)

def _sigmoid(x):
    return jax.nn.sigmoid(x)

def _layernorm(x, axis=-1, eps=1e-05):
    m = jnp.mean(x, axis=axis, keepdims=True)
    v = jnp.var(x, axis=axis, keepdims=True)
    return (x - m) / jnp.sqrt(v + eps)

def _scatter_add(tgt, idx, src, axis=0):
    return tgt.at[idx].add(src)

def _segment_sum(src, seg, n):
    return jax.ops.segment_sum(src, seg, n)
kernel_name = 'mk_macaron_d2_jaxref_r8_a4b6ee'

def setup_inputs(seed: int=0):
    np.random.seed(seed)
    _w = jnp.asarray

    def _L0_attn_setup():
        import math
        import jax, jax.numpy as jnp
        import numpy as np
        B, T, D = (8, 256, 128)

        def _gelu(x):
            c = math.sqrt(2.0 / math.pi)
            return 0.5 * x * (1.0 + jnp.tanh(c * (x + 0.044715 * x * x * x)))

        def _normalize(x, axis):
            n = jnp.linalg.norm(x, axis=axis, keepdims=True)
            return x / jnp.maximum(n, 1e-12)
        key = jax.random.key(seed)
        k1, k2 = jax.random.split(key)
        x = jax.random.normal(k1, (B, T, D), dtype=jnp.float32)
        ema_out = _normalize(jax.random.normal(k2, (D,), dtype=jnp.float32), 0)[..., 0] if False else None
        ema = jax.random.normal(k2, (D,), dtype=jnp.float32)
        ema = ema / jnp.maximum(jnp.linalg.norm(ema), 1e-12)
        return {'x': x, 'ema_out': ema, 'logit_decay': jnp.float32(math.log(0.9 / 0.1)), 'log_tau': jnp.float32(math.log(2.0)), 'log_blend': jnp.float32(math.log(0.3 / 0.7)), 'logit_blend_seq': jnp.float32(0.0)}
    _L0_attn_in = _L0_attn_setup()

    def _L0_ffn_setup():
        import jax, jax.numpy as jnp
        import numpy as np
        NUM_EXPERTS = 8
        CAPACITY = 80
        key = jax.random.key(seed)
        ks = jax.random.split(key, 5)
        D, E, F = (128, NUM_EXPERTS, 512)
        inputs = jax.random.normal(ks[0], (2, 256, D), dtype=jnp.float32)
        gate_w = jax.random.normal(ks[1], (D, E), dtype=jnp.float32) * 0.02
        gate_b = jnp.zeros((E,), dtype=jnp.float32)
        w1 = jax.random.normal(ks[2], (E, D, F), dtype=jnp.float32) * 0.02
        b1 = jnp.zeros((E, F), dtype=jnp.float32)
        w2 = jax.random.normal(ks[3], (E, F, D), dtype=jnp.float32) * 0.02
        b2 = jnp.zeros((E, D), dtype=jnp.float32)
        return {'inputs': inputs, 'gate_w': gate_w, 'gate_b': gate_b, 'w1': w1, 'b1': b1, 'w2': w2, 'b2': b2}
    _L0_ffn_in = _L0_ffn_setup()

    def _L1_attn_setup():
        import jax, jax.numpy as jnp
        import numpy as np
        LN_EPS = 1e-05
        key = jax.random.key(seed)
        k0, k1, k2, k3 = jax.random.split(key, 4)
        B, T, D = (8, 256, 128)
        x = jax.random.normal(k0, (B, T, D), dtype=jnp.float32)
        u = jax.random.normal(k1, (D,), dtype=jnp.float32) * 0.1
        W = jax.random.normal(k2, (3 * D, D), dtype=jnp.float32) * (1.0 / np.sqrt(D))
        b = jax.random.normal(k3, (3 * D,), dtype=jnp.float32) * 0.01
        gamma = jnp.ones((D,), dtype=jnp.float32)
        beta = jnp.zeros((D,), dtype=jnp.float32)
        return {'x': x, 'u': u, 'W': W, 'b': b, 'gamma': gamma, 'beta': beta}
    _L1_attn_in = _L1_attn_setup()

    def _L1_ffn_setup():
        import jax, jax.numpy as jnp
        import numpy as np
        B, L, M = (4, 256, 128)
        G, E = (8, 8)
        CAP_FACTOR = 2.0

        def _ffn_size(m, widening=8.0):
            f = int(widening * m) * 2 // 3
            return f + (8 - f) % 8
        H = _ffn_size(M)

        def _gating_top2(logits, C):
            Gd, Sd, Ed = logits.shape
            raw = jax.nn.softmax(logits, axis=-1)
            idx1 = jnp.argmax(raw, axis=-1)
            m1 = jax.nn.one_hot(idx1, Ed, dtype=logits.dtype)
            gate1 = jnp.sum(raw * m1, axis=-1)
            rest = raw * (1.0 - m1)
            idx2 = jnp.argmax(rest, axis=-1)
            m2 = jax.nn.one_hot(idx2, Ed, dtype=logits.dtype)
            gate2 = jnp.sum(rest * m2, axis=-1)
            p1 = jnp.cumsum(m1, axis=-2) - m1
            m1 = m1 * (p1 < C).astype(m1.dtype)
            p1 = jnp.sum(p1 * m1, axis=-1)
            m1_flat = jnp.sum(m1, axis=-1)
            m1_count = jnp.sum(m1, axis=-2)
            p2 = jnp.cumsum(m2, axis=-2) - m2 + m1_count[:, None, :]
            m2 = m2 * (p2 < C).astype(m2.dtype)
            p2 = jnp.sum(p2 * m2, axis=-1)
            m2_flat = jnp.sum(m2, axis=-1)
            gate1 = gate1 * m1_flat
            gate2 = gate2 * m2_flat
            c1 = (gate1[..., None] * jax.nn.one_hot(idx1, Ed, dtype=jnp.float32))[..., None] * jax.nn.one_hot(p1.astype(jnp.int32), C, dtype=jnp.float32)[:, :, None, :]
            c2 = (gate2[..., None] * jax.nn.one_hot(idx2, Ed, dtype=jnp.float32))[..., None] * jax.nn.one_hot(p2.astype(jnp.int32), C, dtype=jnp.float32)[:, :, None, :]
            combine = (c1 + c2).astype(logits.dtype)
            dispatch = (combine != 0).astype(logits.dtype)
            return (dispatch, combine)
        key = jax.random.key(seed)
        k0, k1, k2, k3, k4 = jax.random.split(key, 5)
        return {'inputs': jax.random.normal(k0, (B, L, M), jnp.float32), 'router_w': jax.random.normal(k1, (M, E), jnp.float32) * 0.02, 'w0_kernel': jax.random.normal(k2, (E, M, H), jnp.float32) * 0.02, 'w1_kernel': jax.random.normal(k3, (E, M, H), jnp.float32) * 0.02, 'wo_kernel': jax.random.normal(k4, (E, H, M), jnp.float32) * 0.02}
    _L1_ffn_in = _L1_ffn_setup()
    _d = {'L0_attn_x': _L0_attn_in['x'], 'L0_attn_ema_out': _L0_attn_in['ema_out'], 'L0_attn_logit_decay': _L0_attn_in['logit_decay'], 'L0_attn_log_tau': _L0_attn_in['log_tau'], 'L0_attn_log_blend': _L0_attn_in['log_blend'], 'L0_attn_logit_blend_seq': _L0_attn_in['logit_blend_seq'], 'L0_ffn_gate_w': _L0_ffn_in['gate_w'], 'L0_ffn_gate_b': _L0_ffn_in['gate_b'], 'L0_ffn_w1': _L0_ffn_in['w1'], 'L0_ffn_b1': _L0_ffn_in['b1'], 'L0_ffn_w2': _L0_ffn_in['w2'], 'L0_ffn_b2': _L0_ffn_in['b2'], 'L1_attn_u': _L1_attn_in['u'], 'L1_attn_W': _L1_attn_in['W'], 'L1_attn_b': _L1_attn_in['b'], 'L1_attn_gamma': _L1_attn_in['gamma'], 'L1_attn_beta': _L1_attn_in['beta'], 'L1_ffn_router_w': _L1_ffn_in['router_w'], 'L1_ffn_w0_kernel': _L1_ffn_in['w0_kernel'], 'L1_ffn_w1_kernel': _L1_ffn_in['w1_kernel'], 'L1_ffn_wo_kernel': _L1_ffn_in['wo_kernel']}
    _x0 = _d['L0_attn_x']
    _d['L0_attn_x'] = jax.random.normal(jax.random.fold_in(jax.random.key(seed), 1), (8, 512, 128), dtype=_x0.dtype)
    del _x0
    return _d

def reference(L0_attn_x, L0_attn_ema_out, L0_attn_logit_decay, L0_attn_log_tau, L0_attn_log_blend, L0_attn_logit_blend_seq, L0_ffn_gate_w, L0_ffn_gate_b, L0_ffn_w1, L0_ffn_b1, L0_ffn_w2, L0_ffn_b2, L1_attn_u, L1_attn_W, L1_attn_b, L1_attn_gamma, L1_attn_beta, L1_ffn_router_w, L1_ffn_w0_kernel, L1_ffn_w1_kernel, L1_ffn_wo_kernel):

    def _L0_attn_ref(x, ema_out, logit_decay, log_tau, log_blend, logit_blend_seq):
        import math
        import jax, jax.numpy as jnp
        import numpy as np
        B, T, D = (8, 256, 128)

        def _gelu(x):
            c = math.sqrt(2.0 / math.pi)
            return 0.5 * x * (1.0 + jnp.tanh(c * (x + 0.044715 * x * x * x)))

        def _normalize(x, axis):
            n = jnp.linalg.norm(x, axis=axis, keepdims=True)
            return x / jnp.maximum(n, 1e-12)
        Bx, Tx, Dx = x.shape
        tau = jnp.exp(log_tau)
        alpha = jax.nn.sigmoid(log_blend)
        w_seq = jax.nn.sigmoid(logit_blend_seq)
        out = _gelu(x)
        out_norm = _normalize(out, -1)
        ema_norm = ema_out / jnp.maximum(jnp.linalg.norm(ema_out), 1e-12)
        ema_sim = jnp.einsum('btd,d->bt', out_norm, ema_norm)
        sim_mat = jnp.einsum('btd,bsd->bts', out_norm, out_norm)
        causal = jnp.tril(jnp.ones((Tx, Tx), dtype=bool), k=-1)
        sim_past = jnp.where(causal[None], sim_mat, -2.0)
        seq_sim = jnp.max(sim_past, axis=-1)
        has_past = (jnp.arange(Tx) > 0)[None, :]
        seq_sim = jnp.where(has_past, seq_sim, ema_sim)
        familiarity = w_seq * seq_sim + (1.0 - w_seq) * ema_sim
        novelty = jnp.exp(-tau * familiarity)
        gate = 1.0 - alpha + alpha * novelty
        return out * gate[..., None]

    def _L0_ffn_ref(inputs, gate_w, gate_b, w1, b1, w2, b2):
        import jax, jax.numpy as jnp
        import numpy as np
        NUM_EXPERTS = 8
        CAPACITY = 80
        D = inputs.shape[-1]
        tokens = inputs.reshape(-1, D)
        logits = tokens @ gate_w + gate_b
        probs = jax.nn.softmax(logits, axis=-1)
        expert_idx = jnp.argmax(probs, axis=-1)
        mask1 = jax.nn.one_hot(expert_idx, NUM_EXPERTS, dtype=jnp.float32)
        pos = jnp.sum(jnp.cumsum(mask1, axis=0) * mask1, axis=-1) - 1.0
        pos = pos.astype(jnp.int32)
        keep = (pos < CAPACITY).astype(jnp.float32)
        gate_prob = jnp.sum(probs * mask1, axis=-1)
        pos_oh = jax.nn.one_hot(pos, CAPACITY, dtype=jnp.float32)
        sec_mask = mask1[:, :, None] * pos_oh[:, None, :] * keep[:, None, None]
        combine_weights = sec_mask * gate_prob[:, None, None]
        dispatch = jnp.einsum('nec,nd->ecd', sec_mask, tokens)
        h = jax.nn.gelu(jnp.einsum('ecd,edf->ecf', dispatch, w1) + b1[:, None, :])
        expert_out = jnp.einsum('ecf,efd->ecd', h, w2) + b2[:, None, :]
        out = jnp.einsum('nec,ecd->nd', combine_weights, expert_out)
        return out.reshape(inputs.shape)

    def _L1_attn_ref(x, u, W, b, gamma, beta):
        import jax, jax.numpy as jnp
        import numpy as np
        LN_EPS = 1e-05
        B, T, D = x.shape
        mean = jnp.mean(x, axis=-1, keepdims=True)
        var = jnp.var(x, axis=-1, keepdims=True)
        xn = (x - mean) * jax.lax.rsqrt(var + LN_EPS) * gamma + beta
        proj = jnp.einsum('btd,ed->bte', xn, W) + b
        cand, g_z, g_r = jnp.split(proj, 3, axis=-1)
        z = jax.nn.sigmoid(g_z)
        r = jax.nn.sigmoid(g_r)

        def step(s, inp):
            c_t, z_t, r_t = inp
            h_tilde = jnp.tanh(c_t + r_t * (u * s))
            s_new = z_t * s + (1.0 - z_t) * h_tilde
            return (s_new, s_new)
        s0 = jnp.zeros((B, D), dtype=x.dtype)
        _, ys = jax.lax.scan(step, s0, (cand.transpose(1, 0, 2), z.transpose(1, 0, 2), r.transpose(1, 0, 2)))
        return ys.transpose(1, 0, 2)

    def _L1_ffn_ref(inputs, router_w, w0_kernel, w1_kernel, wo_kernel):
        import jax, jax.numpy as jnp
        import numpy as np
        B, L, M = (4, 256, 128)
        G, E = (8, 8)
        CAP_FACTOR = 2.0

        def _ffn_size(m, widening=8.0):
            f = int(widening * m) * 2 // 3
            return f + (8 - f) % 8
        H = _ffn_size(M)

        def _gating_top2(logits, C):
            Gd, Sd, Ed = logits.shape
            raw = jax.nn.softmax(logits, axis=-1)
            idx1 = jnp.argmax(raw, axis=-1)
            m1 = jax.nn.one_hot(idx1, Ed, dtype=logits.dtype)
            gate1 = jnp.sum(raw * m1, axis=-1)
            rest = raw * (1.0 - m1)
            idx2 = jnp.argmax(rest, axis=-1)
            m2 = jax.nn.one_hot(idx2, Ed, dtype=logits.dtype)
            gate2 = jnp.sum(rest * m2, axis=-1)
            p1 = jnp.cumsum(m1, axis=-2) - m1
            m1 = m1 * (p1 < C).astype(m1.dtype)
            p1 = jnp.sum(p1 * m1, axis=-1)
            m1_flat = jnp.sum(m1, axis=-1)
            m1_count = jnp.sum(m1, axis=-2)
            p2 = jnp.cumsum(m2, axis=-2) - m2 + m1_count[:, None, :]
            m2 = m2 * (p2 < C).astype(m2.dtype)
            p2 = jnp.sum(p2 * m2, axis=-1)
            m2_flat = jnp.sum(m2, axis=-1)
            gate1 = gate1 * m1_flat
            gate2 = gate2 * m2_flat
            c1 = (gate1[..., None] * jax.nn.one_hot(idx1, Ed, dtype=jnp.float32))[..., None] * jax.nn.one_hot(p1.astype(jnp.int32), C, dtype=jnp.float32)[:, :, None, :]
            c2 = (gate2[..., None] * jax.nn.one_hot(idx2, Ed, dtype=jnp.float32))[..., None] * jax.nn.one_hot(p2.astype(jnp.int32), C, dtype=jnp.float32)[:, :, None, :]
            combine = (c1 + c2).astype(logits.dtype)
            dispatch = (combine != 0).astype(logits.dtype)
            return (dispatch, combine)
        Bb, Ll, Mm = inputs.shape
        S = Bb * Ll // G
        x = inputs.reshape(G, S, Mm)
        logits = jnp.einsum('GSM,ME->GSE', x, router_w)
        cap = int(CAP_FACTOR * S / E)
        C = (cap + 3) // 4 * 4
        dispatch, combine = _gating_top2(logits, C)
        expert_inputs = jnp.einsum('GSEC,GSM->EGCM', dispatch, x)
        layer_w0 = jnp.einsum('EGCM,EMH->EGCH', expert_inputs, w0_kernel)
        layer_w1 = jnp.einsum('EGCM,EMH->EGCH', expert_inputs, w1_kernel)
        hidden = jax.nn.gelu(layer_w0, approximate=True) * layer_w1
        expert_outputs = jnp.einsum('EGCH,EHM->EGCM', hidden, wo_kernel)
        out = jnp.einsum('EGCM,GSEC->GSM', expert_outputs, combine)
        return out.reshape(Bb, Ll, Mm)
    x = L0_attn_x
    x = x + 0.5 * _L0_ffn_ref(_layernorm(x, axis=-1), L0_ffn_gate_w, L0_ffn_gate_b, L0_ffn_w1, L0_ffn_b1, L0_ffn_w2, L0_ffn_b2)
    x = x + _L0_attn_ref(_layernorm(x, axis=-1), L0_attn_ema_out, L0_attn_logit_decay, L0_attn_log_tau, L0_attn_log_blend, L0_attn_logit_blend_seq)
    x = x + 0.5 * _L0_ffn_ref(_layernorm(x, axis=-1), L0_ffn_gate_w, L0_ffn_gate_b, L0_ffn_w1, L0_ffn_b1, L0_ffn_w2, L0_ffn_b2)
    x = x + 0.5 * _L1_ffn_ref(_layernorm(x, axis=-1), L1_ffn_router_w, L1_ffn_w0_kernel, L1_ffn_w1_kernel, L1_ffn_wo_kernel)
    x = x + _L1_attn_ref(_layernorm(x, axis=-1), L1_attn_u, L1_attn_W, L1_attn_b, L1_attn_gamma, L1_attn_beta)
    x = x + 0.5 * _L1_ffn_ref(_layernorm(x, axis=-1), L1_ffn_router_w, L1_ffn_w0_kernel, L1_ffn_w1_kernel, L1_ffn_wo_kernel)
    return x

_drawn_inputs = setup_inputs


def setup_inputs(seed=0):
    import zlib

    import numpy as np

    out = dict(_drawn_inputs(seed))
    spreads = {'L0_ffn_gate_b': (0.0, 0.8),
     'L0_ffn_b1': (0.0, 0.8),
     'L0_ffn_b2': (0.0, 0.8),
     'L1_attn_gamma': (1.0, 0.2),
     'L1_attn_beta': (0.0, 0.1)}
    factors = {'L0_attn_ema_out': 8.0,
     'L0_ffn_gate_w': 8.0,
     'L0_ffn_w1': 8.0,
     'L0_ffn_w2': 8.0,
     'L1_attn_u': 8.0,
     'L1_attn_b': 8.0,
     'L1_ffn_router_w': 8.0,
     'L1_ffn_w0_kernel': 8.0,
     'L1_ffn_w1_kernel': 8.0,
     'L1_ffn_wo_kernel': 8.0}
    for name, (base, spread) in spreads.items():
        noise = np.random.default_rng([zlib.crc32(name.encode()), seed]).standard_normal(out[name].shape)
        drawn = base * np.exp(spread * noise) if base else spread * noise
        out[name] = jnp.asarray(drawn.astype(out[name].dtype))
    for name, factor in factors.items():
        out[name] = (out[name] * factor).astype(out[name].dtype)
    return out
```

```python
from contextlib import ExitStack

import concourse.bass as bass
from concourse import mybir

F32 = mybir.dt.float32
F16 = mybir.dt.float16
BF16 = mybir.dt.bfloat16
I32 = mybir.dt.int32
U32 = mybir.dt.uint32
ALU = mybir.AluOpType
ACT = mybir.ActivationFunctionType
AX = mybir.AxisListType.X

P = 128
D = 128
B, T = 8, 512
NT = B * T // P
TPB = T // P
E = 8
LN_EPS = 1e-5

CAP0 = 80
F0 = 512
FC0 = F0 // P

CAP1 = 128
H1 = 688
HC1 = -(-H1 // P)
HREST = H1 - (HC1 - 1) * P
HALF = B // 2
SLOTS1 = B * E * CAP1
SKIP = 1 << 16

CH = 128
NCH = T // CH


def flat(ap):
    return ap.rearrange("p a b -> p (a b)")


def after(eng, sem, value):
    if not (isinstance(value, int) and value <= 0):
        eng.wait_ge(sem, value)


def twice_each(eng, n, body):
    for u in range(2):
        body(0, u)
    with eng.Fori(1, n) as i:
        for u in range(2):
            body(i, u)


class Chain:

    def __init__(self, eng, sem):
        self.eng, self.sem, self.n = eng, sem, 0

    def __call__(self, instruction):
        self.n += 1
        instruction.then_inc(self.sem, 1)
        self.eng.wait_ge(self.sem, self.n)


class Stage:

    used = []

    def __init__(self, nc, ctx, name):
        self.nc, self.ctx, self.name = nc, ctx, name

    def sb(self, name, shape, dt=F32):
        return self.ctx.enter_context(self.nc.sbuf_tensor(f"{self.name}_{name}", shape, dt))

    def ps(self, name, shape, dt=F32):
        return self.ctx.enter_context(self.nc.psum_tensor(f"{self.name}_{name}", shape, dt))

    def sem(self, name):
        handle = self.nc.alloc_semaphore(f"{self.name}_{name}")
        Stage.used.append(handle)
        return handle

    def block(self):
        return self.ctx.enter_context(self.nc.Block())


def recycle(nc):
    nc.clear_and_free_semaphores(list(Stage.used))
    Stage.used.clear()
    nc.all_engine_barrier()


def setup(nc, k, dram):
    with ExitStack() as ctx:
        st = Stage(nc, ctx, "set")
        zeros = st.sb("zeros", [P, 16 * D])
        wide = st.sb("wide", [P, NT], I32)
        iota = st.sb("iota", [P, E * CAP0], I32)
        ids = st.sb("ids", [P, 3, NT], I32)
        bcol = st.sb("bcol", [E * FC0, P])
        wrows = st.sb("wrows", [P, 3, D])
        scal = st.sb("scal", [P, 8])
        nscal = st.sb("nscal", [P, 8])
        ema = st.sb("ema", [P, 4])
        pt = st.ps("pt", [P, 512])
        pe_ = st.ps("pe", [P, 512])
        s_load = st.sem("load")
        s_zero = st.sem("zero")
        s_zdma = st.sem("zdma")
        s_pool = st.sem("pool")
        s_iota = st.sem("iota")
        s_tr = st.sem("tr")
        s_sum = st.sem("sum")
        s_act = st.sem("act")
        s_vec = st.sem("vec")
        block = st.block()
        LOADS = 16 * 12

        @block.sync
        def _(sp):
            sp.dma_start(k.X[:, :, :], dram.x.rearrange("b (j p) d -> p (b j) d", p=P)).then_inc(s_load, 16)
            sp.dma_start(k.GW0[:, :], dram.gate_w).then_inc(s_load, 16)
            sp.dma_start(k.RW1[:, :], dram.router_w).then_inc(s_load, 16)
            sp.dma_start(k.GB0[0:1, 0, :], dram.gate_b.rearrange("(a e) -> a e", a=1)).then_inc(s_load, 16)
            sp.dma_start(k.B2[0:1, :], dram.b2.rearrange("(a e) d -> a (e d)", a=1)).then_inc(s_load, 16)
            sp.dma_start(bcol[:, :], dram.b1.rearrange("e (c p) -> (e c) p", p=P)).then_inc(s_load, 16)
            sp.dma_start(wrows[:, :, :], dram.W.rearrange("(c p) d -> p c d", p=P)).then_inc(s_load, 16)
            with nc.allow_non_contiguous_dma("a few columns of one word"):
                sp.dma_start(ema[:, 0:1], dram.ema.rearrange("(p a) -> p a", a=1)).then_inc(s_load, 16)
                cols = k.COLS[:, :]
                sp.dma_start(cols[:, 0:1], dram.u.rearrange("(p a) -> p a", a=1)).then_inc(s_load, 16)
                sp.dma_start(cols[:, 1:2], dram.gamma.rearrange("(p a) -> p a", a=1)).then_inc(s_load, 16)
                sp.dma_start(cols[:, 2:3], dram.beta.rearrange("(p a) -> p a", a=1)).then_inc(s_load, 16)
                sp.dma_start(cols[:, 3:6], dram.b.rearrange("(c p) -> p c", p=P)).then_inc(s_load, 16)
            sp.wait_ge(s_zero, 1)
            rows = 16 * P
            for y in dram.expert_in + dram.delta0:
                for n in range(NT // 16):
                    sp.dma_start(y[n * rows:(n + 1) * rows, :].rearrange("(p a) d -> p (a d)", p=P),
                                 zeros[:, :]).then_inc(s_zdma, 16)
            sp.wait_ge(s_zdma, 16 * 4 * (NT // 16))

        @block.scalar
        def _(act):
            for n, name in enumerate((dram.log_tau, dram.log_blend, dram.logit_blend_seq)):
                act.dma_start(scal[:, n:n + 1], name.rearrange("(a e) -> a e", a=1).to_broadcast([P, 1]))\
                   .then_inc(s_act, 16)
            act.wait_ge(s_act, 48)
            nc.scalar.activation(nscal[:, 0:1], scal[:, 0:1], ACT.Exp).then_inc(s_act, 1)
            nc.scalar.activation(nscal[:, 1:3], scal[:, 1:3], ACT.Exp, scale=-1.0).then_inc(s_act, 1)
            act.wait_ge(s_tr, 1)
            nc.scalar.copy(k.B1T[:, :], pt[:, 0:E * FC0]).then_inc(s_act, 1)
            nc.scalar.copy(k.WT[:, :], pt[:, P:P + 3 * P]).then_inc(s_act, 1)
            act.wait_ge(s_sum, 1)
            nc.scalar.activation(ema[:, 2:3], pe_[:, 0:1], ACT.Sqrt).then_inc(s_act, 1)

        @block.gpsimd
        def _(pool):
            nc.gpsimd.memset(k.IDENT[:, :], 1.0).then_inc(s_iota, 1)
            nc.gpsimd.memset(k.TRIU[:, :], 1.0).then_inc(s_iota, 1)
            nc.gpsimd.memset(k.ONESB[:, :], 1.0).then_inc(s_iota, 1)
            nc.gpsimd.memset(k.ONES[:, :], 1.0).then_inc(s_iota, 1)
            nc.gpsimd.memset(k.PAST[:, :], 0.0).then_inc(s_iota, 1)
            nc.gpsimd.memset(k.FIRST[:, :], -4.0).then_inc(s_iota, 1)
            nc.gpsimd.memset(k.RESET[:, :], 1.0).then_inc(s_iota, 1)
            nc.gpsimd.iota(iota[:, :], pattern=[[1, E * CAP0]], base=0, channel_multiplier=0).then_inc(s_iota, 1)
            nc.gpsimd.iota(wide[:, :], pattern=[[0, 2], [CAP1, HALF], [0, TPB]],
                           base=E * HALF * CAP1 - 1, channel_multiplier=0).then_inc(s_iota, 1)
            nc.gpsimd.iota(ids[:, 0, :], pattern=[[1, NT]], base=0, channel_multiplier=0).then_inc(s_iota, 1)
            nc.gpsimd.iota(ids[:, 1, :], pattern=[[0, NT]], base=0, channel_multiplier=1).then_inc(s_iota, 1)
            nc.gpsimd.iota(ids[:, 2, :], pattern=[[0, NT]], base=1, channel_multiplier=0).then_inc(s_iota, 1)
            for e in range(E):
                nc.gpsimd.memset(k.RANK[:, e:e + 1], float(E - e)).then_inc(s_iota, 1)
            pool.wait_ge(s_iota, 12 + E)
            nc.gpsimd.affine_select(out=k.IDENT[:, :], in_=k.IDENT[:, :], compare_op=ALU.is_equal, fill=0.0,
                                    base=0, pattern=[[-1, P]], channel_multiplier=1).then_inc(s_pool, 1)
            nc.gpsimd.affine_select(out=k.TRIU[:, :], in_=k.TRIU[:, :], compare_op=ALU.is_ge, fill=0.0,
                                    base=0, pattern=[[1, P]], channel_multiplier=-1).then_inc(s_pool, 1)
            nc.gpsimd.affine_select(out=k.PAST[:, :], in_=k.PAST[:, :], compare_op=ALU.is_gt,
                                    fill=-4.0, base=0, pattern=[[-1, P]], channel_multiplier=1).then_inc(s_pool, 1)
            nc.gpsimd.memset(k.FIRST[0:1, 0:NT:TPB], 0.0).then_inc(s_pool, 1)
            nc.gpsimd.memset(k.RESET[:, 0:E * NT:NT], 0.0).then_inc(s_pool, 1)

        @block.vector
        def _(dve):
            link = Chain(dve, s_vec)
            nc.vector.memset(zeros[:, :], 0.0).then_inc(s_zero, 1)
            dve.wait_ge(s_pool, 5)
            nc.vector.tensor_copy(k.IDENTB[:, :], k.IDENT[:, :]).then_inc(s_zero, 1)
            link(nc.vector.tensor_copy(k.IOTA[:, :], iota[:, :]))
            link(nc.vector.tensor_copy(k.BASE[:, :], wide[:, :]))
            link(nc.vector.tensor_copy(k.IDS[:, :, :], ids[:, :, :].rearrange("p a t -> p t a")))
            dve.wait_ge(s_load, LOADS)
            for t in range(1, NT):
                nc.vector.tensor_copy(k.GB0[0:1, t, :], k.GB0[0:1, 0, :]).then_inc(s_zero, 1)
            link(nc.vector.tensor_tensor(ema[:, 1:2], ema[:, 0:1], ema[:, 0:1], ALU.mult))
            dve.wait_ge(s_act, 50)
            link(nc.vector.tensor_scalar(k.SCAL[:, 0:1], nscal[:, 0:1], -1.0, None, ALU.mult))
            link(nc.vector.tensor_scalar(nscal[:, 1:3], nscal[:, 1:3], 1.0, None, ALU.add))
            link(nc.vector.reciprocal(k.SCAL[:, 1:3], nscal[:, 1:3]))
            link(nc.vector.tensor_scalar(k.SCAL[:, 3:5], k.SCAL[:, 1:3], -1.0, 1.0, ALU.mult, ALU.add))
            dve.wait_ge(s_act, 53)
            link(nc.vector.tensor_scalar(ema[:, 2:3], ema[:, 2:3], 1e-12, None, ALU.max))
            link(nc.vector.reciprocal(ema[:, 3:4], ema[:, 2:3]))
            link(nc.vector.tensor_tensor(k.EMA[:, 0:1], ema[:, 0:1], ema[:, 3:4], ALU.mult))

        @block.tensor
        def _(pe):
            pe.wait_ge(s_load, LOADS)
            pe.wait_ge(s_pool, 5)
            nc.tensor.transpose(pt[:, 0:E * FC0], bcol[:, :], k.IDENT[0:E * FC0, 0:E * FC0])
            for c in range(3):
                last = nc.tensor.transpose(pt[:, P + c * P:P + (c + 1) * P], wrows[:, c, :], k.IDENT[:, :])
            last.then_inc(s_tr, 1)
            pe.wait_ge(s_vec, 4)
            nc.tensor.matmul(pe_[:, 0:1], k.ONES[:, :], ema[:, 1:2], start=True, stop=True).then_inc(s_sum, 1)


def statistics(nc, st, dve, link, k):
    s_bn = st.sem("bn")
    with dve.Fori(0, NT // 8) as i:
        for u in range(8):
            nc.vector.bn_stats(k.BN[:, i * 8 + u, :], k.X[:, i * 8 + u, :]).then_inc(s_bn, 1)
    dve.wait_ge(s_bn, NT)
    link(nc.vector.tensor_tensor(k.ST[:, 0, :], k.BN[:, :, 1], k.BN[:, :, 4], ALU.add))
    link(nc.vector.tensor_tensor(k.ST[:, 1, :], k.BN[:, :, 1], k.BN[:, :, 4], ALU.subtract))
    link(nc.vector.tensor_tensor(k.ST[:, 2, :], k.BN[:, :, 2], k.BN[:, :, 5], ALU.add))
    link(nc.vector.tensor_scalar(k.MEAN[:, :], k.ST[:, 0, :], 0.5, None, ALU.mult))
    link(nc.vector.tensor_tensor(k.ST[:, 0, :], k.ST[:, 1, :], k.ST[:, 1, :], ALU.mult))
    link(nc.vector.tensor_scalar(k.ST[:, 2, :], k.ST[:, 2, :], 1.0 / D, LN_EPS, ALU.mult, ALU.add))
    link(nc.vector.scalar_tensor_tensor(out=k.VARE[:, :], in0=k.ST[:, 0, :], scalar=0.25, in1=k.ST[:, 2, :],
                                        op0=ALU.mult, op1=ALU.add))


def normalize(nc, name, k, weights=None, rows=None, keep=None, keep_t=None, bias=None):
    with ExitStack() as ctx:
        st = Stage(nc, ctx, name)
        xns = [st.sb(f"xns{u}", [P, TPB, D]) for u in range(2)]
        xts = [st.sb(f"xts{u}", [P, T]) for u in range(2)]
        psT = [st.ps(f"psT{u}", [P, T]) for u in range(2)]
        s_vec = st.sem("vec")
        s_std = st.sem("std")
        s_xn = st.sem("xn")
        s_kept = st.sem("kept")
        s_store = [st.sem(f"store{u}") for u in range(2)]
        s_tr = st.sem("tr")
        s_xt = st.sem("xt")
        s_lg = st.sem("lg")

        block = st.block()

        @block.vector
        def _(dve):
            link = Chain(dve, s_vec)
            statistics(nc, st, dve, link, k)
            dve.wait_ge(s_std, 1)
            link(nc.vector.reciprocal(k.RSTD[:, :], k.ST[:, 0, :]))

            def norm(i, u):
                b = 2 * i + u
                after(dve, s_tr, b - 1)
                if rows is not None:
                    after(dve, s_store[u], 16 * i)
                if keep is not None:
                    after(dve, s_kept, b - 1)
                for j in range(TPB):
                    t = b * TPB + j
                    nc.vector.tensor_scalar(xns[u][:, j, :], k.X[:, t, :], k.MEAN[:, bass.ds(t, 1)],
                                            k.RSTD[:, bass.ds(t, 1)], ALU.subtract, ALU.mult).then_inc(s_xn, 1)

            twice_each(dve, B // 2, norm)

        @block.scalar
        def _(act):
            act.wait_ge(s_vec, 7)
            nc.scalar.activation(k.ST[:, 0, :], k.VARE[:, :], ACT.Sqrt).then_inc(s_std, 1)

            def evacuate(i, u):
                b = 2 * i + u
                if keep_t is None:
                    after(act, s_lg, b - 1)
                act.wait_ge(s_tr, b + 1)
                if keep_t is None:
                    nc.scalar.copy(xts[u][:, :], psT[u][:, :]).then_inc(s_xt, 1)
                else:
                    nc.scalar.activation(keep_t[:, bass.ds(b * T, T)], psT[u][:, :], ACT.Identity,
                                         bias=k.COLS[:, 2:3], scale=k.COLS[:, 1:2]).then_inc(s_xt, 1)

            twice_each(act, B // 2, evacuate)

        if keep is not None:
            @block.gpsimd
            def _(pool):
                def copy(i, u):
                    b = 2 * i + u
                    pool.wait_ge(s_xn, TPB * (b + 1))
                    nc.gpsimd.tensor_copy(keep[:, bass.ds(b * TPB, TPB), :], xns[u][:, :, :]).then_inc(s_kept, 1)

                twice_each(pool, B // 2, copy)

        if rows is not None:
            @block.sync
            def _(sp):
                def store(i, u):
                    b = 2 * i + u
                    sp.wait_ge(s_xn, TPB * (b + 1))
                    sp.dma_start(rows[bass.ds(b * T, T), :].rearrange("(j p) d -> p j d", p=P),
                                 xns[u][:, :, :]).then_inc(s_store[u], 16)

                twice_each(sp, B // 2, store)
                for u in range(2):
                    sp.wait_ge(s_store[u], 16 * B // 2)

        @block.tensor
        def _(pe):
            if weights is not None:
                if bias is not None:
                    nc.tensor.matmul(k.psL[:, 0:NT * E], k.ONES[0:1, :], bias, start=True, stop=False,
                                     skip_group_check=True)

            def turn(i, u):
                b = 2 * i + u
                pe.wait_ge(s_xn, TPB * (b + 1))
                after(pe, s_xt, b - 1)
                for j in range(TPB):
                    last = nc.tensor.transpose(psT[u][:, j * P:(j + 1) * P], xns[u][:, j, :], k.IDENT[:, :])
                last.then_inc(s_tr, 1)
                if weights is None:
                    return
                pe.wait_ge(s_xt, b + 1)
                for j in range(TPB):
                    last = nc.tensor.matmul(k.psL[:, bass.ds((b * TPB + j) * E, E)], xts[u][:, j * P:(j + 1) * P],
                                            weights, start=bias is None, stop=True, skip_group_check=True)
                last.then_inc(s_lg, 1)

            twice_each(pe, B // 2, turn)


def softmax_over_experts(nc, dve, link, k, w, s_exp):
    L = k.psL[:, 0:NT * E].rearrange("p (t e) -> p t e", e=E)
    over = lambda v: v.unsqueeze(2).to_broadcast([P, NT, E])
    link(nc.vector.tensor_reduce(w.m[:, :], L, AX, ALU.max))
    link(nc.vector.tensor_tensor(w.p[:, :, :], L, over(w.m[:, :]), ALU.subtract))
    dve.wait_ge(s_exp, 1)
    link(nc.vector.tensor_reduce(w.m[:, :], w.q[:, :, :], AX, ALU.add))
    link(nc.vector.reciprocal(w.r[:, :], w.m[:, :]))
    link(nc.vector.tensor_tensor(w.p[:, :, :], w.q[:, :, :], over(w.r[:, :]), ALU.mult))


def first_largest(nc, link, k, w, p, value, rank, mask):
    over = lambda v: v.unsqueeze(2).to_broadcast([P, NT, E])
    ranks = k.RANK[:, :].unsqueeze(1).to_broadcast([P, NT, E])
    link(nc.vector.tensor_reduce(value, p, AX, ALU.max))
    link(nc.vector.tensor_tensor(w.q[:, :, :], p, over(value), ALU.is_equal))
    link(nc.vector.tensor_tensor(w.q[:, :, :], w.q[:, :, :], ranks, ALU.mult))
    link(nc.vector.tensor_reduce(rank, w.q[:, :, :], AX, ALU.max))
    link(nc.vector.tensor_tensor(mask, w.q[:, :, :], over(rank), ALU.is_equal))


class Work:

    def __init__(self, st):
        self.p, self.q, self.s = (st.sb(n, [P, NT, E]) for n in "pqs")
        self.m, self.r, self.a, self.b, self.c, self.g = (st.sb("v" + n, [P, NT]) for n in "mrabcg")


def route0(nc, name, k):
    with ExitStack() as ctx:
        st = Stage(nc, ctx, name)
        w = Work(st)
        mask = st.sb("mask", [P, NT, E], BF16)
        te = st.sb("te", [P, E * NT])
        sc = st.sb("sc", [P, E * NT])
        NB = 4
        hot = [st.sb(f"hot{i}", [P, E * CAP0], BF16) for i in range(NB)]
        tok = st.sb("tok", [P, E, 3])
        row = st.sb("row", [P, 2, E])
        psC = st.ps("psC", [P, 2, NT * E])
        psS = st.ps("psS", [P, 512])
        s_vec = st.sem("vec")
        s_exp = st.sem("exp")
        s_cnt = st.sem("cnt")
        s_hot = st.sem("hot")
        s_use = st.sem("use")
        block = st.block()

        @block.scalar
        def _(act):
            act.wait_ge(s_vec, 2)
            nc.scalar.activation(w.q[:, :, :], w.p[:, :, :], ACT.Exp).then_inc(s_exp, 1)

        @block.vector
        def _(dve):
            link = Chain(dve, s_vec)
            softmax_over_experts(nc, dve, link, k, w, s_exp)
            first_largest(nc, link, k, w, w.p[:, :, :], w.g[:, :], w.a[:, :], mask[:, :, :])
            assert link.n == 10
            dve.wait_ge(s_cnt, 1)
            link(nc.vector.tensor_copy(te[:, :].rearrange("p (e t) -> p e t", e=E),
                                       psC[:, 1, :].rearrange("p (t e) -> p e t", e=E)))
            link(nc.vector.tensor_tensor_scan(sc[:, :], k.RESET[:, :], te[:, :], 0.0, ALU.mult, ALU.add))
            link(nc.vector.tensor_tensor(sc[:, :], sc[:, :], te[:, :], ALU.subtract))
            link(nc.vector.tensor_tensor(w.q[:, :, :], psC[:, 0, :].rearrange("p (t e) -> p t e", e=E),
                                         sc[:, :].rearrange("p (e t) -> p t e", e=E), ALU.add))
            link(nc.vector.tensor_tensor(w.q[:, :, :], w.q[:, :, :], mask[:, :, :], ALU.mult))
            link(nc.vector.tensor_reduce(w.b[:, :], w.q[:, :, :], AX, ALU.add))
            link(nc.vector.tensor_scalar(w.a[:, :], w.a[:, :], -float(CAP0), float(E * CAP0 - 1), ALU.mult, ALU.add))
            link(nc.vector.tensor_tensor(w.a[:, :], w.a[:, :], w.b[:, :], ALU.add))
            link(nc.vector.tensor_scalar(w.c[:, :], w.b[:, :], CAP0 + 0.5, float(SKIP), ALU.is_gt, ALU.mult))
            link(nc.vector.tensor_tensor(w.a[:, :], w.a[:, :], w.c[:, :], ALU.add))
            link(nc.vector.tensor_scalar(w.c[:, :], w.b[:, :], CAP0 + 0.5, 0.5, ALU.is_le, ALU.mult))
            link(nc.vector.tensor_tensor(k.GATE0[:, :], w.c[:, :], w.g[:, :], ALU.mult))
            for t in range(NT):
                after(dve, s_use, t - NB + 1)
                nc.vector.tensor_scalar(hot[t % NB][:, :], k.IOTA[:, :], w.a[:, t:t + 1], None,
                                        ALU.is_equal).then_inc(s_hot, 1)
            dve.wait_ge(s_use, NT)
            link(nc.vector.tensor_copy(tok[0:CAP0, :, :], psS[0:CAP0, 0:3 * E].rearrange("p (e a) -> p e a", a=3)))
            link(nc.vector.scalar_tensor_tensor(out=row[0:CAP0, 0, :], in0=tok[0:CAP0, :, 0], scalar=float(P),
                                                in1=tok[0:CAP0, :, 1], op0=ALU.mult, op1=ALU.add))
            link(nc.vector.tensor_scalar(row[0:CAP0, 1, :], tok[0:CAP0, :, 2], -float(SKIP), float(SKIP),
                                         ALU.mult, ALU.add))
            link(nc.vector.tensor_tensor(row[0:CAP0, 1, :], row[0:CAP0, 1, :], row[0:CAP0, 0, :], ALU.add))
            link(nc.vector.tensor_copy(k.SLOT_ROW[0:CAP0, :, :], row[0:CAP0, :, :]))

        @block.tensor
        def _(pe):
            pe.wait_ge(s_vec, 10)
            nc.tensor.matmul(psC[:, 0, :], k.TRIU[:, :], flat(mask[:, :, :]), start=True, stop=True,
                             skip_group_check=True)
            nc.tensor.matmul(psC[:, 1, :], k.ONESB[:, :], flat(mask[:, :, :]), start=True, stop=True,
                             skip_group_check=True).then_inc(s_cnt, 1)
            for t in range(NT):
                pe.wait_ge(s_hot, t + 1)
                for e in range(E):
                    last = nc.tensor.matmul(psS[0:CAP0, 3 * e:3 * e + 3], hot[t % NB][:, e * CAP0:(e + 1) * CAP0],
                                            k.IDS[:, t, :], start=(t == 0 and e == 0), stop=(t == NT - 1),
                                            skip_group_check=True)
                last.then_inc(s_use, 1)


def experts0(nc, name, k, dram, delta):
    with ExitStack() as ctx:
        st = Stage(nc, ctx, name)
        xe = st.sb("xe", [P, E, D])
        xet = st.sb("xet", [P, E * CAP0])
        w1 = [st.sb(f"w1{u}", [P, F0]) for u in range(2)]
        w2 = [st.sb(f"w2{u}", [P, FC0, D]) for u in range(2)]
        hid = [st.sb(f"hid{u}", [P, FC0, CAP0]) for u in range(2)]
        eo = st.sb("eo", [P, E, D])
        y = st.sb("y", [P, NT, D])
        psX = st.ps("psX", [P, 2, 512])
        psA = [st.ps(f"psA{u}", [P, 512]) for u in range(2)]
        psB = [st.ps(f"psB{u}", [P, 512]) for u in range(2)]
        s_w = [st.sem(f"w{u}") for u in range(2)]
        s_gat = st.sem("gat")
        s_tr = st.sem("tr")
        s_xt = st.sem("xt")
        s_up = st.sem("up")
        s_hid = st.sem("hid")
        s_dn = st.sem("dn")
        s_eo = st.sem("eo")
        s_sca = st.sem("sca")
        s_y = st.sem("y")
        s_x = st.sem("x")
        block = st.block()

        @block.sync
        def _(sp):
            def load(i, u):
                e = 2 * i + u
                after(sp, s_dn, e - 1)
                sp.dma_start(w1[u][:, :], dram.w1[bass.ds(e, 1), :, :].rearrange("a d f -> (a d) f"))\
                  .then_inc(s_w[u], 16)
                sp.dma_start(w2[u][:, :, :], dram.w2[bass.ds(e, 1), :, :].rearrange("a (c p) d -> p (a c) d", p=P))\
                  .then_inc(s_w[u], 16)

            twice_each(sp, E // 2, load)
            sp.wait_ge(s_sca, 16 * E)
            for q in range(4):
                n = NT // 4
                sp.dma_start(y[:, q * n:(q + 1) * n, :],
                             delta[q * n * P:(q + 1) * n * P, :].rearrange("(t p) d -> p t d", p=P)).then_inc(s_y, 16)

        @block.gpsimd
        def _(pool):
            for e in range(E):
                nc.gpsimd.indirect_dma_start(out=xe[0:CAP0, e, :], out_offset=None, in_=dram.normed[:, :],
                                             in_offset=bass.IndirectOffsetOnAxis(ap=k.SLOT_ROW[0:CAP0, 0, e:e + 1],
                                                                                 axis=0)).then_inc(s_gat, 16)
            for e in range(E):
                pool.wait_ge(s_eo, e + 1)
                nc.gpsimd.indirect_dma_start(out=delta[:, :],
                                             out_offset=bass.IndirectOffsetOnAxis(ap=k.SLOT_ROW[0:CAP0, 1, e:e + 1],
                                                                                  axis=0),
                                             in_=eo[0:CAP0, e, :], in_offset=None, bounds_check=NT * P - 1,
                                             oob_is_err=False).then_inc(s_sca, 16)

        @block.tensor
        def _(pe):
            pe.wait_ge(s_gat, 16 * E)
            for e in range(E):
                last = nc.tensor.transpose(psX[:, e // 4, (e % 4) * CAP0:(e % 4 + 1) * CAP0], xe[0:CAP0, e, :],
                                           k.IDENT[0:CAP0, 0:CAP0])
            last.then_inc(s_tr, 1)
            pe.wait_ge(s_xt, 2)

            def expert(i, u):
                e = 2 * i + u
                pe.wait_ge(s_w[u], 32 * (i + 1))
                for c in range(FC0):
                    last = nc.tensor.matmul(psA[u][:, c * CAP0:(c + 1) * CAP0], w1[u][:, c * P:(c + 1) * P],
                                            xet[:, bass.ds(e * CAP0, CAP0)], start=True, stop=True)
                last.then_inc(s_up, 1)
                after(pe, s_eo, e - 1)
                nc.tensor.matmul(psB[u][0:CAP0, 0:D], k.ONES[0:1, 0:CAP0], k.B2[0:1, bass.ds(e * D, D)],
                                 start=True, stop=False)
                pe.wait_ge(s_hid, FC0 * (e + 1))
                for c in range(FC0):
                    last = nc.tensor.matmul(psB[u][0:CAP0, 0:D], hid[u][:, c, :], w2[u][:, c, :],
                                            start=False, stop=(c == FC0 - 1))
                last.then_inc(s_dn, 1)

            twice_each(pe, E // 2, expert)

        @block.scalar
        def _(act):
            def gelu(i, u):
                e = 2 * i + u
                after(act, s_dn, e - 1)
                act.wait_ge(s_up, e + 1)
                for c in range(FC0):
                    nc.scalar.activation(hid[u][:, c, :], psA[u][:, c * CAP0:(c + 1) * CAP0], ACT.Gelu_apprx_tanh,
                                         bias=k.B1T[:, bass.ds(e * FC0 + c, 1)]).then_inc(s_hid, 1)

            twice_each(act, E // 2, gelu)

        @block.vector
        def _(dve):
            dve.wait_ge(s_tr, 1)
            for h in range(2):
                nc.vector.tensor_copy(xet[:, h * 4 * CAP0:(h + 1) * 4 * CAP0], psX[:, h, 0:4 * CAP0]).then_inc(s_xt, 1)

            def evacuate(i, u):
                e = 2 * i + u
                dve.wait_ge(s_dn, e + 1)
                nc.vector.tensor_copy(eo[0:CAP0, bass.ds(e, 1), :].rearrange("p a d -> p (a d)"),
                                      psB[u][0:CAP0, 0:D]).then_inc(s_eo, 1)

            twice_each(dve, E // 2, evacuate)
            dve.wait_ge(s_y, 64)
            with dve.Fori(0, NT // 8) as i:
                for u in range(8):
                    t = i * 8 + u
                    nc.vector.scalar_tensor_tensor(out=k.X[:, t, :], in0=y[:, t, :], scalar=k.GATE0[:, bass.ds(t, 1)],
                                                   in1=k.X[:, t, :], op0=ALU.mult, op1=ALU.add).then_inc(s_x, 1)


def attention0(nc, name, k):
    with ExitStack() as ctx:
        st = Stage(nc, ctx, name)
        xns = [st.sb(f"xns{u}", [P, TPB, D]) for u in range(2)]
        gos = [st.sb(f"gos{u}", [P, TPB, D]) for u in range(2)]
        sq = st.sb("sq", [P, TPB, D])
        go = st.sb("go", [P, NT, D])
        ons = [st.sb(f"ons{u}", [P, TPB, D]) for u in range(2)]
        ont = [st.sb(f"ont{u}", [P, T]) for u in range(2)]
        ss = st.sb("ss", [P, NT])
        rn = st.sb("rn", [P, NT])
        seq = st.sb("seq", [P, NT])
        fam = st.sb("fam", [P, NT])
        em = st.sb("em", [P, NT])
        gate = st.sb("gate", [P, NT])
        psT = [st.ps(f"psT{u}", [P, T]) for u in range(2)]
        psM = [st.ps(f"psM{j}", [P, T]) for j in range(TPB)]
        psE = st.ps("psE", [P, 512])
        s_vec = st.sem("vec")
        s_std = st.sem("std")
        s_xn = st.sem("xn")
        s_go = st.sem("go")
        s_sq = st.sem("sq")
        s_ss = st.sem("ss")
        s_cp = st.sem("cp")
        s_nrm = st.sem("nrm")
        s_on = st.sem("on")
        s_tr = st.sem("tr")
        s_ot = st.sem("ot")
        s_sim = st.sem("sim")
        s_max = st.sem("max")
        s_nov = st.sem("nov")
        s_x = st.sem("x")
        block = st.block()

        @block.vector
        def _(dve):
            link = Chain(dve, s_vec)
            statistics(nc, st, dve, link, k)
            dve.wait_ge(s_std, 1)
            link(nc.vector.reciprocal(k.RSTD[:, :], k.ST[:, 0, :]))

            def norm(i, u):
                b = 2 * i + u
                after(dve, s_go, b - 1)
                for j in range(TPB):
                    t = b * TPB + j
                    nc.vector.tensor_scalar(xns[u][:, j, :], k.X[:, t, :], k.MEAN[:, bass.ds(t, 1)],
                                            k.RSTD[:, bass.ds(t, 1)], ALU.subtract, ALU.mult).then_inc(s_xn, 1)
                dve.wait_ge(s_go, b + 1)
                after(dve, s_ss, b)
                nc.vector.tensor_tensor(sq[:, :, :], gos[u][:, :, :], gos[u][:, :, :], ALU.mult).then_inc(s_sq, 1)
                dve.wait_ge(s_sq, b + 1)
                nc.vector.tensor_reduce(ss[:, bass.ds(b * TPB, TPB)], sq[:, :, :], AX, ALU.add).then_inc(s_ss, 1)

            twice_each(dve, B // 2, norm)
            dve.wait_ge(s_nrm, 1)
            link(nc.vector.tensor_scalar(rn[:, :], rn[:, :], 1e-12, None, ALU.max))
            link(nc.vector.reciprocal(rn[:, :], rn[:, :]))
            dve.wait_ge(s_cp, B)

            def similar(i, u):
                b = 2 * i + u
                after(dve, s_tr, b - 1)
                for j in range(TPB):
                    t = b * TPB + j
                    nc.vector.tensor_scalar(ons[u][:, j, :], go[:, t, :], rn[:, bass.ds(t, 1)], None,
                                            ALU.mult).then_inc(s_on, 1)
                for j in range(TPB):
                    dve.wait_ge(s_sim, b * TPB + j + 1)
                    nc.vector.tensor_reduce(seq[:, bass.ds(b * TPB + j, 1)], psM[j][:, 0:(j + 1) * P], AX, ALU.max)\
                      .then_inc(s_max, 1)

            twice_each(dve, B // 2, similar)
            dve.wait_ge(s_max, NT)
            link(nc.vector.tensor_copy(em[:, :], psE[:, 0:NT]))
            link(nc.vector.tensor_tensor(fam[:, :], em[:, :], k.FIRST[:, :], ALU.add))
            link(nc.vector.tensor_tensor(seq[:, :], seq[:, :], fam[:, :], ALU.max))
            link(nc.vector.tensor_scalar(fam[:, :], em[:, :], k.SCAL[:, 4:5], None, ALU.mult))
            link(nc.vector.scalar_tensor_tensor(out=fam[:, :], in0=seq[:, :], scalar=k.SCAL[:, 2:3], in1=fam[:, :],
                                                op0=ALU.mult, op1=ALU.add))
            dve.wait_ge(s_nov, 1)
            link(nc.vector.tensor_scalar(gate[:, :], gate[:, :], k.SCAL[:, 1:2], k.SCAL[:, 3:4], ALU.mult, ALU.add))
            with dve.Fori(0, NT // 8) as i:
                for u in range(8):
                    t = i * 8 + u
                    nc.vector.scalar_tensor_tensor(out=k.X[:, t, :], in0=go[:, t, :], scalar=gate[:, bass.ds(t, 1)],
                                                   in1=k.X[:, t, :], op0=ALU.mult, op1=ALU.add).then_inc(s_x, 1)

        @block.scalar
        def _(act):
            act.wait_ge(s_vec, 7)
            nc.scalar.activation(k.ST[:, 0, :], k.VARE[:, :], ACT.Sqrt).then_inc(s_std, 1)

            def gelu(i, u):
                b = 2 * i + u
                after(act, s_cp, b - 1)
                after(act, s_sq, b - 1)
                act.wait_ge(s_xn, TPB * (b + 1))
                nc.scalar.activation(gos[u][:, :, :], xns[u][:, :, :], ACT.Gelu_apprx_tanh).then_inc(s_go, 1)

            twice_each(act, B // 2, gelu)
            act.wait_ge(s_ss, B)
            nc.scalar.activation(rn[:, :], ss[:, :], ACT.Sqrt).then_inc(s_nrm, 1)

            def turned(i, u):
                b = 2 * i + u
                after(act, s_sim, (b - 1) * TPB)
                act.wait_ge(s_tr, b + 1)
                nc.scalar.copy(ont[u][:, :], psT[u][:, :]).then_inc(s_ot, 1)

            twice_each(act, B // 2, turned)
            act.wait_ge(s_vec, 15)
            nc.scalar.activation(gate[:, :], fam[:, :], ACT.Exp, scale=k.SCAL[:, 0:1]).then_inc(s_nov, 1)

        @block.gpsimd
        def _(pool):
            def copy(i, u):
                b = 2 * i + u
                pool.wait_ge(s_go, b + 1)
                nc.gpsimd.tensor_copy(go[:, bass.ds(b * TPB, TPB), :], gos[u][:, :, :]).then_inc(s_cp, 1)

            twice_each(pool, B // 2, copy)

        @block.tensor
        def _(pe):
            def batch(i, u):
                b = 2 * i + u
                pe.wait_ge(s_on, TPB * (b + 1))
                after(pe, s_ot, b - 1)
                for j in range(TPB):
                    last = nc.tensor.transpose(psT[u][:, j * P:(j + 1) * P], ons[u][:, j, :], k.IDENT[:, :])
                last.then_inc(s_tr, 1)
                pe.wait_ge(s_ot, b + 1)
                for j in range(TPB):
                    n = (j + 1) * P
                    after(pe, s_max, (b - 1) * TPB + j + 1)
                    mine = ont[u][:, j * P:(j + 1) * P]
                    nc.tensor.matmul(psM[j][:, 0:n], mine, ont[u][:, 0:n], start=True, stop=False)
                    nc.tensor.matmul(psM[j][:, n - P:n], k.IDENTB[:, :], k.PAST[:, :], start=False, stop=True)
                    nc.tensor.matmul(psE[:, bass.ds(b * TPB + j, 1)], mine, k.EMA[:, 0:1], start=True, stop=True,
                                     skip_group_check=True).then_inc(s_sim, 1)

            twice_each(pe, B // 2, batch)


def route1(nc, name, k):
    with ExitStack() as ctx:
        st = Stage(nc, ctx, name)
        w = Work(st)
        mask = st.sb("mask", [P, 2, NT, E], BF16)
        cnt = st.sb("cnt", [P, B, E])
        pos = st.sb("pos", [P, 2, NT])
        rank = st.sb("rank", [P, 2, NT])
        val = st.sb("val", [P, 2, NT])
        kb = st.sb("kb", [P, 2, NT])
        psC = st.ps("psC", [P, 2, NT * E])
        psN = st.ps("psN", [P, 512])
        s_vec = st.sem("vec")
        s_exp = st.sem("exp")
        s_cnt = st.sem("cnt")
        block = st.block()
        over = lambda v: v.unsqueeze(2).to_broadcast([P, NT, E])

        @block.scalar
        def _(act):
            act.wait_ge(s_vec, 2)
            nc.scalar.activation(w.q[:, :, :], w.p[:, :, :], ACT.Exp).then_inc(s_exp, 1)

        @block.vector
        def _(dve):
            link = Chain(dve, s_vec)
            softmax_over_experts(nc, dve, link, k, w, s_exp)
            first_largest(nc, link, k, w, w.p[:, :, :], val[:, 0, :], rank[:, 0, :], mask[:, 0, :, :])
            link(nc.vector.tensor_tensor(w.s[:, :, :], w.q[:, :, :], over(rank[:, 0, :]), ALU.not_equal))
            link(nc.vector.tensor_tensor(w.s[:, :, :], w.s[:, :, :], w.p[:, :, :], ALU.mult))
            first_largest(nc, link, k, w, w.s[:, :, :], val[:, 1, :], rank[:, 1, :], mask[:, 1, :, :])
            assert link.n == 17
            dve.wait_ge(s_cnt, 1)
            link(nc.vector.tensor_scalar(cnt[:, :, :], psN[:, 0:B * E].rearrange("p (g e) -> p g e", e=E),
                                         float(CAP1), None, ALU.min))
            link(nc.vector.tensor_tensor(w.q[:, :, :], psC[:, 0, :].rearrange("p (t e) -> p t e", e=E),
                                         mask[:, 0, :, :], ALU.mult))
            link(nc.vector.tensor_reduce(pos[:, 0, :], w.q[:, :, :], AX, ALU.add))
            link(nc.vector.tensor_tensor(w.q[:, :, :].rearrange("p (g j) e -> p g j e", j=TPB),
                                         psC[:, 1, :].rearrange("p (g j e) -> p g j e", j=TPB, e=E),
                                         cnt[:, :, :].unsqueeze(2).to_broadcast([P, B, TPB, E]), ALU.add))
            link(nc.vector.tensor_tensor(w.q[:, :, :], w.q[:, :, :], mask[:, 1, :, :], ALU.mult))
            link(nc.vector.tensor_reduce(pos[:, 1, :], w.q[:, :, :], AX, ALU.add))
            base = k.BASE[:, :].unsqueeze(1).to_broadcast([P, 2, NT])
            link(nc.vector.scalar_tensor_tensor(out=flat(rank[:, :, :]), in0=flat(rank[:, :, :]),
                                                scalar=-float(HALF * CAP1), in1=flat(pos[:, :, :]),
                                                op0=ALU.mult, op1=ALU.add))
            link(nc.vector.tensor_tensor(rank[:, :, :], rank[:, :, :], base, ALU.add))
            link(nc.vector.tensor_scalar(kb[:, :, :], pos[:, :, :], CAP1 + 0.5, float(SKIP), ALU.is_gt, ALU.mult))
            link(nc.vector.tensor_tensor(rank[:, :, :], rank[:, :, :], kb[:, :, :], ALU.add))
            link(nc.vector.tensor_copy(k.ROW1[:, :, :], rank[:, :, :]))
            link(nc.vector.tensor_scalar(kb[:, :, :], pos[:, :, :], CAP1 + 0.5, 0.5, ALU.is_le, ALU.mult))
            link(nc.vector.tensor_tensor(k.GATE1[:, :, :], kb[:, :, :], val[:, :, :], ALU.mult))

        @block.tensor
        def _(pe):
            pe.wait_ge(s_vec, 17)
            for c in range(2):
                out = psC[:, c, :].rearrange("p (g j e) -> p g j e", j=TPB, e=E)
                m = mask[:, c, :, :].rearrange("p (g j) e -> p g j e", j=TPB)
                nc.tensor.matmul(psC[:, c, :], k.TRIU[:, :], mask[:, c, :, :].rearrange("p t e -> p (t e)"),
                                 start=True, stop=False, skip_group_check=True)
                for s in range(1, TPB):
                    nc.tensor.matmul(out[:, :, s:TPB, :], k.ONESB[:, :], m[:, :, 0:TPB - s, :], start=False,
                                     stop=(s == TPB - 1), skip_group_check=True)
            for j in range(TPB):
                last = nc.tensor.matmul(psN[:, 0:B * E], k.ONESB[:, :],
                                        mask[:, 0, :, :].rearrange("p (g j) e -> p g j e", j=TPB)[:, :, j, :],
                                        start=(j == 0), stop=(j == TPB - 1), skip_group_check=True)
            last.then_inc(s_cnt, 1)


def experts1(nc, name, k, dram):
    with ExitStack() as ctx:
        st = Stage(nc, ctx, name)
        got = st.sb("got", [P, 2, NT, D])
        w0 = [st.sb(f"w0{u}", [P, H1]) for u in range(2)]
        w1 = [st.sb(f"w1{u}", [P, H1]) for u in range(2)]
        wo = [st.sb(f"wo{u}", [P, HC1, D]) for u in range(2)]
        xe = [st.sb(f"xe{u}", [P, HALF, D]) for u in range(2)]
        xet = [st.sb(f"xet{u}", [P, HALF * CAP1]) for u in range(2)]
        ge = [st.sb(f"ge{c}", [P, 512]) for c in range(2)]
        hid = [st.sb(f"hid{c}", [P, 512]) for c in range(3)]
        eot = st.sb("eot", [P, 512])
        eo = [st.sb(f"eo{u}", [P, HALF, D]) for u in range(2)]
        psA = [st.ps(f"psA{c}", [P, 512]) for c in range(2)]
        psB = [st.ps(f"psB{c}", [P, 512]) for c in range(2)]
        psX = st.ps("psX", [P, 512])
        psY = st.ps("psY", [P, 512])
        psO = st.ps("psO", [P, 512])
        s_in = [st.sem(f"in{h}") for h in range(2)]
        s_w = [st.sem(f"w{u}") for u in range(2)]
        s_xe = [st.sem(f"xe{u}") for u in range(2)]
        s_tr = st.sem("tr")
        s_xt = st.sem("xt")
        s_up = st.sem("up")
        s_ge = st.sem("ge")
        s_hid = st.sem("hid")
        s_dn = st.sem("dn")
        s_unit = st.sem("unit")
        s_et = st.sem("et")
        s_eb = st.sem("eb")
        s_eo = st.sem("eo")
        s_out = [st.sem(f"out{u}") for u in range(2)]
        s_got = [st.sem(f"got{h}") for h in range(2)]
        s_zero = st.sem("zero")
        s_x = st.sem("x")
        block = st.block()
        width = [P] * (HC1 - 1) + [HREST]
        EI = [d.rearrange("(e g c) d -> e c g d", g=HALF, c=CAP1) for d in dram.expert_in]
        EO = [d.rearrange("(e g c) d -> e c g d", g=HALF, c=CAP1) for d in dram.expert_out]
        HT = NT // 2

        def units(eng, body):
            for h in range(2):
                for u in range(2):
                    body(E * h + u, u, E // 2 * h, u, h)
                with eng.Fori(1, E // 2) as q:
                    for u in range(2):
                        body(E * h + 2 * q + u, 2 * q + u, E // 2 * h + q, u, h)

        @block.gpsimd
        def _(pool):
            for h in range(2):
                for t in range(h * HT, (h + 1) * HT):
                    for c in range(2):
                        nc.gpsimd.indirect_dma_start(
                            out=dram.expert_in[h][:, :],
                            out_offset=bass.IndirectOffsetOnAxis(ap=k.ROW1[:, c, t:t + 1], axis=0),
                            in_=k.XN[:, t, :], in_offset=None, bounds_check=SLOTS1 // 2 - 1,
                            oob_is_err=False).then_inc(s_in[h], 16)
            pool.wait_ge(s_zero, 1)
            for h in range(2):
                for u in range(2):
                    pool.wait_ge(s_out[u], 16 * (E // 2) * (h + 1))
                for t in range(h * HT, (h + 1) * HT):
                    for c in range(2):
                        nc.gpsimd.indirect_dma_start(
                            out=got[:, c, t, :], out_offset=None, in_=dram.expert_out[h][:, :],
                            in_offset=bass.IndirectOffsetOnAxis(ap=k.ROW1[:, c, t:t + 1], axis=0),
                            bounds_check=SLOTS1 // 2 - 1, oob_is_err=False).then_inc(s_got[h], 16)

        @block.sync
        def _(sp):
            def store(n, e, u, h):
                sp.wait_ge(s_eb, n + 1)
                sp.dma_start(EO[h][bass.ds(e, 1), :, :, :].rearrange("a c g d -> (a c) g d"), eo[u][:, :, :])\
                  .then_inc(s_out[u], 16)

            def load(n, e, i, u, h):
                after(sp, s_unit, n - 1)
                sp.dma_start(w0[u][:, :], dram.w0k[bass.ds(e, 1), :, :].rearrange("a d f -> (a d) f"))\
                  .then_inc(s_w[u], 16)
                sp.dma_start(w1[u][:, :], dram.w1k[bass.ds(e, 1), :, :].rearrange("a d f -> (a d) f"))\
                  .then_inc(s_w[u], 16)
                sp.dma_start(wo[u][:, 0:HC1 - 1, :], dram.wok[bass.ds(e, 1), 0:(HC1 - 1) * P, :]
                             .rearrange("a (c p) d -> p (a c) d", p=P)).then_inc(s_w[u], 16)
                sp.dma_start(wo[u][0:HREST, HC1 - 1, :], dram.wok[bass.ds(e, 1), (HC1 - 1) * P:H1, :]
                             .rearrange("a p d -> (a p) d")).then_inc(s_w[u], 16)
                if isinstance(n, int):
                    sp.wait_ge(s_in[h], 16 * 2 * HT)
                sp.dma_start(xe[u][:, :, :], EI[h][bass.ds(e, 1), :, :, :].rearrange("a c g d -> (a c) g d"))\
                  .then_inc(s_xe[u], 16)
                if isinstance(e, int) and e == 0:
                    if h == 1:
                        store(n - 1, E - 1, 1 - u, 0)
                else:
                    store(n - 1, e - 1, 1 - u, h)

            units(sp, load)
            store(2 * E - 1, E - 1, 1, 1)

        @block.tensor
        def _(pe):
            def unit(n, e, i, u, h):
                pe.wait_ge(s_xe[u], 16 * (i + 1))
                after(pe, s_xt, n)
                for g in range(HALF):
                    last = nc.tensor.transpose(psX[:, g * CAP1:(g + 1) * CAP1], xe[u][:, g, :], k.IDENT[:, :])
                last.then_inc(s_tr, 1)
                pe.wait_ge(s_w[u], 64 * (i + 1))
                pe.wait_ge(s_xt, n + 1)

                def down(c):
                    pe.wait_ge(s_hid, HC1 * n + c + 1)
                    if c == 0:
                        after(pe, s_et, n)
                    m = width[c]
                    mm = nc.tensor.matmul(psY[:, :], wo[u][0:m, c, :], hid[c % 3][0:m, :], start=(c == 0),
                                          stop=(c == HC1 - 1))
                    mm.then_inc(s_dn, 1)

                for c in range(HC1):
                    m = width[c]
                    after(pe, s_hid, HC1 * n + c - 1)
                    nc.tensor.matmul(psA[c % 2][0:m, :], w0[u][:, c * P:c * P + m], xet[u][:, :], start=True,
                                     stop=True)
                    nc.tensor.matmul(psB[c % 2][0:m, :], w1[u][:, c * P:c * P + m], xet[u][:, :], start=True,
                                     stop=True).then_inc(s_up, 1)
                    if c >= 1:
                        down(c - 1)
                down(HC1 - 1)
                pe.wait_ge(s_et, n + 1)
                after(pe, s_eb, n)
                for g in range(HALF):
                    last = nc.tensor.transpose(psO[:, g * P:(g + 1) * P], eot[:, g * CAP1:(g + 1) * CAP1],
                                               k.IDENT[:, :])
                last.then_inc(s_unit, 1)

            units(pe, unit)

        @block.scalar
        def _(act):
            def unit(n, e, i, u, h):
                act.wait_ge(s_tr, n + 1)
                after(act, s_up, HC1 * (n - 1))
                nc.scalar.copy(xet[u][:, :], psX[:, :]).then_inc(s_xt, 1)
                for c in range(HC1):
                    m = width[c]
                    act.wait_ge(s_up, HC1 * n + c + 1)
                    after(act, s_hid, HC1 * n + c - 1)
                    nc.scalar.activation(ge[c % 2][0:m, :], psA[c % 2][0:m, :], ACT.Gelu_apprx_tanh)\
                      .then_inc(s_ge, 1)
                act.wait_ge(s_dn, HC1 * (n + 1))
                after(act, s_unit, n)
                nc.scalar.copy(eot[:, :], psY[:, :]).then_inc(s_et, 1)

            units(act, unit)

        @block.vector
        def _(dve):
            nc.vector.memset(got[:, :, :, :], 0.0).then_inc(s_zero, 1)

            def unit(n, e, i, u, h):
                for c in range(HC1):
                    m = width[c]
                    dve.wait_ge(s_ge, HC1 * n + c + 1)
                    after(dve, s_dn, HC1 * n + c - 2)
                    nc.vector.tensor_tensor(hid[c % 3][0:m, :], ge[c % 2][0:m, :], psB[c % 2][0:m, :], ALU.mult)\
                      .then_inc(s_hid, 1)
                dve.wait_ge(s_unit, n + 1)
                after(dve, s_out[u], 16 * i)
                nc.vector.tensor_copy(flat(eo[u][:, :, :]), psO[:, :]).then_inc(s_eb, 1)

            units(dve, unit)
            for h in range(2):
                dve.wait_ge(s_got[h], 16 * 2 * HT)
                for c in range(2):
                    with dve.Fori(h * HT // 8, (h + 1) * HT // 8) as i:
                        for u in range(8):
                            t = i * 8 + u
                            nc.vector.scalar_tensor_tensor(
                                out=k.X[:, t, :], in0=got[:, c, t, :], scalar=k.GATE1[:, c, bass.ds(t, 1)],
                                in1=k.X[:, t, :], op0=ALU.mult, op1=ALU.add).then_inc(s_x, 1)
                    dve.wait_ge(s_x, HT * (2 * h + c + 1))


def attention1(nc, name, k):
    with ExitStack() as ctx:
        st = Stage(nc, ctx, name)
        D0 = [st.sb(f"D0{u}", [P, CH + 1, B, 3]) for u in range(2)]
        D1 = [st.sb(f"D1{u}", [P, CH + 1, B, 3]) for u in range(2)]
        Z = [st.sb(f"Z{u}", [P, CH + 1, B]) for u in range(2)]
        R = st.sb("R", [P, CH, B])
        S = [st.sb(f"S{u}", [P, CH + 1, B, 3]) for u in range(2)]
        HB = B // 2
        psG = [[st.ps(f"ps{n}{q}", [P, 512]) for q in range(2)] for n in "czr"]
        psO = [st.ps(f"psO{q}", [P, 512]) for q in range(2)]
        s_init = st.sem("init")
        s_pj = st.sem("pj")
        s_ev = st.sem("ev")
        s_ru = st.sem("ru")
        s_a = st.sem("a")
        s_hy = st.sem("hy")
        s_tr = st.sem("tr")
        s_x = st.sem("x")
        block = st.block()
        XT = k.XT[:, :].rearrange("p (b t) -> p b t", b=B)
        STEPS = CH + 1

        def gate_piece(act, ch, n, b):
            u = ch % 2
            src = psG[n][b // HB][:, (b % HB) * CH:(b % HB + 1) * CH]
            bias = k.COLS[:, 3 + n:4 + n]
            if n == 0:
                out, func = D1[u][:, 0:CH, b, 2], ACT.Identity
            elif n == 1:
                out, func = Z[u][:, 0:CH, b], ACT.Sigmoid
            else:
                out, func = R[:, :, b], ACT.Sigmoid
            nc.scalar.activation(out, src, func, bias=bias).then_inc(s_ev, 1)

        PIECES = [(n, b) for n in (1, 2, 0) for b in range(B)]

        @block.scalar
        def _(act):
            act.wait_ge(s_pj, 1)
            act.wait_ge(s_init, 6)
            for n, b in PIECES:
                gate_piece(act, 0, n, b)
            for ch in range(NCH):
                u = ch % 2
                todo = list(PIECES) if ch + 1 < NCH else []
                for r in range(CH):
                    act.wait_ge(s_a, ch * STEPS + r + 1)
                    nc.scalar.activation(D0[u][:, r + 1, :, 1], S[u][:, r, :, 2], ACT.Tanh).then_inc(s_hy, 1)
                    if r >= 8 and r % 4 == 0 and todo:
                        if r == 8:
                            act.wait_ge(s_pj, ch + 2)
                            if ch >= 1:
                                act.wait_ge(s_ru, 2 * ch)
                        gate_piece(act, ch + 1, *todo.pop(0))
                assert not todo

        @block.gpsimd
        def _(pool):
            for u in range(2):
                nc.gpsimd.memset(D0[u][:, :, :, :], 0.0).then_inc(s_init, 1)
                nc.gpsimd.memset(D1[u][:, :, :, :], 0.0).then_inc(s_init, 1)
                nc.gpsimd.memset(S[u][:, CH, :, :], 0.0).then_inc(s_init, 1)
            pool.wait_ge(s_init, 6)
            for ch in range(NCH):
                u = ch % 2
                pool.wait_ge(s_ev, len(PIECES) * ch + 2 * B)
                nc.gpsimd.tensor_scalar(D1[u][:, 1:CH + 1, :, 0], Z[u][:, 0:CH, :], -1.0, 1.0, ALU.mult, ALU.add)\
                  .then_inc(s_ru, 1)
                nc.gpsimd.tensor_scalar(D0[u][:, 0:CH, :, 2], R[:, :, :], k.COLS[:, 0:1], None, ALU.mult)\
                  .then_inc(s_ru, 1)

        @block.tensor
        def _(pe):
            def project(ch):
                if ch >= 1:
                    pe.wait_ge(s_ev, len(PIECES) * ch)
                for n in range(3):
                    for q in range(2):
                        last = nc.tensor.matmul(psG[n][q][:, :], k.WT[:, n * P:(n + 1) * P],
                                                XT[:, q * HB:(q + 1) * HB, ch * CH:(ch + 1) * CH],
                                                start=True, stop=True)
                last.then_inc(s_pj, 1)

            project(0)
            for ch in range(NCH):
                if ch + 1 < NCH:
                    project(ch + 1)
                pe.wait_ge(s_a, (ch + 1) * STEPS)
                if ch >= 1:
                    pe.wait_ge(s_x, B * ch)
                for b in range(B):
                    last = nc.tensor.transpose(psO[b // HB][:, (b % HB) * P:(b % HB + 1) * P],
                                               S[ch % 2][:, 1:CH + 1, b, 1], k.IDENT[:, :])
                last.then_inc(s_tr, 1)

        @block.vector
        def _(dve):
            def add_piece(ch, b):
                t = b * TPB + ch
                nc.vector.tensor_tensor(k.X[:, t, :], k.X[:, t, :], psO[b // HB][:, (b % HB) * P:(b % HB + 1) * P],
                                        ALU.add).then_inc(s_x, 1)

            dve.wait_ge(s_init, 6)
            for ch in range(NCH):
                u = ch % 2
                dve.wait_ge(s_ev, len(PIECES) * (ch + 1))
                dve.wait_ge(s_ru, 2 * (ch + 1))
                if ch >= 1:
                    dve.wait_ge(s_a, ch * STEPS)
                nc.vector.tensor_copy(D1[u][:, 0, :, 1], S[1 - u][:, CH, :, 1]).then_inc(s_hy, 1)
                for r in range(STEPS):
                    dve.wait_ge(s_hy, ch * (2 * CH + 1) + 2 * r + 1)
                    nc.vector.tensor_tensor_scan(S[u][:, r, :, :].rearrange("p b a -> p (b a)"),
                                                 D0[u][:, r, :, :].rearrange("p b a -> p (b a)"),
                                                 D1[u][:, r, :, :].rearrange("p b a -> p (b a)"), 0.0,
                                                 ALU.mult, ALU.add).then_inc(s_a, 1)
                    if r == CH:
                        break
                    dve.wait_ge(s_a, ch * STEPS + r + 1)
                    nc.vector.tensor_tensor(D1[u][:, r + 1, :, 1], Z[u][:, r, :], S[u][:, r, :, 1], ALU.mult)\
                      .then_inc(s_hy, 1)
                    if ch >= 1 and r >= 16 and r % 8 == 0 and r // 8 - 2 < B:
                        if r == 16:
                            dve.wait_ge(s_tr, ch)
                        add_piece(ch - 1, r // 8 - 2)
            dve.wait_ge(s_tr, NCH)
            for b in range(B):
                add_piece(NCH - 1, b)


def store(nc, k, out):
    with ExitStack() as ctx:
        st = Stage(nc, ctx, "store")
        s_out = st.sem("out")
        block = st.block()

        @block.sync
        def _(sp):
            sp.dma_start(out.rearrange("b (j p) d -> p (b j) d", p=P), k.X[:, :, :]).then_inc(s_out, 16)
            sp.wait_ge(s_out, 16)


class Names:
    pass


def macaron(nc, x, ema, log_tau, log_blend, logit_blend_seq, gate_w, gate_b, w1, b1, w2, b2,
            u, W, b, gamma, beta, router_w, w0k, w1k, wok, out):
    dram = Names()
    dram.x, dram.ema, dram.log_tau, dram.log_blend, dram.logit_blend_seq = x, ema, log_tau, log_blend, logit_blend_seq
    dram.gate_w, dram.gate_b, dram.w1, dram.b1, dram.w2, dram.b2 = gate_w, gate_b, w1, b1, w2, b2
    dram.u, dram.W, dram.b, dram.gamma, dram.beta = u, W, b, gamma, beta
    dram.router_w, dram.w0k, dram.w1k, dram.wok = router_w, w0k, w1k, wok
    dram.normed = nc.dram_tensor("normed", (B * T, D), F32).ap()
    dram.delta0 = [nc.dram_tensor(f"delta{n}", (B * T, D), F32).ap() for n in range(2)]
    dram.expert_in = [nc.dram_tensor(f"expert_in{h}", (SLOTS1 // 2, D), F32).ap() for h in range(2)]
    dram.expert_out = [nc.dram_tensor(f"expert_out{h}", (SLOTS1 // 2, D), F32).ap() for h in range(2)]
    with ExitStack() as ctx:
        st = Stage(nc, ctx, "k")
        k = Names()
        k.X = st.sb("X", [P, NT, D])
        k.BN = st.sb("BN", [P, NT, 6])
        k.ST = st.sb("ST", [P, 3, NT])
        k.MEAN = st.sb("MEAN", [P, NT])
        k.VARE = st.sb("VARE", [P, NT])
        k.RSTD = st.sb("RSTD", [P, NT])
        k.IDENT = st.sb("IDENT", [P, P])
        k.TRIU = st.sb("TRIU", [P, P], BF16)
        k.ONESB = st.sb("ONESB", [P, P], BF16)
        k.ONES = st.sb("ONES", [P, P])
        k.IDENTB = st.sb("IDENTB", [P, P], BF16)
        k.PAST = st.sb("PAST", [P, P], BF16)
        k.FIRST = st.sb("FIRST", [P, NT])
        k.RESET = st.sb("RESET", [P, E * NT])
        k.IOTA = st.sb("IOTA", [P, E * CAP0], F16)
        k.BASE = st.sb("BASE", [P, NT])
        k.IDS = st.sb("IDS", [P, NT, 3], BF16)
        k.RANK = st.sb("RANK", [P, E])
        k.GW0 = st.sb("GW0", [P, E])
        k.RW1 = st.sb("RW1", [P, E])
        k.GB0 = st.sb("GB0", [1, NT, E])
        k.B2 = st.sb("B2", [1, E * D])
        k.B1T = st.sb("B1T", [P, E * FC0])
        k.WT = st.sb("WT", [P, 3 * D])
        k.COLS = st.sb("COLS", [P, 8])
        k.SCAL = st.sb("SCAL", [P, 8])
        k.EMA = st.sb("EMA", [P, 2])
        k.GATE0 = st.sb("GATE0", [P, NT])
        k.SLOT_ROW = st.sb("SLOT_ROW", [P, 2, E], U32)
        k.ROW1 = st.sb("ROW1", [P, 2, NT], U32)
        k.GATE1 = st.sb("GATE1", [P, 2, NT])

        def ffn0(n):
            with ExitStack() as own:
                k.psL = Stage(nc, own, f"f0{n}").ps("psL", [P, 512])
                normalize(nc, f"n0{n}", k, weights=k.GW0[:, :], rows=dram.normed, bias=flat(k.GB0[0:1, :, :]))
                route0(nc, f"r0{n}", k)
            experts0(nc, f"e0{n}", k, dram, dram.delta0[n])

        def ffn1(n):
            with ExitStack() as own:
                mine = Stage(nc, own, f"f1{n}")
                k.XN = mine.sb("XN", [P, NT, D])
                with ExitStack() as logits:
                    k.psL = Stage(nc, logits, f"l1{n}").ps("psL", [P, 512])
                    normalize(nc, f"n1{n}", k, weights=k.RW1[:, :], keep=k.XN)
                    route1(nc, f"r1{n}", k)
                experts1(nc, f"e1{n}", k, dram)

        stages = [lambda: ffn0(0), lambda: attention0(nc, "a0", k), lambda: ffn0(1), lambda: ffn1(0)]

        def attn1():
            with ExitStack() as own:
                k.XT = Stage(nc, own, "t1").sb("XT", [P, B * T])
                normalize(nc, "n2", k, keep_t=k.XT)
                attention1(nc, "a1", k)

        stages += [attn1, lambda: ffn1(1)]
        Stage.used.clear()
        setup(nc, k, dram)
        for n, s in enumerate(stages):
            if n == 3:
                recycle(nc)
            s()
        store(nc, k, out)



_INS = ['L0_attn_x', 'L0_attn_ema_out', 'L0_attn_log_tau', 'L0_attn_log_blend', 'L0_attn_logit_blend_seq',
        'L0_ffn_gate_w', 'L0_ffn_gate_b', 'L0_ffn_w1', 'L0_ffn_b1', 'L0_ffn_w2', 'L0_ffn_b2',
        'L1_attn_u', 'L1_attn_W', 'L1_attn_b', 'L1_attn_gamma', 'L1_attn_beta',
        'L1_ffn_router_w', 'L1_ffn_w0_kernel', 'L1_ffn_w1_kernel', 'L1_ffn_wo_kernel']
_OUT = (B, T, D)


def kernel(**inputs):
    import numpy as _np
    import concourse.bacc as _bacc
    from concourse import mybir as _mybir
    from concourse.bass_utils import run_bass_kernel_spmd as _run

    nc = _bacc.Bacc("TRN2", target_bir_lowering=False, num_devices=1)
    arrays, args = {}, []
    for name in _INS:
        a = _np.ascontiguousarray(inputs[name])
        arrays[f"in_{name}_dram"] = a
        args.append(nc.dram_tensor(f"in_{name}_dram", a.shape, _mybir.dt.from_np(a.dtype), kind="ExternalInput").ap())
    out = nc.dram_tensor("out_0_dram", _OUT, _mybir.dt.float32, kind="ExternalOutput").ap()
    macaron(nc, *args, out)
    r = _run(nc, [arrays], core_ids=[0])
    return r.results[0]["out_0_dram"]
```

```python
from contextlib import ExitStack

import concourse.bass as bass
from concourse import mybir

F32 = mybir.dt.float32
F16 = mybir.dt.float16
F32R = mybir.dt.float32r
BF16 = mybir.dt.bfloat16
I32 = mybir.dt.int32
U32 = mybir.dt.uint32
ALU = mybir.AluOpType
ACT = mybir.ActivationFunctionType
AX = mybir.AxisListType.X

P = 128
D = 128
B, T = 8, 512
NT = B * T // P
TPB = T // P
E = 8
LN_EPS = 1e-5

CAP0 = 80
F0 = 512
FC0 = F0 // P

CAP1 = 128
H1 = 688
HC1 = -(-H1 // P)
HREST = H1 - (HC1 - 1) * P
HALF = B // 2
SLOTS1 = B * E * CAP1
SKIP = 1 << 16

CH = 128
NCH = T // CH


def flat(ap):
    return ap.rearrange("p a b -> p (a b)")


def after(eng, sem, value):
    if not (isinstance(value, int) and value <= 0):
        eng.wait_ge(sem, value)


def twice_each(eng, n, body):
    for u in range(2):
        body(0, u)
    with eng.Fori(1, n) as i:
        for u in range(2):
            body(i, u)


class Chain:

    def __init__(self, eng, sem):
        self.eng, self.sem, self.n = eng, sem, 0

    def __call__(self, instruction):
        self.n += 1
        instruction.then_inc(self.sem, 1)
        self.eng.wait_ge(self.sem, self.n)


class Stage:

    used = []

    def __init__(self, nc, ctx, name):
        self.nc, self.ctx, self.name = nc, ctx, name

    def sb(self, name, shape, dt=F32):
        return self.ctx.enter_context(self.nc.sbuf_tensor(f"{self.name}_{name}", shape, dt))

    def ps(self, name, shape, dt=F32):
        return self.ctx.enter_context(self.nc.psum_tensor(f"{self.name}_{name}", shape, dt))

    def sem(self, name):
        handle = self.nc.alloc_semaphore(f"{self.name}_{name}")
        Stage.used.append(handle)
        return handle

    def block(self):
        return self.ctx.enter_context(self.nc.Block())


def recycle(nc):
    nc.clear_and_free_semaphores(list(Stage.used))
    Stage.used.clear()
    nc.all_engine_barrier()


def setup(nc, k, dram):
    with ExitStack() as ctx:
        st = Stage(nc, ctx, "set")
        zeros = k.ZEROS
        iota = st.sb("iota", [P, E * CAP1], I32)
        ids = st.sb("ids", [P, 3, NT], I32)
        bcol = st.sb("bcol", [E * FC0, P])
        wrows = st.sb("wrows", [P, 3, D])
        scal = st.sb("scal", [P, 8])
        nscal = st.sb("nscal", [P, 8])
        ema = st.sb("ema", [P, 4])
        pt = st.ps("pt", [P, 512])
        pe_ = st.ps("pe", [P, 512])
        s_load = st.sem("load")
        s_zero = st.sem("zero")
        k.s_zeroed = st.sem("zeroed")
        s_pool = st.sem("pool")
        s_iota = st.sem("iota")
        s_tr = st.sem("tr")
        s_sum = st.sem("sum")
        s_act = st.sem("act")
        s_vec = st.sem("vec")
        block = st.block()
        LOADS = 16 * 12

        @block.sync
        def _(sp):
            sp.dma_start(k.X[:, :, :], dram.x.rearrange("b (j p) d -> p (b j) d", p=P)).then_inc(s_load, 16)
            sp.dma_start(k.GW0[:, :], dram.gate_w).then_inc(s_load, 16)
            sp.dma_start(k.RW1[:, :], dram.router_w).then_inc(s_load, 16)
            sp.dma_start(k.GB0[0:1, 0, :], dram.gate_b.rearrange("(a e) -> a e", a=1)).then_inc(s_load, 16)
            sp.dma_start(k.B2[0:1, :], dram.b2.rearrange("(a e) d -> a (e d)", a=1)).then_inc(s_load, 16)
            sp.dma_start(bcol[:, :], dram.b1.rearrange("e (c p) -> (e c) p", p=P)).then_inc(s_load, 16)
            sp.dma_start(wrows[:, :, :], dram.W.rearrange("(c p) d -> p c d", p=P)).then_inc(s_load, 16)
            with nc.allow_non_contiguous_dma("a few columns of one word"):
                sp.dma_start(ema[:, 0:1], dram.ema.rearrange("(p a) -> p a", a=1)).then_inc(s_load, 16)
                cols = k.COLS[:, :]
                sp.dma_start(cols[:, 0:1], dram.u.rearrange("(p a) -> p a", a=1)).then_inc(s_load, 16)
                sp.dma_start(cols[:, 1:2], dram.gamma.rearrange("(p a) -> p a", a=1)).then_inc(s_load, 16)
                sp.dma_start(cols[:, 2:3], dram.beta.rearrange("(p a) -> p a", a=1)).then_inc(s_load, 16)
                sp.dma_start(cols[:, 3:6], dram.b.rearrange("(c p) -> p c", p=P)).then_inc(s_load, 16)
            sp.wait_ge(s_zero, 1)
            rows = 16 * P
            for y in dram.delta0 + dram.delta1:
                for n in range(NT // 16):
                    sp.dma_start(y[n * rows:(n + 1) * rows, :].rearrange("(p a) d -> p (a d)", p=P),
                                 zeros[:, :]).then_inc(k.s_zeroed, 16)

        @block.scalar
        def _(act):
            for n, name in enumerate((dram.log_tau, dram.log_blend, dram.logit_blend_seq)):
                act.dma_start(scal[:, n:n + 1], name.rearrange("(a e) -> a e", a=1).to_broadcast([P, 1]))\
                   .then_inc(s_act, 16)
            act.wait_ge(s_act, 48)
            nc.scalar.activation(nscal[:, 0:1], scal[:, 0:1], ACT.Exp).then_inc(s_act, 1)
            nc.scalar.activation(nscal[:, 1:3], scal[:, 1:3], ACT.Exp, scale=-1.0).then_inc(s_act, 1)
            act.wait_ge(s_tr, 1)
            nc.scalar.copy(k.B1T[:, :], pt[:, 0:E * FC0]).then_inc(s_act, 1)
            nc.scalar.copy(k.WT[:, :], pt[:, P:P + 3 * P]).then_inc(s_act, 1)
            act.wait_ge(s_sum, 1)
            nc.scalar.activation(ema[:, 2:3], pe_[:, 0:1], ACT.Sqrt).then_inc(s_act, 1)

        @block.gpsimd
        def _(pool):
            nc.gpsimd.memset(k.IDENT[:, :], 1.0).then_inc(s_iota, 1)
            nc.gpsimd.memset(k.TRIU[:, :], 1.0).then_inc(s_iota, 1)
            nc.gpsimd.memset(k.ONESB[:, :], 1.0).then_inc(s_iota, 1)
            nc.gpsimd.memset(k.ONES[:, :], 1.0).then_inc(s_iota, 1)
            nc.gpsimd.memset(k.PAST[:, :], 0.0).then_inc(s_iota, 1)
            nc.gpsimd.memset(k.FIRST[:, :], -4.0).then_inc(s_iota, 1)
            nc.gpsimd.memset(k.COLS[:, 6:7], LN_EPS).then_inc(s_iota, 1)
            nc.gpsimd.memset(k.RESET[:, :], 1.0).then_inc(s_iota, 1)
            nc.gpsimd.iota(iota[:, :], pattern=[[1, E * CAP1]], base=0, channel_multiplier=0).then_inc(s_iota, 1)
            nc.gpsimd.iota(ids[:, 0, :], pattern=[[1, NT]], base=0, channel_multiplier=0).then_inc(s_iota, 1)
            nc.gpsimd.iota(ids[:, 1, :], pattern=[[0, NT]], base=0, channel_multiplier=1).then_inc(s_iota, 1)
            nc.gpsimd.iota(ids[:, 2, :], pattern=[[0, NT]], base=1, channel_multiplier=0).then_inc(s_iota, 1)
            for e in range(E):
                nc.gpsimd.memset(k.RANK[:, e:e + 1], float(E - e)).then_inc(s_iota, 1)
            pool.wait_ge(s_iota, 12 + E)
            nc.gpsimd.affine_select(out=k.IDENT[:, :], in_=k.IDENT[:, :], compare_op=ALU.is_equal, fill=0.0,
                                    base=0, pattern=[[-1, P]], channel_multiplier=1).then_inc(s_pool, 1)
            nc.gpsimd.affine_select(out=k.TRIU[:, :], in_=k.TRIU[:, :], compare_op=ALU.is_ge, fill=0.0,
                                    base=0, pattern=[[1, P]], channel_multiplier=-1).then_inc(s_pool, 1)
            nc.gpsimd.affine_select(out=k.PAST[:, :], in_=k.PAST[:, :], compare_op=ALU.is_gt,
                                    fill=-4.0, base=0, pattern=[[-1, P]], channel_multiplier=1).then_inc(s_pool, 1)
            nc.gpsimd.memset(k.FIRST[0:1, 0:NT:TPB], 0.0).then_inc(s_pool, 1)
            nc.gpsimd.memset(k.RESET[:, 0:E * NT:NT], 0.0).then_inc(s_pool, 1)

        @block.vector
        def _(dve):
            link = Chain(dve, s_vec)
            nc.vector.memset(zeros[:, :], 0.0).then_inc(s_zero, 1)
            dve.wait_ge(s_pool, 5)
            nc.vector.tensor_copy(k.IDENTB[:, :], k.IDENT[:, :]).then_inc(s_zero, 1)
            link(nc.vector.tensor_copy(k.IOTA[:, :], iota[:, :]))
            link(nc.vector.tensor_copy(k.IDS[:, :, :], ids[:, :, :].rearrange("p a t -> p t a")))
            dve.wait_ge(s_load, LOADS)
            for t in range(1, NT):
                nc.vector.tensor_copy(k.GB0[0:1, t, :], k.GB0[0:1, 0, :]).then_inc(s_zero, 1)
            link(nc.vector.tensor_tensor(ema[:, 1:2], ema[:, 0:1], ema[:, 0:1], ALU.mult))
            dve.wait_ge(s_act, 50)
            link(nc.vector.tensor_scalar(k.SCAL[:, 0:1], nscal[:, 0:1], -1.0, None, ALU.mult))
            link(nc.vector.tensor_scalar(nscal[:, 1:3], nscal[:, 1:3], 1.0, None, ALU.add))
            link(nc.vector.reciprocal(k.SCAL[:, 1:3], nscal[:, 1:3]))
            link(nc.vector.tensor_scalar(k.SCAL[:, 3:5], k.SCAL[:, 1:3], -1.0, 1.0, ALU.mult, ALU.add))
            dve.wait_ge(s_act, 53)
            link(nc.vector.tensor_scalar(ema[:, 2:3], ema[:, 2:3], 1e-12, None, ALU.max))
            link(nc.vector.reciprocal(ema[:, 3:4], ema[:, 2:3]))
            link(nc.vector.tensor_tensor(k.EMA[:, 0:1], ema[:, 0:1], ema[:, 3:4], ALU.mult))

        @block.tensor
        def _(pe):
            pe.wait_ge(s_load, LOADS)
            pe.wait_ge(s_pool, 5)
            nc.tensor.transpose(pt[:, 0:E * FC0], bcol[:, :], k.IDENT[0:E * FC0, 0:E * FC0])
            for c in range(3):
                last = nc.tensor.transpose(pt[:, P + c * P:P + (c + 1) * P], wrows[:, c, :], k.IDENT[:, :])
            last.then_inc(s_tr, 1)
            pe.wait_ge(s_vec, 3)
            nc.tensor.matmul(pe_[:, 0:1], k.ONES[:, :], ema[:, 1:2], start=True, stop=True).then_inc(s_sum, 1)


GROUPS = [slice(g * 8, (g + 1) * 8) for g in range(NT // 8)]
QUADS = 2


def tiles_of(group):
    return list(range(NT))[group]


class Fold:

    def __init__(self, nc, st, k, delta, gate, groups=GROUPS):
        self.nc, self.k, self.delta, self.gate, self.groups = nc, k, delta, gate, groups
        self.y = st.sb("y", [P, NT, D])
        self.s_y = [st.sem(f"y{g}") for g in range(len(groups))]
        self.s_f = st.sem("f")

    def load(self, sp):
        for g, group in enumerate(self.groups):
            sp.dma_start(self.y[:, group, :], self.delta.rearrange("(t p) d -> p t d", p=P)[:, group, :])\
              .then_inc(self.s_y[g], 16)

    def add(self, dve, g):
        nc, k, group = self.nc, self.k, self.groups[g]
        dve.wait_ge(self.s_y[g], 16)
        if self.gate is None:
            for q in range(QUADS):
                quad = slice(group.start + 4 * q * (group.step or 1), group.start + (4 * q + 3) * (group.step or 1) + 1,
                             group.step)
                nc.vector.tensor_tensor(k.X[:, quad, :], k.X[:, quad, :], self.y[:, quad, :], ALU.add)\
                  .then_inc(self.s_f, 4)
        else:
            for t in tiles_of(group):
                nc.vector.scalar_tensor_tensor(out=k.X[:, t, :], in0=self.y[:, t, :], scalar=self.gate[:, t:t + 1],
                                               in1=k.X[:, t, :], op0=ALU.mult, op1=ALU.add).then_inc(self.s_f, 1)


class Norm:

    def __init__(self, nc, st, k, xn, groups=GROUPS, fold=None):
        self.nc, self.k, self.xn, self.groups, self.fold = nc, k, xn, groups, fold
        self.s_bn = st.sem("bn")
        self.s_mv = st.sem("mv")
        self.s_std = st.sem("std")
        self.s_rs = st.sem("rs")
        self.s_nb = st.sem("nb")
        self.s_xv = st.sem("xv")
        self.s_xa = st.sem("xa")

    MV = 7

    def vector(self, dve):
        nc, k = self.nc, self.k
        for g in range(len(self.groups) + 1):
            if g < len(self.groups):
                if self.fold is not None:
                    self.fold.add(dve, g)
                for n, t in enumerate(tiles_of(self.groups[g])):
                    if self.fold is not None and (self.fold.gate is not None or n % 4 == 0):
                        dve.wait_ge(self.fold.s_f, 8 * g + n + (1 if self.fold.gate is not None else 4))
                    nc.vector.bn_stats(k.BN[:, t, :], k.X[:, t, :]).then_inc(self.s_bn, 1)
            if g >= 1:
                group = self.groups[g - 1]
                dve.wait_ge(self.s_std, g)
                nc.vector.reciprocal(k.RSTD[:, group], k.STD[:, group]).then_inc(self.s_rs, 1)
                dve.wait_ge(self.s_rs, g)
                for t in tiles_of(group)[0::2]:
                    nc.vector.tensor_scalar(self.xn[:, t, :], k.X[:, t, :], k.MEAN[:, t:t + 1], k.RSTD[:, t:t + 1],
                                            ALU.subtract, ALU.mult).then_inc(self.s_xv, 1)

    def gpsimd(self, pool):
        nc, k, tt = self.nc, self.k, self.nc.gpsimd.tensor_tensor
        for g, group in enumerate(self.groups):
            mean_e, var_e, mean_o, var_o = (k.BN[:, group, i] for i in (1, 2, 4, 5))
            dif, var, both = k.DIF[:, group], k.VAR[:, group], k.BOTH[:, group]
            n = self.MV * g
            pool.wait_ge(self.s_bn, 8 * (g + 1))
            tt(dif, mean_e, mean_o, ALU.subtract).then_inc(self.s_mv, 1)
            tt(var, var_e, var_o, ALU.add).then_inc(self.s_mv, 1)
            tt(both, mean_e, mean_o, ALU.add).then_inc(self.s_mv, 1)
            pool.wait_ge(self.s_mv, n + 3)
            tt(dif, dif, dif, ALU.mult).then_inc(self.s_mv, 1)
            nc.gpsimd.tensor_scalar(k.MEAN[:, group], both, 0.5, None, ALU.mult).then_inc(self.s_mv, 1)
            pool.wait_ge(self.s_mv, n + 5)
            nc.gpsimd.tensor_scalar(dif, dif, D / 4.0, None, ALU.mult).then_inc(self.s_mv, 1)
            pool.wait_ge(self.s_mv, n + 6)
            tt(var, var, dif, ALU.add).then_inc(self.s_mv, 1)
            nc.gpsimd.tensor_scalar(both, k.MEAN[:, group], -1.0, None, ALU.mult).then_inc(self.s_nb, 1)
            pool.wait_ge(self.s_nb, 2 * g + 1)
            pool.wait_ge(self.s_rs, g + 1)
            tt(k.NBIAS[:, group], both, k.RSTD[:, group], ALU.mult).then_inc(self.s_nb, 1)

    def root(self, act, g):
        group = self.groups[g]
        act.wait_ge(self.s_mv, self.MV * (g + 1))
        self.nc.scalar.activation(self.k.STD[:, group], self.k.VAR[:, group], ACT.Sqrt, scale=1.0 / D,
                                  bias=self.k.COLS[:, 6:7]).then_inc(self.s_std, 1)

    def odd_tiles(self, act, g):
        k = self.k
        act.wait_ge(self.s_nb, 2 * (g + 1))
        for t in tiles_of(self.groups[g])[1::2]:
            self.nc.scalar.activation(self.xn[:, t, :], k.X[:, t, :], ACT.Identity, scale=k.RSTD[:, t:t + 1],
                                      bias=k.NBIAS[:, t:t + 1]).then_inc(self.s_xa, 1)

    def wait_quad(self, eng, q):
        eng.wait_ge(self.s_xv, 2 * (q + 1))
        eng.wait_ge(self.s_xa, 2 * (q + 1))


def normalize(nc, name, k, delta=None, gate=None, weights=None, rows=None, keep_t=None, bias=None, groups=GROUPS):
    with ExitStack() as ctx:
        st = Stage(nc, ctx, name)
        xn = k.xn
        xts = [st.sb(f"xts{u}", [P, T]) for u in range(2)]
        psT = [st.ps(f"psT{u}", [P, T]) for u in range(3)]
        s_tr = st.sem("tr")
        s_xt = st.sem("xt")
        s_lg = st.sem("lg")
        fold = Fold(nc, st, k, delta, gate, groups) if delta is not None else None
        norm = Norm(nc, st, k, xn, groups, fold)
        QUADS_ALL = QUADS * len(groups)
        quads = [tiles_of(g)[4 * q:4 * q + 4] for g in groups for q in range(QUADS)]
        block = st.block()

        @block.vector
        def _(dve):
            norm.vector(dve)

        @block.gpsimd
        def _(pool):
            norm.gpsimd(pool)

        @block.scalar
        def _(act):
            def copy(q):
                if keep_t is None and q >= 2:
                    act.wait_ge(s_lg, q - 1)
                act.wait_ge(s_tr, q + 1)
                if keep_t is None:
                    nc.scalar.copy(xts[q % 2][:, :], psT[q % 3][:, :]).then_inc(s_xt, 1)
                else:
                    b, ch = quads[q][0] // TPB, quads[q][0] % TPB
                    nc.scalar.activation(
                        keep_t[:, :].rearrange("p (b t) -> p b t", b=B)[:, b:b + 4, ch * P:(ch + 1) * P],
                        psT[q % 3][:, :].rearrange("p (b t) -> p b t", b=4), ACT.Identity,
                        bias=k.COLS[:, 2:3], scale=k.COLS[:, 1:2]).then_inc(s_xt, 1)

            norm.root(act, 0)
            for g in range(len(groups)):
                norm.odd_tiles(act, g)
                if g + 1 < len(groups):
                    norm.root(act, g + 1)
                for q in range(QUADS * g, QUADS * (g + 1)):
                    copy(q)

        @block.sync
        def _(sp):
            if fold is not None:
                fold.load(sp)
            if rows is not None:
                for q in range(QUADS_ALL):
                    norm.wait_quad(sp, q)
                    sp.dma_start(rows[q * T:(q + 1) * T, :].rearrange("(j p) d -> p j d", p=P),
                                 xn[:, q * TPB:(q + 1) * TPB, :]).then_inc(k.s_rows, 16)

        @block.tensor
        def _(pe):
            if bias is not None:
                nc.tensor.matmul(k.psL[:, 0:NT * E], k.ONES[0:1, :], bias, start=True, stop=False,
                                 skip_group_check=True)

            def logits(q):
                pe.wait_ge(s_xt, q + 1)
                for j, t in enumerate(quads[q]):
                    last = nc.tensor.matmul(k.psL[:, t * E:(t + 1) * E], xts[q % 2][:, j * P:(j + 1) * P],
                                            weights, start=bias is None, stop=True, skip_group_check=True)
                last.then_inc(s_lg, 1)

            for q in range(QUADS_ALL):
                norm.wait_quad(pe, q)
                if q >= 3:
                    pe.wait_ge(s_xt, q - 2)
                for j, t in enumerate(quads[q]):
                    last = nc.tensor.transpose(psT[q % 3][:, j * P:(j + 1) * P], xn[:, t, :], k.IDENT[:, :])
                last.then_inc(s_tr, 1)
                if weights is not None and q >= 1:
                    logits(q - 1)
            if weights is not None:
                logits(QUADS_ALL - 1)


def softmax_over_experts(nc, dve, link, k, w, s_exp):
    L = k.psL[:, 0:NT * E].rearrange("p (t e) -> p t e", e=E)
    over = lambda v: v.unsqueeze(2).to_broadcast([P, NT, E])
    link(nc.vector.tensor_reduce(w.m[:, :], L, AX, ALU.max))
    link(nc.vector.tensor_tensor(w.p[:, :, :], L, over(w.m[:, :]), ALU.subtract))
    dve.wait_ge(s_exp, 1)
    link(nc.vector.tensor_reduce(w.m[:, :], w.q[:, :, :], AX, ALU.add))
    link(nc.vector.reciprocal(w.r[:, :], w.m[:, :]))
    link(nc.vector.tensor_tensor(w.p[:, :, :], w.q[:, :, :], over(w.r[:, :]), ALU.mult))


def first_largest(nc, link, k, w, p, value, rank, mask):
    over = lambda v: v.unsqueeze(2).to_broadcast([P, NT, E])
    ranks = k.RANK[:, :].unsqueeze(1).to_broadcast([P, NT, E])
    link(nc.vector.tensor_reduce(value, p, AX, ALU.max))
    link(nc.vector.tensor_tensor(w.q[:, :, :], p, over(value), ALU.is_equal))
    link(nc.vector.tensor_tensor(w.q[:, :, :], w.q[:, :, :], ranks, ALU.mult))
    link(nc.vector.tensor_reduce(rank, w.q[:, :, :], AX, ALU.max))
    link(nc.vector.tensor_tensor(mask, w.q[:, :, :], over(rank), ALU.is_equal))


class Work:

    def __init__(self, st):
        self.p, self.q, self.s = (st.sb(n, [P, NT, E]) for n in "pqs")
        self.m, self.r, self.a, self.b, self.c, self.g = (st.sb("v" + n, [P, NT]) for n in "mrabcg")


def route0(nc, name, k):
    with ExitStack() as ctx:
        st = Stage(nc, ctx, name)
        w = Work(st)
        mask = st.sb("mask", [P, NT, E], BF16)
        te = st.sb("te", [P, E * NT])
        sc = st.sb("sc", [P, E * NT])
        NB = 4
        hot = [st.sb(f"hot{i}", [P, E * CAP0], BF16) for i in range(NB)]
        tok = st.sb("tok", [P, E, 3])
        row = st.sb("row", [P, 2, E])
        psC = st.ps("psC", [P, 2, NT * E])
        psS = st.ps("psS", [P, 512])
        s_vec = st.sem("vec")
        s_exp = st.sem("exp")
        s_cnt = st.sem("cnt")
        s_hot = st.sem("hot")
        s_use = st.sem("use")
        block = st.block()

        @block.scalar
        def _(act):
            act.wait_ge(s_vec, 2)
            nc.scalar.activation(w.q[:, :, :], w.p[:, :, :], ACT.Exp).then_inc(s_exp, 1)

        @block.vector
        def _(dve):
            link = Chain(dve, s_vec)
            softmax_over_experts(nc, dve, link, k, w, s_exp)
            first_largest(nc, link, k, w, w.p[:, :, :], w.g[:, :], w.a[:, :], mask[:, :, :])
            assert link.n == 10
            dve.wait_ge(s_cnt, 1)
            link(nc.vector.tensor_copy(te[:, :].rearrange("p (e t) -> p e t", e=E),
                                       psC[:, 1, :].rearrange("p (t e) -> p e t", e=E)))
            link(nc.vector.tensor_tensor_scan(sc[:, :], k.RESET[:, :], te[:, :], 0.0, ALU.mult, ALU.add))
            link(nc.vector.tensor_tensor(sc[:, :], sc[:, :], te[:, :], ALU.subtract))
            link(nc.vector.tensor_tensor(w.q[:, :, :], psC[:, 0, :].rearrange("p (t e) -> p t e", e=E),
                                         sc[:, :].rearrange("p (e t) -> p t e", e=E), ALU.add))
            link(nc.vector.tensor_tensor(w.q[:, :, :], w.q[:, :, :], mask[:, :, :], ALU.mult))
            link(nc.vector.tensor_reduce(w.b[:, :], w.q[:, :, :], AX, ALU.add))
            link(nc.vector.tensor_scalar(w.a[:, :], w.a[:, :], -float(CAP0), float(E * CAP0 - 1), ALU.mult, ALU.add))
            link(nc.vector.tensor_tensor(w.a[:, :], w.a[:, :], w.b[:, :], ALU.add))
            link(nc.vector.tensor_scalar(w.c[:, :], w.b[:, :], CAP0 + 0.5, float(SKIP), ALU.is_gt, ALU.mult))
            link(nc.vector.tensor_tensor(w.a[:, :], w.a[:, :], w.c[:, :], ALU.add))
            link(nc.vector.tensor_scalar(w.c[:, :], w.b[:, :], CAP0 + 0.5, 0.5, ALU.is_le, ALU.mult))
            link(nc.vector.tensor_tensor(k.GATE0[:, :], w.c[:, :], w.g[:, :], ALU.mult))
            for t in range(NT):
                after(dve, s_use, t - NB + 1)
                nc.vector.tensor_scalar(hot[t % NB][:, :], k.IOTA[:, 0:E * CAP0], w.a[:, t:t + 1], None,
                                        ALU.is_equal).then_inc(s_hot, 1)
            dve.wait_ge(s_use, NT)
            link(nc.vector.tensor_copy(tok[0:CAP0, :, :], psS[0:CAP0, 0:3 * E].rearrange("p (e a) -> p e a", a=3)))
            link(nc.vector.scalar_tensor_tensor(out=row[0:CAP0, 0, :], in0=tok[0:CAP0, :, 0], scalar=float(P),
                                                in1=tok[0:CAP0, :, 1], op0=ALU.mult, op1=ALU.add))
            link(nc.vector.tensor_scalar(row[0:CAP0, 1, :], tok[0:CAP0, :, 2], -float(SKIP), float(SKIP),
                                         ALU.mult, ALU.add))
            link(nc.vector.tensor_tensor(row[0:CAP0, 1, :], row[0:CAP0, 1, :], row[0:CAP0, 0, :], ALU.add))
            link(nc.vector.tensor_copy(k.SLOT_ROW[0:CAP0, :, :], row[0:CAP0, :, :]))

        @block.tensor
        def _(pe):
            pe.wait_ge(s_vec, 10)
            nc.tensor.matmul(psC[:, 0, :], k.TRIU[:, :], flat(mask[:, :, :]), start=True, stop=True,
                             skip_group_check=True)
            nc.tensor.matmul(psC[:, 1, :], k.ONESB[:, :], flat(mask[:, :, :]), start=True, stop=True,
                             skip_group_check=True).then_inc(s_cnt, 1)
            for t in range(NT):
                pe.wait_ge(s_hot, t + 1)
                for e in range(E):
                    last = nc.tensor.matmul(psS[0:CAP0, 3 * e:3 * e + 3], hot[t % NB][:, e * CAP0:(e + 1) * CAP0],
                                            k.IDS[:, t, :], start=(t == 0 and e == 0), stop=(t == NT - 1),
                                            skip_group_check=True)
                last.then_inc(s_use, 1)


def experts0(nc, name, k, dram, delta):
    with ExitStack() as ctx:
        st = Stage(nc, ctx, name)
        xe = st.sb("xe", [P, E, D])
        xet = st.sb("xet", [P, E * CAP0])
        w1 = [st.sb(f"w1{u}", [P, F0]) for u in range(2)]
        w2 = [st.sb(f"w2{u}", [P, FC0, D]) for u in range(2)]
        hid = [st.sb(f"hid{u}", [P, FC0, CAP0]) for u in range(2)]
        eo = st.sb("eo", [P, E, D])
        psX = st.ps("psX", [P, 2, 512])
        psA = [st.ps(f"psA{u}", [P, 512]) for u in range(2)]
        psB = [st.ps(f"psB{u}", [P, 512]) for u in range(2)]
        s_w = [st.sem(f"w{u}") for u in range(2)]
        s_gat = st.sem("gat")
        s_tr = st.sem("tr")
        s_xt = st.sem("xt")
        s_up = st.sem("up")
        s_hid = st.sem("hid")
        s_dn = st.sem("dn")
        s_eo = st.sem("eo")
        s_sca = st.sem("sca")
        block = st.block()

        @block.sync
        def _(sp):
            def load(i, u):
                e = 2 * i + u
                after(sp, s_dn, e - 1)
                sp.dma_start(w1[u][:, :], dram.w1[bass.ds(e, 1), :, :].rearrange("a d f -> (a d) f"))\
                  .then_inc(s_w[u], 16)
                sp.dma_start(w2[u][:, :, :], dram.w2[bass.ds(e, 1), :, :].rearrange("a (c p) d -> p (a c) d", p=P))\
                  .then_inc(s_w[u], 16)

            twice_each(sp, E // 2, load)
            sp.wait_ge(s_sca, 16 * E)

        @block.gpsimd
        def _(pool):
            pool.wait_ge(k.s_rows, 16 * B)
            for e in range(E):
                nc.gpsimd.indirect_dma_start(out=xe[0:CAP0, e, :], out_offset=None, in_=dram.normed[:, :],
                                             in_offset=bass.IndirectOffsetOnAxis(ap=k.SLOT_ROW[0:CAP0, 0, e:e + 1],
                                                                                 axis=0)).then_inc(s_gat, 16)
            pool.wait_ge(k.s_zeroed, 16 * 4 * (NT // 16))
            for e in range(E):
                pool.wait_ge(s_eo, e + 1)
                nc.gpsimd.indirect_dma_start(out=delta[:, :],
                                             out_offset=bass.IndirectOffsetOnAxis(ap=k.SLOT_ROW[0:CAP0, 1, e:e + 1],
                                                                                  axis=0),
                                             in_=eo[0:CAP0, e, :], in_offset=None, bounds_check=NT * P - 1,
                                             oob_is_err=False).then_inc(s_sca, 16)

        @block.tensor
        def _(pe):
            pe.wait_ge(s_gat, 16 * E)
            for e in range(E):
                last = nc.tensor.transpose(psX[:, e // 4, (e % 4) * CAP0:(e % 4 + 1) * CAP0], xe[0:CAP0, e, :],
                                           k.IDENT[0:CAP0, 0:CAP0])
            last.then_inc(s_tr, 1)
            pe.wait_ge(s_xt, 2)

            def expert(i, u):
                e = 2 * i + u
                pe.wait_ge(s_w[u], 32 * (i + 1))
                for c in range(FC0):
                    last = nc.tensor.matmul(psA[u][:, c * CAP0:(c + 1) * CAP0], w1[u][:, c * P:(c + 1) * P],
                                            xet[:, bass.ds(e * CAP0, CAP0)], start=True, stop=True)
                last.then_inc(s_up, 1)
                after(pe, s_eo, e - 1)
                nc.tensor.matmul(psB[u][0:CAP0, 0:D], k.ONES[0:1, 0:CAP0], k.B2[0:1, bass.ds(e * D, D)],
                                 start=True, stop=False)
                pe.wait_ge(s_hid, FC0 * (e + 1))
                for c in range(FC0):
                    last = nc.tensor.matmul(psB[u][0:CAP0, 0:D], hid[u][:, c, :], w2[u][:, c, :],
                                            start=False, stop=(c == FC0 - 1))
                last.then_inc(s_dn, 1)

            twice_each(pe, E // 2, expert)

        @block.scalar
        def _(act):
            def gelu(i, u):
                e = 2 * i + u
                after(act, s_dn, e - 1)
                act.wait_ge(s_up, e + 1)
                for c in range(FC0):
                    nc.scalar.activation(hid[u][:, c, :], psA[u][:, c * CAP0:(c + 1) * CAP0], ACT.Gelu_apprx_tanh,
                                         bias=k.B1T[:, bass.ds(e * FC0 + c, 1)]).then_inc(s_hid, 1)

            twice_each(act, E // 2, gelu)

        @block.vector
        def _(dve):
            dve.wait_ge(s_tr, 1)
            for h in range(2):
                nc.vector.tensor_copy(xet[:, h * 4 * CAP0:(h + 1) * 4 * CAP0], psX[:, h, 0:4 * CAP0]).then_inc(s_xt, 1)

            def evacuate(i, u):
                e = 2 * i + u
                dve.wait_ge(s_dn, e + 1)
                nc.vector.tensor_copy(eo[0:CAP0, bass.ds(e, 1), :].rearrange("p a d -> p (a d)"),
                                      psB[u][0:CAP0, 0:D]).then_inc(s_eo, 1)

            twice_each(dve, E // 2, evacuate)


def attention0(nc, name, k, delta, gate):
    with ExitStack() as ctx:
        st = Stage(nc, ctx, name)
        xn = st.sb("xn", [P, NT, D])
        go = st.sb("go", [P, NT, D])
        on = st.sb("on", [P, NT, D])
        sq = st.sb("sq", [P, 2, D])
        ont = [st.sb(f"ont{u}", [P, T]) for u in range(2)]
        ss = st.sb("ss", [P, NT])
        rn = st.sb("rn", [P, NT])
        seq = st.sb("seq", [P, NT])
        fam = st.sb("fam", [P, NT])
        em = st.sb("em", [P, NT])
        att = st.sb("att", [P, NT])
        psT = [st.ps(f"psT{u}", [P, T]) for u in range(2)]
        psM = [st.ps(f"psM{j}", [P, T]) for j in range(TPB)]
        psE = [st.ps(f"psE{h}", [P, 512]) for h in range(2)]
        s_go = st.sem("go")
        s_ss = st.sem("ss")
        s_nrm = st.sem("nrm")
        s_rn = st.sem("rn")
        s_on = st.sem("on")
        s_tr = st.sem("tr")
        s_ot = st.sem("ot")
        s_sim = st.sem("sim")
        s_max = st.sem("max")
        s_vec = st.sem("vec")
        s_nov = st.sem("nov")
        s_x = st.sem("x")
        STEPS = 5
        PARTS = [range(0, 2), range(2, B)]
        cols = [slice(p[0] * TPB, (p[-1] + 1) * TPB) for p in PARTS]
        halves = [slice(h * NT // 2, (h + 1) * NT // 2) for h in range(2)]
        fold = Fold(nc, st, k, delta, gate)
        norm = Norm(nc, st, k, xn, GROUPS, fold)
        block = st.block()

        @block.sync
        def _(sp):
            fold.load(sp)

        @block.gpsimd
        def _(pool):
            norm.gpsimd(pool)

        @block.vector
        def _(dve):
            norm.vector(dve)

            def inverse(n):
                dve.wait_ge(s_nrm, n + 1)
                nc.vector.tensor_scalar(rn[:, cols[n]], rn[:, cols[n]], 1e-12, None, ALU.max).then_inc(s_rn, 1)
                dve.wait_ge(s_rn, 2 * n + 1)
                nc.vector.reciprocal(rn[:, cols[n]], rn[:, cols[n]]).then_inc(s_rn, 1)

            def largest(b):
                for t in range(b * TPB, (b + 1) * TPB):
                    dve.wait_ge(s_sim, t + 1)
                    nc.vector.tensor_reduce(seq[:, t:t + 1], psM[t % TPB][:, 0:(t % TPB + 1) * P], AX, ALU.max)\
                      .then_inc(s_max, 1)

            link = Chain(dve, s_vec)

            def familiar(h):
                c = halves[h]
                dve.wait_ge(s_max, NT // 2 * (h + 1))
                link(nc.vector.tensor_tensor(fam[:, c], psE[h][:, c], k.FIRST[:, c], ALU.add))
                link(nc.vector.tensor_tensor(seq[:, c], seq[:, c], fam[:, c], ALU.max))
                link(nc.vector.tensor_scalar(em[:, c], psE[h][:, c], k.SCAL[:, 4:5], None, ALU.mult))
                link(nc.vector.scalar_tensor_tensor(out=fam[:, c], in0=seq[:, c], scalar=k.SCAL[:, 2:3],
                                                    in1=em[:, c], op0=ALU.mult, op1=ALU.add))

            def attended(h):
                c = halves[h]
                dve.wait_ge(s_nov, h + 1)
                link(nc.vector.tensor_scalar(att[:, c], att[:, c], k.SCAL[:, 1:2], k.SCAL[:, 3:4], ALU.mult, ALU.add))

            def add(t):
                nc.vector.scalar_tensor_tensor(out=k.X[:, t, :], in0=go[:, t, :], scalar=att[:, t:t + 1],
                                               in1=k.X[:, t, :], op0=ALU.mult, op1=ALU.add).then_inc(s_x, 1)

            inverse(0)
            largest(0)
            inverse(1)
            for b in range(1, B):
                largest(b)
                if b == B // 2 - 1:
                    familiar(0)
                if b == B // 2:
                    attended(0)
                if b >= B // 2 and b < B - 1:
                    for t in range((b - B // 2) * 6, min((b - B // 2 + 1) * 6, NT // 2)):
                        add(t)
            familiar(1)
            attended(1)
            for t in range(NT // 2, NT):
                add(t)

        @block.scalar
        def _(act):
            def gelu(b):
                norm.wait_quad(act, b)
                nc.scalar.activation(go[:, b * TPB:(b + 1) * TPB, :], xn[:, b * TPB:(b + 1) * TPB, :],
                                     ACT.Gelu_apprx_tanh).then_inc(s_go, 1)

            def length(b):
                act.wait_ge(s_go, b + 1)
                for t in range(b * TPB, (b + 1) * TPB):
                    if t >= 2:
                        act.wait_ge(s_ss, t - 1)
                    nc.scalar.activation(sq[:, t % 2, :], go[:, t, :], ACT.Square, accum_out=ss[:, t:t + 1])\
                      .then_inc(s_ss, 1)

            def root(n):
                act.wait_ge(s_ss, cols[n].stop)
                nc.scalar.activation(rn[:, cols[n]], ss[:, cols[n]], ACT.Sqrt).then_inc(s_nrm, 1)

            def unit(b):
                for t in range(b * TPB, (b + 1) * TPB):
                    nc.scalar.activation(on[:, t, :], go[:, t, :], ACT.Identity, scale=rn[:, t:t + 1])\
                      .then_inc(s_on, 1)

            def turned(b):
                if b >= 2:
                    act.wait_ge(s_sim, (b - 1) * TPB)
                act.wait_ge(s_tr, b + 1)
                nc.scalar.copy(ont[b % 2][:, :], psT[b % 2][:, :]).then_inc(s_ot, 1)

            norm.root(act, 0)
            for g in range(len(GROUPS)):
                norm.odd_tiles(act, g)
                if g + 1 < len(GROUPS):
                    norm.root(act, g + 1)
            gelu(0)
            gelu(1)
            length(0)
            length(1)
            root(0)
            gelu(2)
            act.wait_ge(s_rn, 2)
            unit(0)
            gelu(3)
            unit(1)
            turned(0)
            length(2)
            length(3)
            for b in range(4, B):
                gelu(b)
                if b == 5:
                    turned(1)
                if b >= 5:
                    length(b - 1)
            length(B - 1)
            root(1)
            act.wait_ge(s_rn, 4)
            for b in range(2, B + 1):
                if b < B:
                    unit(b)
                if b >= 3:
                    turned(b - 1)
                if b == 6:
                    act.wait_ge(s_vec, STEPS - 1)
                    nc.scalar.activation(att[:, halves[0]], fam[:, halves[0]], ACT.Exp, scale=k.SCAL[:, 0:1])\
                      .then_inc(s_nov, 1)
            act.wait_ge(s_vec, 2 * STEPS - 1)
            nc.scalar.activation(att[:, halves[1]], fam[:, halves[1]], ACT.Exp, scale=k.SCAL[:, 0:1])\
              .then_inc(s_nov, 1)

        @block.tensor
        def _(pe):
            def turn(b):
                pe.wait_ge(s_on, TPB * (b + 1))
                if b >= 2:
                    pe.wait_ge(s_ot, b - 1)
                for j in range(TPB):
                    last = nc.tensor.transpose(psT[b % 2][:, j * P:(j + 1) * P], on[:, b * TPB + j, :],
                                               k.IDENT[:, :])
                last.then_inc(s_tr, 1)

            turn(0)
            for b in range(B):
                if b + 1 < B:
                    turn(b + 1)
                pe.wait_ge(s_ot, b + 1)
                for j in range(TPB):
                    t, n = b * TPB + j, (j + 1) * P
                    if b >= 1:
                        pe.wait_ge(s_max, t - TPB + 1)
                    mine = ont[b % 2][:, j * P:(j + 1) * P]
                    nc.tensor.matmul(psM[j][:, 0:n], mine, ont[b % 2][:, 0:n], start=True, stop=False)
                    nc.tensor.matmul(psM[j][:, n - P:n], k.IDENTB[:, :], k.PAST[:, :], start=False, stop=True)
                    nc.tensor.matmul(psE[t // (NT // 2)][:, t:t + 1], mine, k.EMA[:, 0:1], start=True, stop=True,
                                     skip_group_check=True).then_inc(s_sim, 1)


def route1(nc, name, k):
    with ExitStack() as ctx:
        st = Stage(nc, ctx, name)
        w = Work(st)
        mask = st.sb("mask", [P, 2, NT, E], BF16)
        cnt = st.sb("cnt", [P, B, E])
        pos = st.sb("pos", [P, 2, NT])
        rank = st.sb("rank", [P, 2, NT])
        val = st.sb("val", [P, 2, NT])
        kb = st.sb("kb", [P, 2, NT])
        gt = st.sb("gt", [P, 2, NT])
        slot = st.sb("slot", [P, 2, NT])
        rec = st.sb("rec", [P, 2, NT, 6], BF16)
        part = st.sb("part", [P, 2, NT])
        NB = 4
        hot = [st.sb(f"hot{i}", [P, E * CAP1], BF16) for i in range(NB)]
        got = st.sb("got", [P, B * E, 6])
        row = st.sb("row", [P, 2, B * E])
        psM = st.ps("psM", [P, 512])
        s_hot = st.sem("hot")
        s_use = st.sem("use")
        psC = st.ps("psC", [P, 2, NT * E])
        psN = st.ps("psN", [P, 512])
        s_vec = st.sem("vec")
        s_exp = st.sem("exp")
        s_cnt = st.sem("cnt")
        block = st.block()
        over = lambda v: v.unsqueeze(2).to_broadcast([P, NT, E])

        @block.sync
        def _(sp):
            sp.wait_ge(k.s_rows, 16 * B)

        @block.scalar
        def _(act):
            act.wait_ge(s_vec, 2)
            nc.scalar.activation(w.q[:, :, :], w.p[:, :, :], ACT.Exp).then_inc(s_exp, 1)

        @block.vector
        def _(dve):
            link = Chain(dve, s_vec)
            softmax_over_experts(nc, dve, link, k, w, s_exp)
            first_largest(nc, link, k, w, w.p[:, :, :], val[:, 0, :], rank[:, 0, :], mask[:, 0, :, :])
            link(nc.vector.tensor_tensor(w.s[:, :, :], w.q[:, :, :], over(rank[:, 0, :]), ALU.not_equal))
            link(nc.vector.tensor_tensor(w.s[:, :, :], w.s[:, :, :], w.p[:, :, :], ALU.mult))
            first_largest(nc, link, k, w, w.s[:, :, :], val[:, 1, :], rank[:, 1, :], mask[:, 1, :, :])
            assert link.n == 17
            dve.wait_ge(s_cnt, 1)
            link(nc.vector.tensor_scalar(cnt[:, :, :], psN[:, 0:B * E].rearrange("p (g e) -> p g e", e=E),
                                         float(CAP1), None, ALU.min))
            link(nc.vector.tensor_tensor(w.q[:, :, :], psC[:, 0, :].rearrange("p (t e) -> p t e", e=E),
                                         mask[:, 0, :, :], ALU.mult))
            link(nc.vector.tensor_reduce(pos[:, 0, :], w.q[:, :, :], AX, ALU.add))
            link(nc.vector.tensor_tensor(w.q[:, :, :].rearrange("p (g j) e -> p g j e", j=TPB),
                                         psC[:, 1, :].rearrange("p (g j e) -> p g j e", j=TPB, e=E),
                                         cnt[:, :, :].unsqueeze(2).to_broadcast([P, B, TPB, E]), ALU.add))
            link(nc.vector.tensor_tensor(w.q[:, :, :], w.q[:, :, :], mask[:, 1, :, :], ALU.mult))
            link(nc.vector.tensor_reduce(pos[:, 1, :], w.q[:, :, :], AX, ALU.add))
            link(nc.vector.tensor_scalar(kb[:, :, :], pos[:, :, :], CAP1 + 0.5, 0.5, ALU.is_le, ALU.mult))
            link(nc.vector.tensor_tensor(gt[:, :, :], kb[:, :, :], val[:, :, :], ALU.mult))
            link(nc.vector.tensor_scalar(kb[:, :, :], gt[:, :, :], 0.0, float(SKIP), ALU.is_equal, ALU.mult))
            link(nc.vector.scalar_tensor_tensor(out=flat(slot[:, :, :]), in0=flat(rank[:, :, :]),
                                                scalar=-float(CAP1), in1=flat(pos[:, :, :]),
                                                op0=ALU.mult, op1=ALU.add))
            link(nc.vector.scalar_tensor_tensor(out=flat(slot[:, :, :]), in0=flat(kb[:, :, :]),
                                                scalar=float(E * CAP1 - 1), in1=flat(slot[:, :, :]),
                                                op0=ALU.add, op1=ALU.add))
            for c in range(2):
                nc.vector.tensor_copy(rec[:, c, :, 0:3], k.IDS[:, :, :]).then_inc(s_hot, 1)
            link(nc.vector.tensor_copy(rec[:, :, :, 3], gt[:, :, :]))
            link(nc.vector.tensor_tensor(part[:, :, :], gt[:, :, :], rec[:, :, :, 3], ALU.subtract))
            link(nc.vector.tensor_copy(rec[:, :, :, 4], part[:, :, :]))
            link(nc.vector.tensor_tensor(part[:, :, :], part[:, :, :], rec[:, :, :, 4], ALU.subtract))
            link(nc.vector.tensor_copy(rec[:, :, :, 5], part[:, :, :]))
            for n in range(2 * NT):
                t, c = n // 2, n % 2
                if n >= NB:
                    dve.wait_ge(s_use, n - NB + 1)
                nc.vector.tensor_scalar(hot[n % NB][:, :], k.IOTA[:, :], slot[:, c, t:t + 1], None,
                                        ALU.is_equal).then_inc(s_hot, 1)
            dve.wait_ge(s_use, 2 * NT)
            link(nc.vector.tensor_copy(got[:, :, :], psM[:, 0:6 * B * E].rearrange("p (g a) -> p g a", a=6)))
            link(nc.vector.scalar_tensor_tensor(out=row[:, 0, :], in0=got[:, :, 0], scalar=float(P),
                                                in1=got[:, :, 1], op0=ALU.mult, op1=ALU.add))
            link(nc.vector.tensor_scalar(row[:, 1, :], got[:, :, 2], -float(SKIP), float(SKIP), ALU.mult, ALU.add))
            link(nc.vector.tensor_tensor(row[:, 1, :], row[:, 1, :], row[:, 0, :], ALU.add))
            link(nc.vector.tensor_copy(k.SRC_ROW[:, :], row[:, 0, :]))
            link(nc.vector.tensor_copy(k.DST_ROW[:, :], row[:, 1, :]))
            link(nc.vector.tensor_tensor(k.SGATE[:, :], got[:, :, 3], got[:, :, 4], ALU.add))
            link(nc.vector.tensor_tensor(k.SGATE[:, :], k.SGATE[:, :], got[:, :, 5], ALU.add))

        @block.tensor
        def _(pe):
            pe.wait_ge(s_vec, 17)
            for c in range(2):
                out = psC[:, c, :].rearrange("p (g j e) -> p g j e", j=TPB, e=E)
                m = mask[:, c, :, :].rearrange("p (g j) e -> p g j e", j=TPB)
                nc.tensor.matmul(psC[:, c, :], k.TRIU[:, :], mask[:, c, :, :].rearrange("p t e -> p (t e)"),
                                 start=True, stop=False, skip_group_check=True)
                for s in range(1, TPB):
                    nc.tensor.matmul(out[:, :, s:TPB, :], k.ONESB[:, :], m[:, :, 0:TPB - s, :], start=False,
                                     stop=(s == TPB - 1), skip_group_check=True)
            for j in range(TPB):
                last = nc.tensor.matmul(psN[:, 0:B * E], k.ONESB[:, :],
                                        mask[:, 0, :, :].rearrange("p (g j) e -> p g j e", j=TPB)[:, :, j, :],
                                        start=(j == 0), stop=(j == TPB - 1), skip_group_check=True)
            last.then_inc(s_cnt, 1)
            for n in range(2 * NT):
                t, c = n // 2, n % 2
                pe.wait_ge(s_hot, n + 3)
                for e in range(E):
                    at = 6 * (t // TPB * E + e)
                    last = nc.tensor.matmul(psM[:, at:at + 6], hot[n % NB][:, e * CAP1:(e + 1) * CAP1],
                                            rec[:, c, t, :], start=(n == 0 and e == 0), stop=(n == 2 * NT - 1),
                                            skip_group_check=True)
                last.then_inc(s_use, 1)


def experts1(nc, name, k, dram, delta):
    with ExitStack() as ctx:
        st = Stage(nc, ctx, name)
        HP = HC1 * P
        raw = st.sb("raw", [P, 3, HP])
        wh = [st.sb(f"wh{u}", [P, 3, HP], F32R) for u in range(2)]
        wl = [st.sb(f"wl{u}", [P, 3, HP], F32R) for u in range(2)]
        xe = [st.sb(f"xe{h}", [P, HALF, D]) for h in range(2)]
        xh = [st.sb(f"xh{h}", [P, 512], F32R) for h in range(2)]
        xl = [st.sb(f"xl{h}", [P, 512], F32R) for h in range(2)]
        ge = [st.sb(f"ge{c}", [P, 512]) for c in range(2)]
        hid = [st.sb(f"hid{c}", [P, 512]) for c in range(2)]
        hh = [st.sb(f"hh{c}", [P, 512], F32R) for c in range(3)]
        hl = [st.sb(f"hl{c}", [P, 512], F32R) for c in range(3)]
        eot = st.sb("eot", [P, 512])
        eo = [st.sb(f"eo{h}", [P, HALF, D]) for h in range(2)]
        psA = [st.ps(f"psA{c}", [P, 512]) for c in range(2)]
        psB = [st.ps(f"psB{c}", [P, 512]) for c in range(2)]
        psY = [st.ps(f"psY{h}", [P, 512]) for h in range(2)]
        psX = st.ps("psX", [P, 512])
        psO = st.ps("psO", [P, 512])
        s_zero = st.sem("zero")
        s_w = st.sem("w")
        s_wh = st.sem("wh")
        s_wl = st.sem("wl")
        s_xe = [st.sem(f"xe{h}") for h in range(2)]
        s_tr = st.sem("tr")
        s_xh = st.sem("xh")
        s_xl = st.sem("xl")
        s_up = st.sem("up")
        s_ge = st.sem("ge")
        s_hid = st.sem("hid")
        s_hh = st.sem("hh")
        s_hl = st.sem("hl")
        s_dn = st.sem("dn")
        s_et = st.sem("et")
        s_op = st.sem("op")
        s_eo = st.sem("eo")
        s_sc = [st.sem(f"sc{h}") for h in range(2)]
        block = st.block()
        f32 = lambda ap: ap.bitcast(F32)

        def rounds(eng, body, drain):
            def one(q):
                for u in range(2):
                    for h in range(2):
                        body(4 * q + 2 * u + h, 2 * q + u, u, h,
                             isinstance(q, int) and q == E // 2 - 1 and u == 1 and h == 1)
            one(0)
            with eng.Fori(1, E // 2 - 1) as q:
                one(q)
            one(E // 2 - 1)
            drain()

        @block.sync
        def _(sp):
            sp.wait_ge(s_zero, 1)

            def load(e):
                after(sp, s_wl, 3 * e)
                for n, w in enumerate((dram.w0k, dram.w1k)):
                    sp.dma_start(raw[:, n, 0:H1], w[bass.ds(e, 1), :, :].rearrange("a d f -> (a d) f"))\
                      .then_inc(s_w, 16)
                sp.dma_start(raw[:, 2, 0:HP - P].rearrange("p (c d) -> p c d", c=HC1 - 1),
                             dram.wok[bass.ds(e, 1), 0:HP - P, :].rearrange("a (c p) d -> p (a c) d", p=P))\
                  .then_inc(s_w, 16)
                sp.dma_start(raw[0:HREST, 2, HP - P:HP],
                             dram.wok[bass.ds(e, 1), HP - P:H1, :].rearrange("a p d -> (a p) d")).then_inc(s_w, 16)

            load(0)
            with sp.Fori(1, E) as e:
                load(e)

        @block.gpsimd
        def _(pool):
            def gather(n):
                e, h = n // 2, n % 2
                if n >= 2:
                    pool.wait_ge(s_tr, n - 1)
                for g in range(HALF):
                    col = (h * HALF + g) * E + e
                    nc.gpsimd.indirect_dma_start(
                        out=xe[h][:, g, :], out_offset=None, in_=dram.normed[:, :],
                        in_offset=bass.IndirectOffsetOnAxis(ap=k.SRC_ROW[:, col:col + 1], axis=0))\
                      .then_inc(s_xe[h], 16)

            def scatter(n):
                e, h = n // 2, n % 2
                if e >= 1:
                    pool.wait_ge(s_sc[h], 16 * HALF * e)
                for g in range(HALF):
                    col = (h * HALF + g) * E + e
                    pool.wait_ge(s_eo, HALF * n + g + 1)
                    nc.gpsimd.indirect_dma_start(
                        out=delta[:, :], out_offset=bass.IndirectOffsetOnAxis(ap=k.DST_ROW[:, col:col + 1], axis=0),
                        in_=eo[h][:, g, :], in_offset=None, bounds_check=B * T - 1, oob_is_err=False,
                        compute_op=ALU.add).then_inc(s_sc[h], 16)

            AHEAD = 4
            pool.wait_ge(k.s_rows, 16 * B)
            for n in range(AHEAD):
                gather(n)
            for n in range(2 * E):
                if n + AHEAD < 2 * E:
                    gather(n + AHEAD)
                scatter(n)
            for h in range(2):
                pool.wait_ge(s_sc[h], 16 * HALF * E)

        @block.tensor
        def _(pe):
            def turn(n, e, h):
                pe.wait_ge(s_xe[h], 16 * HALF * (e + 1))
                after(pe, s_xl, n)
                for g in range(HALF):
                    last = nc.tensor.transpose(psX[:, g * CAP1:(g + 1) * CAP1], xe[h][:, g, :], k.IDENT[:, :])
                last.then_inc(s_tr, 1)

            def three(out, n, c, u, mh, ml, first, last):
                cs = slice(c * P, (c + 1) * P)
                nc.tensor.matmul(out, wh[u][:, n, cs], mh, start=first, stop=False)
                nc.tensor.matmul(out, wh[u][:, n, cs], ml, start=False, stop=False)
                return nc.tensor.matmul(out, wl[u][:, n, cs], mh, start=False, stop=last)

            def down(n, c, u, h):
                pe.wait_ge(s_hl, HC1 * n + c + 1)
                if c == 0:
                    after(pe, s_et, n - 1)
                three(psY[h][:, :], 2, c, u, hh[c % 3][:, :], hl[c % 3][:, :], c == 0, c == HC1 - 1)\
                    .then_inc(s_dn, 1)

            def turn_back(n):
                pe.wait_ge(s_et, n + 1)
                after(pe, s_eo, HALF * n)
                for g in range(HALF):
                    last = nc.tensor.transpose(psO[:, g * P:(g + 1) * P], eot[:, g * CAP1:(g + 1) * CAP1],
                                               k.IDENT[:, :])
                last.then_inc(s_op, 1)

            def unit(n, e, u, h, last):
                pe.wait_ge(s_xl, n + 1)
                pe.wait_ge(s_wl, 3 * e + 3)
                for c in range(HC1):
                    after(pe, s_hid, HC1 * n + c - 1)
                    three(psA[c % 2][:, :], 0, c, u, xh[h][:, :], xl[h][:, :], True, True)
                    three(psB[c % 2][:, :], 1, c, u, xh[h][:, :], xl[h][:, :], True, True).then_inc(s_up, 1)
                    if c >= 2:
                        down(n, c - 2, u, h)
                    elif not (isinstance(n, int) and n == 0):
                        down(n - 1, HC1 - 2 + c, u if h else 1 - u, 1 - h)
                    if c == 2 and not last:
                        turn(n + 1, e + h, 1 - h)
                    if c == 4 and not (isinstance(n, int) and n == 0):
                        turn_back(n - 1)

            def drain():
                n = 2 * E - 1
                down(n, HC1 - 2, 1, 1)
                down(n, HC1 - 1, 1, 1)
                turn_back(n)

            turn(0, 0, 0)
            rounds(pe, unit, drain)

        @block.scalar
        def _(act):
            def weight(e, n, u):
                if n == 0:
                    act.wait_ge(s_w, 64 * (e + 1))
                    after(act, s_dn, HC1 * 2 * (e - 1))
                nc.scalar.copy(wh[u][:, n, :], raw[:, n, :]).then_inc(s_wh, 1)

            def rows(n, h):
                after(act, s_up, HC1 * (n - 1))
                act.wait_ge(s_tr, n + 1)
                nc.scalar.copy(xh[h][:, :], psX[:, :]).then_inc(s_xh, 1)

            def high(n, c):
                act.wait_ge(s_hid, HC1 * n + c + 1)
                after(act, s_dn, HC1 * n + c - 2)
                nc.scalar.copy(hh[c % 3][:, :], hid[c % 2][:, :]).then_inc(s_hh, 1)

            def result(n, h):
                act.wait_ge(s_dn, HC1 * (n + 1))
                after(act, s_op, n)
                nc.scalar.copy(eot[:, :], psY[h][:, :]).then_inc(s_et, 1)

            def unit(n, e, u, h, last):
                first = isinstance(n, int) and n == 0
                for c in range(HC1):
                    act.wait_ge(s_up, HC1 * n + c + 1)
                    after(act, s_hid, HC1 * n + c - 1)
                    nc.scalar.activation(ge[c % 2][:, :], psA[c % 2][:, :], ACT.Gelu_apprx_tanh).then_inc(s_ge, 1)
                    if c >= 1:
                        high(n, c - 1)
                    elif not first:
                        high(n - 1, HC1 - 1)
                    if c == 2 and not first:
                        result(n - 1, 1 - h)
                    if c == 3 and not last:
                        rows(n + 1, 1 - h)
                    if not (isinstance(e, int) and e == E - 1):
                        if h == 0 and c in (3, 5):
                            weight(e + 1, (c - 3) // 2, 1 - u)
                        if h == 1 and c == 2:
                            weight(e + 1, 2, 1 - u)

            def drain():
                high(2 * E - 1, HC1 - 1)
                result(2 * E - 1, 1)

            for n in range(3):
                weight(0, n, 0)
            rows(0, 0)
            rounds(act, unit, drain)

        @block.vector
        def _(dve):
            nc.vector.memset(raw[:, :, :], 0.0).then_inc(s_zero, 1)

            def weight(e, n, u):
                dve.wait_ge(s_wh, 3 * e + n + 1)
                nc.vector.tensor_tensor(wl[u][:, n, :], raw[:, n, :], f32(wh[u][:, n, :]), ALU.subtract)\
                  .then_inc(s_wl, 1)

            def rows(n, h):
                dve.wait_ge(s_xh, n + 1)
                nc.vector.tensor_tensor(xl[h][:, :], psX[:, :], f32(xh[h][:, :]), ALU.subtract).then_inc(s_xl, 1)

            def low(n, c):
                dve.wait_ge(s_hh, HC1 * n + c + 1)
                nc.vector.tensor_tensor(hl[c % 3][:, :], hid[c % 2][:, :], f32(hh[c % 3][:, :]), ALU.subtract)\
                  .then_inc(s_hl, 1)

            def gated(n, e, h):
                dve.wait_ge(s_op, n + 1)
                after(dve, s_sc[h], 16 * HALF * e)
                for g in range(HALF):
                    col = (h * HALF + g) * E + e
                    nc.vector.tensor_scalar(eo[h][:, g, :], psO[:, g * P:(g + 1) * P],
                                            k.SGATE[:, bass.ds(col, 1)], None, ALU.mult).then_inc(s_eo, 1)

            def unit(n, e, u, h, last):
                first = isinstance(n, int) and n == 0
                for c in range(HC1):
                    after(dve, s_hl, HC1 * n + c - 1)
                    dve.wait_ge(s_ge, HC1 * n + c + 1)
                    nc.vector.tensor_tensor(hid[c % 2][:, :], ge[c % 2][:, :], psB[c % 2][:, :], ALU.mult)\
                      .then_inc(s_hid, 1)
                    if c >= 1:
                        low(n, c - 1)
                    elif not first:
                        low(n - 1, HC1 - 1)
                    if c == 3 and not last:
                        rows(n + 1, 1 - h)
                    if c == 5 and not first:
                        gated(n - 1, e + h - 1, 1 - h)
                    if not (isinstance(e, int) and e == E - 1):
                        if h == 0 and c in (3, 5):
                            weight(e + 1, (c - 3) // 2, 1 - u)
                        if h == 1 and c == 2:
                            weight(e + 1, 2, 1 - u)

            def drain():
                low(2 * E - 1, HC1 - 1)
                gated(2 * E - 1, E - 1, 1)

            for n in range(3):
                weight(0, n, 0)
            rows(0, 0)
            rounds(dve, unit, drain)


def attention1(nc, name, k):
    with ExitStack() as ctx:
        st = Stage(nc, ctx, name)
        D0 = [st.sb(f"D0{u}", [P, CH + 1, B, 3]) for u in range(2)]
        D1 = [st.sb(f"D1{u}", [P, CH + 1, B, 3]) for u in range(2)]
        Z = [st.sb(f"Z{u}", [P, CH + 1, B]) for u in range(2)]
        R = st.sb("R", [P, CH, B])
        S = [st.sb(f"S{u}", [P, CH + 1, B, 3]) for u in range(2)]
        HB = B // 2
        psG = [[st.ps(f"ps{n}{q}", [P, 512]) for q in range(2)] for n in "czr"]
        psO = [st.ps(f"psO{q}", [P, 512]) for q in range(2)]
        s_init = st.sem("init")
        s_pj = st.sem("pj")
        s_ev = st.sem("ev")
        s_ru = st.sem("ru")
        s_a = st.sem("a")
        s_hy = st.sem("hy")
        s_tr = st.sem("tr")
        s_x = st.sem("x")
        block = st.block()
        XT = k.XT[:, :].rearrange("p (b t) -> p b t", b=B)
        STEPS = CH + 1

        def gate_piece(act, ch, n, b):
            u = ch % 2
            src = psG[n][b // HB][:, (b % HB) * CH:(b % HB + 1) * CH]
            bias = k.COLS[:, 3 + n:4 + n]
            if n == 0:
                out, func = D1[u][:, 0:CH, b, 2], ACT.Identity
            elif n == 1:
                out, func = Z[u][:, 0:CH, b], ACT.Sigmoid
            else:
                out, func = R[:, :, b], ACT.Sigmoid
            nc.scalar.activation(out, src, func, bias=bias).then_inc(s_ev, 1)

        PIECES = [(n, b) for n in (1, 2, 0) for b in range(B)]

        @block.scalar
        def _(act):
            act.wait_ge(s_pj, 1)
            act.wait_ge(s_init, 6)
            for n, b in PIECES:
                gate_piece(act, 0, n, b)
            for ch in range(NCH):
                u = ch % 2
                todo = list(PIECES) if ch + 1 < NCH else []
                for r in range(CH):
                    act.wait_ge(s_a, ch * STEPS + r + 1)
                    nc.scalar.activation(D0[u][:, r + 1, :, 1], S[u][:, r, :, 2], ACT.Tanh).then_inc(s_hy, 1)
                    if r >= 8 and r % 4 == 0 and todo:
                        if r == 8:
                            act.wait_ge(s_pj, ch + 2)
                            if ch >= 1:
                                act.wait_ge(s_ru, 2 * ch)
                        gate_piece(act, ch + 1, *todo.pop(0))
                assert not todo

        @block.gpsimd
        def _(pool):
            for u in range(2):
                nc.gpsimd.memset(D0[u][:, :, :, :], 0.0).then_inc(s_init, 1)
                nc.gpsimd.memset(D1[u][:, :, :, :], 0.0).then_inc(s_init, 1)
                nc.gpsimd.memset(S[u][:, CH, :, :], 0.0).then_inc(s_init, 1)
            pool.wait_ge(s_init, 6)
            for ch in range(NCH):
                u = ch % 2
                pool.wait_ge(s_ev, len(PIECES) * ch + 2 * B)
                nc.gpsimd.tensor_scalar(D1[u][:, 1:CH + 1, :, 0], Z[u][:, 0:CH, :], -1.0, 1.0, ALU.mult, ALU.add)\
                  .then_inc(s_ru, 1)
                nc.gpsimd.tensor_scalar(D0[u][:, 0:CH, :, 2], R[:, :, :], k.COLS[:, 0:1], None, ALU.mult)\
                  .then_inc(s_ru, 1)

        @block.tensor
        def _(pe):
            def project(ch):
                if ch >= 1:
                    pe.wait_ge(s_ev, len(PIECES) * ch)
                for n in range(3):
                    for q in range(2):
                        last = nc.tensor.matmul(psG[n][q][:, :], k.WT[:, n * P:(n + 1) * P],
                                                XT[:, q * HB:(q + 1) * HB, ch * CH:(ch + 1) * CH],
                                                start=True, stop=True)
                last.then_inc(s_pj, 1)

            project(0)
            for ch in range(NCH):
                if ch + 1 < NCH:
                    project(ch + 1)
                pe.wait_ge(s_a, (ch + 1) * STEPS)
                if ch >= 1:
                    pe.wait_ge(s_x, B * ch)
                for b in range(B):
                    last = nc.tensor.transpose(psO[b // HB][:, (b % HB) * P:(b % HB + 1) * P],
                                               S[ch % 2][:, 1:CH + 1, b, 1], k.IDENT[:, :])
                last.then_inc(s_tr, 1)

        @block.vector
        def _(dve):
            def add_piece(ch, b):
                t = b * TPB + ch
                nc.vector.tensor_tensor(k.X[:, t, :], k.X[:, t, :], psO[b // HB][:, (b % HB) * P:(b % HB + 1) * P],
                                        ALU.add).then_inc(s_x, 1)

            dve.wait_ge(s_init, 6)
            for ch in range(NCH):
                u = ch % 2
                dve.wait_ge(s_ev, len(PIECES) * (ch + 1))
                dve.wait_ge(s_ru, 2 * (ch + 1))
                if ch >= 1:
                    dve.wait_ge(s_a, ch * STEPS)
                nc.vector.tensor_copy(D1[u][:, 0, :, 1], S[1 - u][:, CH, :, 1]).then_inc(s_hy, 1)
                for r in range(STEPS):
                    dve.wait_ge(s_hy, ch * (2 * CH + 1) + 2 * r + 1)
                    nc.vector.tensor_tensor_scan(S[u][:, r, :, :].rearrange("p b a -> p (b a)"),
                                                 D0[u][:, r, :, :].rearrange("p b a -> p (b a)"),
                                                 D1[u][:, r, :, :].rearrange("p b a -> p (b a)"), 0.0,
                                                 ALU.mult, ALU.add).then_inc(s_a, 1)
                    if r == CH:
                        break
                    dve.wait_ge(s_a, ch * STEPS + r + 1)
                    nc.vector.tensor_tensor(D1[u][:, r + 1, :, 1], Z[u][:, r, :], S[u][:, r, :, 1], ALU.mult)\
                      .then_inc(s_hy, 1)
                    if ch >= 1 and r >= 16 and r % 8 == 0 and r // 8 - 2 < B:
                        if r == 16:
                            dve.wait_ge(s_tr, ch)
                        add_piece(ch - 1, r // 8 - 2)
            dve.wait_ge(s_tr, NCH)
            for b in range(B):
                add_piece(NCH - 1, b)


def store(nc, k, out, left):
    with ExitStack() as ctx:
        st = Stage(nc, ctx, "store")
        s_out = st.sem("out")
        fold = Fold(nc, st, k, *left) if left is not None else None
        block = st.block()

        @block.vector
        def _(dve):
            if fold is not None:
                for g in range(len(GROUPS)):
                    fold.add(dve, g)

        @block.sync
        def _(sp):
            if fold is not None:
                fold.load(sp)
            o = out.rearrange("b (j p) d -> p (b j) d", p=P)
            for g, group in enumerate(GROUPS):
                if fold is not None:
                    sp.wait_ge(fold.s_f, 8 * (g + 1))
                sp.dma_start(o[:, group, :], k.X[:, group, :]).then_inc(s_out, 16)
            sp.wait_ge(s_out, 16 * len(GROUPS))


class Names:
    pass


def macaron(nc, x, ema, log_tau, log_blend, logit_blend_seq, gate_w, gate_b, w1, b1, w2, b2,
            u, W, b, gamma, beta, router_w, w0k, w1k, wok, out):
    dram = Names()
    dram.x, dram.ema, dram.log_tau, dram.log_blend, dram.logit_blend_seq = x, ema, log_tau, log_blend, logit_blend_seq
    dram.gate_w, dram.gate_b, dram.w1, dram.b1, dram.w2, dram.b2 = gate_w, gate_b, w1, b1, w2, b2
    dram.u, dram.W, dram.b, dram.gamma, dram.beta = u, W, b, gamma, beta
    dram.router_w, dram.w0k, dram.w1k, dram.wok = router_w, w0k, w1k, wok
    dram.normed = nc.dram_tensor("normed", (B * T, D), F32).ap()
    dram.delta0 = [nc.dram_tensor(f"delta{n}", (B * T, D), F32).ap() for n in range(2)]
    dram.delta1 = [nc.dram_tensor(f"delta_b{n}", (B * T, D), F32).ap() for n in range(2)]
    with ExitStack() as ctx:
        st = Stage(nc, ctx, "k")
        k = Names()
        k.X = st.sb("X", [P, NT, D])
        k.ZEROS = st.sb("ZEROS", [P, 16 * D])
        k.BN = st.sb("BN", [P, NT, 6])
        k.MEAN, k.DIF, k.VAR, k.BOTH, k.STD, k.RSTD, k.NBIAS = (
            st.sb(n, [P, NT]) for n in ("MEAN", "DIF", "VAR", "BOTH", "STD", "RSTD", "NBIAS"))
        k.IDENT = st.sb("IDENT", [P, P])
        k.TRIU = st.sb("TRIU", [P, P], BF16)
        k.ONESB = st.sb("ONESB", [P, P], BF16)
        k.ONES = st.sb("ONES", [P, P])
        k.IDENTB = st.sb("IDENTB", [P, P], BF16)
        k.PAST = st.sb("PAST", [P, P], BF16)
        k.FIRST = st.sb("FIRST", [P, NT])
        k.RESET = st.sb("RESET", [P, E * NT])
        k.IOTA = st.sb("IOTA", [P, E * CAP1], F16)
        k.IDS = st.sb("IDS", [P, NT, 3], BF16)
        k.RANK = st.sb("RANK", [P, E])
        k.GW0 = st.sb("GW0", [P, E])
        k.RW1 = st.sb("RW1", [P, E])
        k.GB0 = st.sb("GB0", [1, NT, E])
        k.B2 = st.sb("B2", [1, E * D])
        k.B1T = st.sb("B1T", [P, E * FC0])
        k.WT = st.sb("WT", [P, 3 * D])
        k.COLS = st.sb("COLS", [P, 8])
        k.SCAL = st.sb("SCAL", [P, 8])
        k.EMA = st.sb("EMA", [P, 2])
        k.GATE0 = st.sb("GATE0", [P, NT])
        k.SLOT_ROW = st.sb("SLOT_ROW", [P, 2, E], U32)
        k.SRC_ROW = st.sb("SRC_ROW", [P, B * E], U32)
        k.DST_ROW = st.sb("DST_ROW", [P, B * E], U32)
        k.SGATE = st.sb("SGATE", [P, B * E])

        def ffn0(n, **kw):
            with ExitStack() as own:
                held = Stage(nc, own, f"f0{n}")
                k.s_rows = held.sem("rows")
                with ExitStack() as routing:
                    k.psL = Stage(nc, routing, f"l0{n}").ps("psL", [P, 512])
                    k.xn = held.sb("xn", [P, NT, D])
                    normalize(nc, f"n0{n}", k, weights=k.GW0[:, :], rows=dram.normed,
                              bias=flat(k.GB0[0:1, :, :]), **kw)
                    route0(nc, f"r0{n}", k)
                experts0(nc, f"e0{n}", k, dram, dram.delta0[n])

        def ffn1(n, **kw):
            with ExitStack() as own:
                held = Stage(nc, own, f"f1{n}")
                k.s_rows = held.sem("rows")
                with ExitStack() as routing:
                    k.psL = Stage(nc, routing, f"l1{n}").ps("psL", [P, 512])
                    k.xn = Stage(nc, routing, f"x1{n}").sb("xn", [P, NT, D])
                    normalize(nc, f"n1{n}", k, weights=k.RW1[:, :], rows=dram.normed, **kw)
                    route1(nc, f"r1{n}", k)
                experts1(nc, f"e1{n}", k, dram, dram.delta1[n])

        def attn1(**kw):
            with ExitStack() as own:
                held = Stage(nc, own, "t1")
                k.XT = held.sb("XT", [P, B * T])
                k.xn = held.sb("xn", [P, NT, D])
                normalize(nc, "n2", k, keep_t=k.XT, groups=[slice(ch, NT, TPB) for ch in range(TPB)], **kw)
                attention1(nc, "a1", k)

        d0, d1, g0 = dram.delta0, dram.delta1, k.GATE0
        stages = [
            lambda: ffn0(0), lambda: attention0(nc, "a0", k, d0[0], g0), lambda: ffn0(1),
            lambda: ffn1(0, delta=d0[1], gate=g0), lambda: attn1(delta=d1[0]), lambda: ffn1(1),
        ]
        Stage.used.clear()
        setup(nc, k, dram)
        for n, s in enumerate(stages):
            if n in (3, 5):
                recycle(nc)
            s()
        store(nc, k, out, (d1[1], None))


_INS = ['L0_attn_x', 'L0_attn_ema_out', 'L0_attn_log_tau', 'L0_attn_log_blend', 'L0_attn_logit_blend_seq',
        'L0_ffn_gate_w', 'L0_ffn_gate_b', 'L0_ffn_w1', 'L0_ffn_b1', 'L0_ffn_w2', 'L0_ffn_b2',
        'L1_attn_u', 'L1_attn_W', 'L1_attn_b', 'L1_attn_gamma', 'L1_attn_beta',
        'L1_ffn_router_w', 'L1_ffn_w0_kernel', 'L1_ffn_w1_kernel', 'L1_ffn_wo_kernel']
_OUT = (B, T, D)


def kernel(**inputs):
    import numpy as _np
    import concourse.bacc as _bacc
    from concourse import mybir as _mybir
    from concourse.bass_utils import run_bass_kernel_spmd as _run

    nc = _bacc.Bacc("TRN2", target_bir_lowering=False, num_devices=1)
    arrays, args = {}, []
    for name in _INS:
        a = _np.ascontiguousarray(inputs[name])
        arrays[f"in_{name}_dram"] = a
        args.append(nc.dram_tensor(f"in_{name}_dram", a.shape, _mybir.dt.from_np(a.dtype), kind="ExternalInput").ap())
    out = nc.dram_tensor("out_0_dram", _OUT, _mybir.dt.float32, kind="ExternalOutput").ap()
    macaron(nc, *args, out)
    r = _run(nc, [arrays], core_ids=[0])
    return r.results[0]["out_0_dram"]
```

```python
from contextlib import ExitStack

import concourse.bass as bass
from concourse import mybir

F32 = mybir.dt.float32
F16 = mybir.dt.float16
F32R = mybir.dt.float32r
BF16 = mybir.dt.bfloat16
I32 = mybir.dt.int32
U32 = mybir.dt.uint32
ALU = mybir.AluOpType
ACT = mybir.ActivationFunctionType
AX = mybir.AxisListType.X

P = 128
D = 128
B, T = 8, 512
NT = B * T // P
TPB = T // P
E = 8
LN_EPS = 1e-5

CAP0 = 80
F0 = 512
FC0 = F0 // P

CAP1 = 128
H1 = 688
HC1 = -(-H1 // P)
HREST = H1 - (HC1 - 1) * P
FULL1 = (HC1 - 1) * P
COL_W0, COL_W1, COL_REST, COL_WO = 0, FULL1, 2 * FULL1, 2 * FULL1 + P
COLS1 = COL_WO + HC1 * P
PIECES1 = [slice(0, COL_W1), slice(COL_W1, COL_WO), slice(COL_WO, COLS1)]
HALF = B // 2
SKIP = 1 << 16

CH = 128
NCH = T // CH


GROUPS = [slice(g * 8, (g + 1) * 8) for g in range(NT // 8)]
QUADS = 2


def flat(ap):
    return ap.rearrange("p a b -> p (a b)")


def after(eng, sem, value):
    if not (isinstance(value, int) and value <= 0):
        eng.wait_ge(sem, value)


class Names:
    pass


class Chain:

    def __init__(self, eng, sem):
        self.eng, self.sem, self.n = eng, sem, 0

    def beside(self, instruction):
        self.n += 1
        instruction.then_inc(self.sem, 1)

    def __call__(self, instruction):
        self.beside(instruction)
        self.eng.wait_ge(self.sem, self.n)


class Stage:

    used = []

    def __init__(self, nc, ctx, name):
        self.nc, self.ctx, self.name = nc, ctx, name

    def sb(self, name, shape, dt=F32):
        return self.ctx.enter_context(self.nc.sbuf_tensor(f"{self.name}_{name}", shape, dt))

    def ps(self, name, shape, dt=F32):
        return self.ctx.enter_context(self.nc.psum_tensor(f"{self.name}_{name}", shape, dt))

    def sem(self, name):
        handle = self.nc.alloc_semaphore(f"{self.name}_{name}")
        Stage.used.append(handle)
        return handle

    def block(self):
        return self.ctx.enter_context(self.nc.Block())


def recycle(nc):
    nc.clear_and_free_semaphores(list(Stage.used))
    Stage.used.clear()
    nc.all_engine_barrier()


def write_zeros(sp, k, delta):
    rows = 16 * P
    for n in range(NT // 16):
        sp.dma_start(delta[n * rows:(n + 1) * rows, :].rearrange("(p a) d -> p (a d)", p=P), k.ZEROS[:, :])\
          .then_inc(k.s_zeroed, 16)


def setup(nc, k, dram):
    with ExitStack() as ctx:
        st = Stage(nc, ctx, "set")
        iota = st.sb("iota", [P, CAP1], I32)
        ids = st.sb("ids", [P, 3, NT], I32)
        bcol = st.sb("bcol", [E * FC0, P])
        wrows = st.sb("wrows", [P, 3, D])
        scal = st.sb("scal", [P, 8])
        nscal = st.sb("nscal", [P, 8])
        ema = st.sb("ema", [P, 4])
        pt = st.ps("pt", [P, 512])
        pe_ = st.ps("pe", [P, 512])
        s_load = st.sem("load")
        s_zero = st.sem("zero")
        k.s_zeroed = st.sem("zeroed")
        k.s_w0 = st.sem("w0")
        k.s_x = [st.sem(f"x{g}") for g in range(len(GROUPS))]
        s_iota = st.sem("iota")
        s_pool = st.sem("pool")
        s_tr = st.sem("tr")
        s_sum = st.sem("sum")
        s_act = st.sem("act")
        s_vec = st.sem("vec")
        block = st.block()
        LOADS = 16 * 10

        @block.sync
        def _(sp):
            sp.dma_start(k.GW0[:, :], dram.gate_w).then_inc(s_load, 16)
            sp.dma_start(k.RW1[:, :], dram.router_w).then_inc(s_load, 16)
            sp.dma_start(k.GB0[0:1, 0, :], dram.gate_b.rearrange("(a e) -> a e", a=1)).then_inc(s_load, 16)
            sp.dma_start(bcol[:, :], dram.b1.rearrange("e (c p) -> (e c) p", p=P)).then_inc(s_load, 16)
            sp.dma_start(wrows[:, :, :], dram.W.rearrange("(c p) d -> p c d", p=P)).then_inc(s_load, 16)
            with nc.allow_non_contiguous_dma("a few columns of one word"):
                sp.dma_start(ema[:, 0:1], dram.ema.rearrange("(p a) -> p a", a=1)).then_inc(s_load, 16)
                cols = k.COLS[:, :]
                sp.dma_start(cols[:, 0:1], dram.u.rearrange("(p a) -> p a", a=1)).then_inc(s_load, 16)
                sp.dma_start(cols[:, 1:2], dram.gamma.rearrange("(p a) -> p a", a=1)).then_inc(s_load, 16)
                sp.dma_start(cols[:, 2:3], dram.beta.rearrange("(p a) -> p a", a=1)).then_inc(s_load, 16)
                sp.dma_start(cols[:, 3:6], dram.b.rearrange("(c p) -> p c", p=P)).then_inc(s_load, 16)
            for g, group in enumerate(GROUPS):
                sp.dma_start(k.X[:, group, :], dram.x.rearrange("b (j p) d -> p (b j) d", p=P)[:, group, :])\
                  .then_inc(k.s_x[g], 16)
            for h in range(2):
                half = slice(h * E // 2, (h + 1) * E // 2)
                sp.dma_start(k.W1[:, half, :], dram.w1[half, :, :].rearrange("e d f -> d e f")).then_inc(k.s_w0, 16)
                sp.dma_start(k.W2[:, half.start * FC0:half.stop * FC0, :],
                             dram.w2[half, :, :].rearrange("e (c p) d -> p (e c) d", p=P)).then_inc(k.s_w0, 16)
            sp.dma_start(k.B2[:, :, :].rearrange("p e d -> p (e d)"),
                         dram.b2.rearrange("(a e) d -> a (e d)", a=1).to_broadcast([P, E * D])).then_inc(k.s_w0, 16)
            sp.wait_ge(s_zero, 1)
            write_zeros(sp, k, dram.delta0[0])

        @block.scalar
        def _(act):
            for n, name in enumerate((dram.log_tau, dram.log_blend, dram.logit_blend_seq)):
                act.dma_start(scal[:, n:n + 1], name.rearrange("(a e) -> a e", a=1).to_broadcast([P, 1]))\
                   .then_inc(s_act, 16)
            act.wait_ge(s_act, 48)
            nc.scalar.activation(nscal[:, 0:1], scal[:, 0:1], ACT.Exp).then_inc(s_act, 1)
            nc.scalar.activation(nscal[:, 1:3], scal[:, 1:3], ACT.Exp, scale=-1.0).then_inc(s_act, 1)
            act.wait_ge(s_tr, 1)
            nc.scalar.copy(k.B1T[:, :], pt[:, 0:E * FC0]).then_inc(s_act, 1)
            nc.scalar.copy(k.WT[:, :], pt[:, P:P + 3 * P]).then_inc(s_act, 1)
            act.wait_ge(s_sum, 1)
            nc.scalar.activation(ema[:, 2:3], pe_[:, 0:1], ACT.Sqrt).then_inc(s_act, 1)

        @block.gpsimd
        def _(pool):
            nc.gpsimd.memset(k.IDENT[:, :], 1.0).then_inc(s_iota, 1)
            nc.gpsimd.memset(k.TRIU[:, :], 1.0).then_inc(s_iota, 1)
            nc.gpsimd.memset(k.ONESB[:, :], 1.0).then_inc(s_iota, 1)
            nc.gpsimd.memset(k.ONES[:, :], 1.0).then_inc(s_iota, 1)
            nc.gpsimd.memset(k.PAST[:, :], 0.0).then_inc(s_iota, 1)
            nc.gpsimd.memset(k.FIRST[:, :], -4.0).then_inc(s_iota, 1)
            nc.gpsimd.memset(k.RESET[:, :], 1.0).then_inc(s_iota, 1)
            nc.gpsimd.iota(iota[:, :], pattern=[[1, CAP1]], base=0, channel_multiplier=0).then_inc(s_iota, 1)
            nc.gpsimd.iota(ids[:, 0, :], pattern=[[1, NT]], base=0, channel_multiplier=0).then_inc(s_iota, 1)
            nc.gpsimd.iota(ids[:, 1, :], pattern=[[0, NT]], base=0, channel_multiplier=1).then_inc(s_iota, 1)
            nc.gpsimd.iota(ids[:, 2, :], pattern=[[0, NT]], base=1, channel_multiplier=0).then_inc(s_iota, 1)
            for e in range(E):
                nc.gpsimd.memset(k.RANK[:, e:e + 1], float(E - e)).then_inc(s_iota, 1)
            pool.wait_ge(s_iota, 11 + E)
            nc.gpsimd.affine_select(out=k.IDENT[:, :], in_=k.IDENT[:, :], compare_op=ALU.is_equal, fill=0.0,
                                    base=0, pattern=[[-1, P]], channel_multiplier=1).then_inc(s_pool, 1)
            nc.gpsimd.affine_select(out=k.TRIU[:, :], in_=k.TRIU[:, :], compare_op=ALU.is_ge, fill=0.0,
                                    base=0, pattern=[[1, P]], channel_multiplier=-1).then_inc(s_pool, 1)
            nc.gpsimd.affine_select(out=k.PAST[:, :], in_=k.PAST[:, :], compare_op=ALU.is_gt,
                                    fill=-4.0, base=0, pattern=[[-1, P]], channel_multiplier=1).then_inc(s_pool, 1)
            nc.gpsimd.memset(k.FIRST[0:1, 0:NT:TPB], 0.0).then_inc(s_pool, 1)
            nc.gpsimd.memset(k.RESET[:, 0:E * NT:NT], 0.0).then_inc(s_pool, 1)

        @block.vector
        def _(dve):
            link = Chain(dve, s_vec)
            nc.vector.memset(k.ZEROS[:, :], 0.0).then_inc(s_zero, 1)
            dve.wait_ge(s_pool, 5)
            nc.vector.tensor_copy(k.IDENTB[:, :], k.IDENT[:, :]).then_inc(s_zero, 1)
            link(nc.vector.tensor_copy(k.IOTA[:, :], iota[:, :]))
            link(nc.vector.tensor_copy(k.IDS[:, :, :], ids[:, :, :].rearrange("p a t -> p t a")))
            dve.wait_ge(s_load, LOADS)
            nc.vector.tensor_copy(k.GB0[0:1, 1:NT, :], k.GB0[0:1, 0:1, :].to_broadcast([1, NT - 1, E])).then_inc(s_zero, 1)
            link(nc.vector.tensor_tensor(ema[:, 1:2], ema[:, 0:1], ema[:, 0:1], ALU.mult))
            dve.wait_ge(s_act, 50)
            link(nc.vector.tensor_scalar(k.SCAL[:, 0:1], nscal[:, 0:1], -1.0, None, ALU.mult))
            link(nc.vector.tensor_scalar(nscal[:, 1:3], nscal[:, 1:3], 1.0, None, ALU.add))
            link(nc.vector.reciprocal(k.SCAL[:, 1:3], nscal[:, 1:3]))
            link(nc.vector.tensor_scalar(k.SCAL[:, 3:5], k.SCAL[:, 1:3], -1.0, 1.0, ALU.mult, ALU.add))
            dve.wait_ge(s_act, 53)
            link(nc.vector.tensor_scalar(ema[:, 2:3], ema[:, 2:3], 1e-12, None, ALU.max))
            link(nc.vector.reciprocal(ema[:, 3:4], ema[:, 2:3]))
            link(nc.vector.tensor_tensor(k.EMA[:, 0:1], ema[:, 0:1], ema[:, 3:4], ALU.mult))

        @block.tensor
        def _(pe):
            pe.wait_ge(s_load, LOADS)
            pe.wait_ge(s_pool, 5)
            n = E * FC0
            nc.tensor.transpose(pt[:, 0:n], bcol[:, :], k.IDENT[0:n, 0:n])
            for c in range(3):
                last = nc.tensor.transpose(pt[:, P + c * P:P + (c + 1) * P], wrows[:, c, :], k.IDENT[:, :])
            last.then_inc(s_tr, 1)
            pe.wait_ge(s_vec, 3)
            nc.tensor.matmul(pe_[:, 0:1], k.ONES[:, :], ema[:, 1:2], start=True, stop=True).then_inc(s_sum, 1)


def tiles_of(group):
    return list(range(NT))[group]


class Fold:

    def __init__(self, nc, st, k, delta, gate):
        self.nc, self.k, self.delta, self.gate = nc, k, delta, gate
        self.y = st.sb("y", [P, NT, D])
        self.s_y = [st.sem(f"y{g}") for g in range(len(GROUPS))]
        self.s_f = st.sem("f")

    def load(self, sp):
        for g, group in enumerate(GROUPS):
            sp.dma_start(self.y[:, group, :], self.delta.rearrange("(t p) d -> p t d", p=P)[:, group, :])\
              .then_inc(self.s_y[g], 16)

    def add(self, dve, g, q):
        nc, k = self.nc, self.k
        if q == 0:
            dve.wait_ge(self.s_y[g], 16)
        quad = slice(GROUPS[g].start + 4 * q, GROUPS[g].start + 4 * q + 4)
        if self.gate is None:
            nc.vector.tensor_tensor(k.X[:, quad, :], k.X[:, quad, :], self.y[:, quad, :], ALU.add)\
              .then_inc(self.s_f, 4)
        else:
            for t in tiles_of(quad):
                nc.vector.scalar_tensor_tensor(out=k.X[:, t, :], in0=self.y[:, t, :], scalar=self.gate[:, t:t + 1],
                                               in1=k.X[:, t, :], op0=ALU.mult, op1=ALU.add).then_inc(self.s_f, 1)


def mean_and_variance(nc, k, link, group, s_var):
    tt, ts = nc.gpsimd.tensor_tensor, nc.gpsimd.tensor_scalar
    mean_e, var_e, mean_o, var_o = (k.BN[:, group, i] for i in (1, 2, 4, 5))
    dif, var, both = k.DIF[:, group], k.VAR[:, group], k.BOTH[:, group]
    link.beside(tt(dif, mean_e, mean_o, ALU.subtract))
    link.beside(tt(var, var_e, var_o, ALU.add))
    link(tt(both, mean_e, mean_o, ALU.add))
    link.beside(tt(dif, dif, dif, ALU.mult))
    link.beside(ts(k.MEAN[:, group], both, 0.5, None, ALU.mult))
    link(ts(var, var, 1.0 / D, LN_EPS, ALU.mult, ALU.add))
    link(ts(dif, dif, 0.25, None, ALU.mult))
    tt(var, var, dif, ALU.add).then_inc(s_var, 1)
    link(ts(both, both, -0.5, None, ALU.mult))


def inverse_root(eng, link, out, v, t, u, fused):
    link.beside(eng.tensor_scalar(u, v, -0.5, None, ALU.mult))
    link(eng.tensor_scalar(out.bitcast(I32), v.bitcast(I32), -0.5, float(0x5F3759DF), ALU.mult, ALU.add))
    for _ in range(3):
        link(eng.tensor_tensor(t, out, out, ALU.mult))
        link(eng.tensor_tensor(t, t, u, ALU.mult))
        if fused:
            link(eng.scalar_tensor_tensor(out=out, in0=t, scalar=1.5, in1=out, op0=ALU.add, op1=ALU.mult))
        else:
            link(eng.tensor_scalar(t, t, 1.5, None, ALU.add))
            link(eng.tensor_tensor(out, out, t, ALU.mult))


class Norm:

    def __init__(self, nc, st, k, xn, fold=None, newton=len(GROUPS), arrive=None):
        self.arrive = arrive
        self.nc, self.k, self.xn, self.fold, self.newton = nc, k, xn, fold, newton
        self.s_bn = st.sem("bn")
        self.s_mv = st.sem("mv")
        self.s_var = st.sem("var")
        self.s_std = st.sem("std")
        self.s_rs = st.sem("rs")
        self.s_nb = st.sem("nb")
        self.s_xv = st.sem("xv")
        self.s_xa = st.sem("xa")

    def moments(self, dve, g, quads=range(QUADS)):
        nc, k = self.nc, self.k
        if self.arrive is not None:
            dve.wait_ge(self.arrive[g], 16)
        for q in quads:
            if self.fold is not None:
                self.fold.add(dve, g, q)
        for n in range(4 * quads[0], 4 * (quads[-1] + 1)):
            t = GROUPS[g].start + n
            if self.fold is not None and (self.fold.gate is not None or n % 4 == 0):
                dve.wait_ge(self.fold.s_f, 8 * g + n + (1 if self.fold.gate is not None else 4))
            nc.vector.bn_stats(k.BN[:, t, :], k.X[:, t, :]).then_inc(self.s_bn, 1)

    def even_tiles(self, dve, g):
        nc, k, group = self.nc, self.k, GROUPS[g]
        if g < self.newton:
            dve.wait_ge(self.s_std, g + 1)
            nc.vector.reciprocal(k.RSTD[:, group], k.STD[:, group]).then_inc(self.s_rs, 1)
            dve.wait_ge(self.s_rs, g + 1)
        else:
            dve.wait_ge(self.s_nb, g + 1)
        for t in tiles_of(group)[0::2]:
            nc.vector.tensor_scalar(self.xn[:, t, :], k.X[:, t, :], k.MEAN[:, t:t + 1], k.RSTD[:, t:t + 1],
                                    ALU.subtract, ALU.mult).then_inc(self.s_xv, 1)

    def vector(self, dve):
        for g in range(len(GROUPS) + 1):
            if g < len(GROUPS):
                self.moments(dve, g)
            if g >= 1:
                self.even_tiles(dve, g - 1)

    def gpsimd(self, pool, link, g, n=1):
        nc, k, group = self.nc, self.k, slice(GROUPS[g].start, GROUPS[g + n - 1].stop)
        pool.wait_ge(self.s_bn, 8 * (g + n))
        mean_and_variance(nc, k, link, group, self.s_var)
        if g < self.newton:
            pool.wait_ge(self.s_rs, g + 1)
        else:
            pool.wait_ge(self.s_var, g + 1)
            inverse_root(nc.gpsimd, link, k.RSTD[:, group], k.VAR[:, group], k.STD[:, group], k.DIF[:, group], False)
        nc.gpsimd.tensor_tensor(k.NBIAS[:, group], k.BOTH[:, group], k.RSTD[:, group], ALU.mult).then_inc(self.s_nb, n)

    def root(self, act, g):
        group = GROUPS[g]
        act.wait_ge(self.s_var, g + 1)
        self.nc.scalar.activation(self.k.STD[:, group], self.k.VAR[:, group], ACT.Sqrt).then_inc(self.s_std, 1)

    def odd_tiles(self, act, g):
        k = self.k
        act.wait_ge(self.s_nb, g + 1)
        for t in tiles_of(GROUPS[g])[1::2]:
            self.nc.scalar.activation(self.xn[:, t, :], k.X[:, t, :], ACT.Identity, scale=k.RSTD[:, t:t + 1],
                                      bias=k.NBIAS[:, t:t + 1]).then_inc(self.s_xa, 1)

    def wait_quad(self, eng, q):
        eng.wait_ge(self.s_xv, 2 * (q + 1))
        eng.wait_ge(self.s_xa, 2 * (q + 1))


def normalize(nc, name, k, dram, routing, delta=None, gate=None, weights=None, rows=None, bias=None,
              base=None, arrive=None):
    with ExitStack() as ctx:
        st = Stage(nc, ctx, name)
        xn = k.xn
        xts = [st.sb(f"xts{u}", [P, T]) for u in range(2)]
        psT = [st.ps(f"psT{u}", [P, T]) for u in range(3)]
        s_tr = st.sem("tr")
        s_xt = st.sem("xt")
        s_lg = st.sem("lg")
        k.s_lg = s_lg
        route = routing(nc, st, k, dram)
        fold = Fold(nc, st, k, delta, gate) if delta is not None else None
        norm = Norm(nc, st, k, xn, fold, arrive=arrive)
        ALL_QUADS = QUADS * len(GROUPS)
        quads = [tiles_of(g)[4 * q:4 * q + 4] for g in GROUPS for q in range(QUADS)]
        block = st.block()

        @block.vector
        def _(dve):
            norm.vector(dve)
            route.vector(dve)

        @block.gpsimd
        def _(pool):
            if routing is route1:
                route.clear()
            link = Chain(pool, norm.s_mv)
            for g in range(len(GROUPS)):
                norm.gpsimd(pool, link, g)
            route.gpsimd(pool)

        @block.scalar
        def _(act):
            def copy(q):
                if q >= 2:
                    act.wait_ge(s_lg, q - 1)
                act.wait_ge(s_tr, q + 1)
                nc.scalar.copy(xts[q % 2][:, :], psT[q % 3][:, :]).then_inc(s_xt, 1)

            norm.root(act, 0)
            for g in range(len(GROUPS)):
                norm.odd_tiles(act, g)
                if g + 1 < len(GROUPS):
                    norm.root(act, g + 1)
                else:
                    route.exponent(act, 0)
                for q in range(QUADS * g, QUADS * (g + 1)):
                    copy(q)
            route.exponent(act, 1)
            if routing is route1:
                route.scalar(act)

        @block.sync
        def _(sp):
            if fold is not None:
                fold.load(sp)
            if rows is not None:
                for q in range(ALL_QUADS):
                    norm.wait_quad(sp, q)
                    sp.dma_start(rows[q * T:(q + 1) * T, :].rearrange("(j p) d -> p j d", p=P),
                                 xn[:, q * TPB:(q + 1) * TPB, :]).then_inc(k.s_rows, 16)
            if base is not None:
                for group in GROUPS:
                    sp.dma_start(base.rearrange("b (j p) d -> p (b j) d", p=P)[:, group, :], k.X[:, group, :])\
                      .then_inc(k.s_base, 16)
            if routing is route1:
                route.sync(sp)

        @block.tensor
        def _(pe):
            if bias is not None:
                for h in range(2):
                    nc.tensor.matmul(k.psL[h][:, 0:NT // 2 * E], k.ONES[0:1, :], bias[:, 0:NT // 2 * E], start=True,
                                     stop=False, skip_group_check=True)

            def logits(q):
                pe.wait_ge(s_xt, q + 1)
                for j, t in enumerate(quads[q]):
                    at = t % (NT // 2) * E
                    last = nc.tensor.matmul(k.psL[t // (NT // 2)][:, at:at + E], xts[q % 2][:, j * P:(j + 1) * P],
                                            weights, start=bias is None, stop=True, skip_group_check=True)
                last.then_inc(s_lg, 1)

            for q in range(ALL_QUADS):
                norm.wait_quad(pe, q)
                if q >= 3:
                    pe.wait_ge(s_xt, q - 2)
                for j, t in enumerate(quads[q]):
                    last = nc.tensor.transpose(psT[q % 3][:, j * P:(j + 1) * P], xn[:, t, :], k.IDENT[:, :])
                last.then_inc(s_tr, 1)
                if q >= 1:
                    logits(q - 1)
            logits(ALL_QUADS - 1)
            route.tensor(pe)


HALVES = [slice(h * NT // 2, (h + 1) * NT // 2) for h in range(2)]


def over_experts(v, c):
    return v[:, c].unsqueeze(2).to_broadcast([P, NT // 2, E])


def softmax_over_experts(nc, dve, link, k, w, h, s_exp):
    c = HALVES[h]
    L = k.psL[h][:, 0:NT // 2 * E].rearrange("p (t e) -> p t e", e=E)
    link(nc.vector.tensor_reduce(w.m[:, c], L, AX, ALU.max))
    link(nc.vector.tensor_tensor(w.p[:, c, :], L, over_experts(w.m, c), ALU.subtract))
    dve.wait_ge(s_exp, h + 1)
    link(nc.vector.tensor_reduce(w.m[:, c], w.q[:, c, :], AX, ALU.add))
    link(nc.vector.reciprocal(w.r[:, c], w.m[:, c]))
    link(nc.vector.tensor_tensor(w.p[:, c, :], w.q[:, c, :], over_experts(w.r, c), ALU.mult))


def first_largest(nc, link, k, w, h, p, value, rank, mask):
    c = HALVES[h]
    ranks = k.RANK[:, :].unsqueeze(1).to_broadcast([P, NT // 2, E])
    link(nc.vector.tensor_reduce(value[:, c], p[:, c, :], AX, ALU.max))
    link(nc.vector.tensor_tensor(w.q[:, c, :], p[:, c, :], over_experts(value, c), ALU.is_equal))
    link(nc.vector.tensor_tensor(w.q[:, c, :], w.q[:, c, :], ranks, ALU.mult))
    link(nc.vector.tensor_reduce(rank[:, c], w.q[:, c, :], AX, ALU.max))
    link(nc.vector.tensor_tensor(mask[:, c, :], w.q[:, c, :], over_experts(rank, c), ALU.is_equal))


class Work:

    def __init__(self, st):
        self.p, self.q, self.s = (st.sb(n, [P, NT, E]) for n in "pqs")
        self.m, self.r, self.a, self.b, self.c, self.g = (st.sb("v" + n, [P, NT]) for n in "mrabcg")


def route0(nc, st, k, dram):
    w = Work(st)
    mask = st.sb("mask", [P, NT, E], BF16)
    te = st.sb("te", [P, E * NT])
    sc = st.sb("sc", [P, E * NT])
    hot = st.sb("hot", [P, NT, CAP0], BF16)
    rec = st.sb("rec", [P, NT, 3, E], BF16)
    tok = st.sb("tok", [P, 3, E])
    row = st.sb("row", [P, 2, E])
    psC = st.ps("psC", [P, 2, NT * E])
    psS = st.ps("psS", [P, 512])
    s_vec = st.sem("vec")
    s_exp = st.sem("exp")
    s_cnt = st.sem("cnt")
    s_rec = st.sem("rec")
    s_hot = st.sem("hot")
    s_use = st.sem("use")

    def exponent(act, h):
        act.wait_ge(s_vec, 10 * h + 2)
        nc.scalar.activation(w.q[:, HALVES[h], :], w.p[:, HALVES[h], :], ACT.Exp).then_inc(s_exp, 1)

    def gpsimd(pool):
        pool.wait_ge(s_vec, 20)
        nc.gpsimd.tensor_tensor(rec[:, :, :, :], mask[:, :, :].unsqueeze(2).to_broadcast([P, NT, 3, E]),
                                k.IDS[:, :, :].unsqueeze(3).to_broadcast([P, NT, 3, E]), ALU.mult)\
          .then_inc(s_rec, 1)

    def vector(dve):
        link = Chain(dve, s_vec)
        for h in range(2):
            dve.wait_ge(k.s_lg, B // 2 * (h + 1))
            softmax_over_experts(nc, dve, link, k, w, h, s_exp)
            first_largest(nc, link, k, w, h, w.p, w.g, w.a, mask)
        assert link.n == 20
        dve.wait_ge(s_cnt, 1)
        link(nc.vector.tensor_copy(te[:, :].rearrange("p (e t) -> p e t", e=E),
                                   psC[:, 1, :].rearrange("p (t e) -> p e t", e=E)))
        link(nc.vector.tensor_tensor_scan(sc[:, :], k.RESET[:, :], te[:, :], 0.0, ALU.mult, ALU.add))
        link(nc.vector.tensor_tensor(sc[:, :], sc[:, :], te[:, :], ALU.subtract))
        link(nc.vector.tensor_tensor(w.q[:, :, :], psC[:, 0, :].rearrange("p (t e) -> p t e", e=E),
                                     sc[:, :].rearrange("p (e t) -> p t e", e=E), ALU.add))
        link(nc.vector.tensor_tensor(w.q[:, :, :], w.q[:, :, :], mask[:, :, :], ALU.mult))
        link(nc.vector.tensor_reduce(w.b[:, :], w.q[:, :, :], AX, ALU.add))
        link(nc.vector.tensor_scalar(w.a[:, :], w.b[:, :], -1.0, None, ALU.add))
        for t in range(NT):
            nc.vector.tensor_scalar(hot[:, t, :], k.IOTA[:, 0:CAP0], w.a[:, t:t + 1], None, ALU.is_equal)\
              .then_inc(s_hot, 1)
        link(nc.vector.tensor_scalar(w.c[:, :], w.b[:, :], CAP0 + 0.5, 0.5, ALU.is_le, ALU.mult))
        link(nc.vector.tensor_tensor(k.GATE0[:, :], w.c[:, :], w.g[:, :], ALU.mult))
        dve.wait_ge(s_use, 1)
        link(nc.vector.tensor_copy(flat(tok[0:CAP0, :, :]), psS[0:CAP0, 0:3 * E]))
        link(nc.vector.scalar_tensor_tensor(out=row[0:CAP0, 0, :], in0=tok[0:CAP0, 0, :], scalar=float(P),
                                            in1=tok[0:CAP0, 1, :], op0=ALU.mult, op1=ALU.add))
        link(nc.vector.tensor_scalar(row[0:CAP0, 1, :], tok[0:CAP0, 2, :], -float(SKIP), float(SKIP),
                                     ALU.mult, ALU.add))
        link(nc.vector.tensor_tensor(row[0:CAP0, 1, :], row[0:CAP0, 1, :], row[0:CAP0, 0, :], ALU.add))
        link(nc.vector.tensor_copy(k.SLOT_ROW[0:CAP0, :, :], row[0:CAP0, :, :]))

    def tensor(pe):
        pe.wait_ge(s_vec, 20)
        nc.tensor.matmul(psC[:, 0, :], k.TRIU[:, :], flat(mask[:, :, :]), start=True, stop=True,
                         skip_group_check=True)
        nc.tensor.matmul(psC[:, 1, :], k.ONESB[:, :], flat(mask[:, :, :]), start=True, stop=True,
                         skip_group_check=True).then_inc(s_cnt, 1)
        pe.wait_ge(s_rec, 1)
        for t in range(NT):
            pe.wait_ge(s_hot, t + 1)
            last = nc.tensor.matmul(psS[0:CAP0, 0:3 * E], hot[:, t, :], rec[:, t, :, :].rearrange("p a e -> p (a e)"),
                                    start=(t == 0), stop=(t == NT - 1))
        last.then_inc(s_use, 1)

    r = Names()
    r.exponent, r.vector, r.gpsimd, r.tensor = exponent, vector, gpsimd, tensor
    return r


def experts0(nc, name, k, dram, delta, zeroed):
    with ExitStack() as ctx:
        st = Stage(nc, ctx, name)
        xe = st.sb("xe", [P, E, D])
        xet = st.sb("xet", [P, E, CAP0])
        hid = [st.sb(f"hid{u}", [P, FC0, CAP0]) for u in range(2)]
        eo = st.sb("eo", [P, E, D])
        psX, psA, psB = ([st.ps(f"ps{n}{u}", [P, 512]) for u in range(2)] for n in "XAB")
        s_gat = [st.sem(f"gat{e}") for e in range(E)]
        s_tr = st.sem("tr")
        s_xt = st.sem("xt")
        s_up = st.sem("up")
        s_hid = st.sem("hid")
        s_dn = st.sem("dn")
        s_eo = st.sem("eo")
        s_sca = st.sem("sca")
        block = st.block()

        @block.gpsimd
        def _(pool):
            pool.wait_ge(k.s_rows, 16 * B)
            for e in range(E):
                nc.gpsimd.indirect_dma_start(out=xe[0:CAP0, e, :], out_offset=None, in_=dram.normed[:, :],
                                             in_offset=bass.IndirectOffsetOnAxis(ap=k.SLOT_ROW[0:CAP0, 0, e:e + 1],
                                                                                 axis=0)).then_inc(s_gat[e], 16)
            pool.wait_ge(k.s_zeroed, zeroed)
            for e in range(E):
                pool.wait_ge(s_eo, e + 1)
                nc.gpsimd.indirect_dma_start(out=delta[:, :],
                                             out_offset=bass.IndirectOffsetOnAxis(ap=k.SLOT_ROW[0:CAP0, 1, e:e + 1],
                                                                                  axis=0),
                                             in_=eo[0:CAP0, e, :], in_offset=None, bounds_check=NT * P - 1,
                                             oob_is_err=False).then_inc(s_sca, 16)
            pool.wait_ge(s_sca, 16 * E)

        @block.tensor
        def _(pe):
            pe.wait_ge(k.s_w0, 16 * 5)

            def turn(e):
                pe.wait_ge(s_gat[e], 16)
                if e >= 2:
                    pe.wait_ge(s_xt, e - 1)
                nc.tensor.transpose(psX[e % 2][:, 0:CAP0], xe[0:CAP0, e, :], k.IDENT[0:CAP0, 0:CAP0])\
                  .then_inc(s_tr, 1)

            def up(e):
                pe.wait_ge(s_xt, e + 1)
                if e >= 2:
                    pe.wait_ge(s_hid, FC0 * (e - 1))
                for c in range(FC0):
                    last = nc.tensor.matmul(psA[e % 2][:, c * CAP0:(c + 1) * CAP0], k.W1[:, e, c * P:(c + 1) * P],
                                            xet[:, e, :], start=True, stop=True)
                last.then_inc(s_up, 1)

            def down(e):
                pe.wait_ge(s_hid, FC0 * (e + 1))
                if e >= 2:
                    pe.wait_ge(s_eo, e - 1)
                for c in range(FC0):
                    last = nc.tensor.matmul(psB[e % 2][0:CAP0, 0:D], hid[e % 2][:, c, :], k.W2[:, e * FC0 + c, :],
                                            start=(c == 0), stop=(c == FC0 - 1))
                last.then_inc(s_dn, 1)

            turn(0)
            for e in range(E + 1):
                if e + 1 < E:
                    turn(e + 1)
                if e < E:
                    up(e)
                if e >= 1:
                    down(e - 1)

        @block.scalar
        def _(act):
            for e in range(E):
                act.wait_ge(s_up, e + 1)
                if e >= 2:
                    act.wait_ge(s_dn, e - 1)
                for c in range(FC0):
                    nc.scalar.activation(hid[e % 2][:, c, :], psA[e % 2][:, c * CAP0:(c + 1) * CAP0],
                                         ACT.Gelu_apprx_tanh, bias=k.B1T[:, e * FC0 + c:e * FC0 + c + 1])\
                      .then_inc(s_hid, 1)

        @block.vector
        def _(dve):
            def turned(e):
                dve.wait_ge(s_tr, e + 1)
                nc.vector.tensor_copy(xet[:, e, :], psX[e % 2][:, 0:CAP0]).then_inc(s_xt, 1)

            turned(0)
            dve.wait_ge(k.s_w0, 16 * 5)
            for e in range(E + 1):
                if e + 1 < E:
                    turned(e + 1)
                if e >= 1:
                    dve.wait_ge(s_dn, e)
                    nc.vector.tensor_tensor(eo[0:CAP0, e - 1, :], psB[(e - 1) % 2][0:CAP0, 0:D],
                                            k.B2[0:CAP0, e - 1, :], ALU.add).then_inc(s_eo, 1)


def attention0(nc, name, k, delta, gate, zero):
    with ExitStack() as ctx:
        st = Stage(nc, ctx, name)
        xn = st.sb("xn", [P, NT, D])
        go = st.sb("go", [P, NT, D])
        on = st.sb("on", [P, NT, D])
        sq = st.sb("sq", [P, 2, D])
        ont = [st.sb(f"ont{u}", [P, 1 + T]) for u in range(2)]
        ss, inv, tmp, minus = (st.sb(v, [P, NT]) for v in ("ss", "inv", "tmp", "minus"))
        rn = st.sb("rn", [P, NT])
        seq = st.sb("seq", [P, NT])
        fam = st.sb("fam", [P, NT])
        em = st.sb("em", [P, NT])
        ems = st.sb("ems", [P, NT])
        att = st.sb("att", [P, NT])
        psT = [st.ps(f"psT{u}", [P, T]) for u in range(2)]
        psM = [st.ps(f"psM{j}", [P, T]) for j in range(TPB)]
        s_go = st.sem("go")
        s_ss = st.sem("ss")
        s_len = st.sem("len")
        s_rn = st.sem("rn")
        s_onv = st.sem("onv")
        s_ona = st.sem("ona")
        s_tr = st.sem("tr")
        s_ot = st.sem("ot")
        s_sim = st.sem("sim")
        s_ema = st.sem("ema")
        s_seq = st.sem("seq")
        s_max = st.sem("max")
        s_vec = st.sem("vec")
        s_nov = st.sem("nov")
        s_x = st.sem("x")
        STEPS = 5
        halves = [slice(h * NT // 2, (h + 1) * NT // 2) for h in range(2)]
        fold = Fold(nc, st, k, delta, gate)
        norm = Norm(nc, st, k, xn, fold, newton=2)
        block = st.block()

        @block.sync
        def _(sp):
            fold.load(sp)
            for other in zero:
                write_zeros(sp, k, other)

        @block.gpsimd
        def _(pool):
            link = Chain(pool, norm.s_mv)
            norm.gpsimd(pool, link, 0)
            norm.gpsimd(pool, link, 1)
            norm.gpsimd(pool, link, 2, 2)

        @block.vector
        def _(dve):
            chain = Chain(dve, s_len)

            def unit(g):
                group = GROUPS[g]
                dve.wait_ge(s_ss, 8 * (g + 1))
                chain(nc.vector.tensor_scalar(ss[:, group], ss[:, group], 1e-24, None, ALU.max))
                inverse_root(nc.vector, chain, inv[:, group], ss[:, group], tmp[:, group], minus[:, group], True)
                nc.vector.tensor_copy(rn[:, group], inv[:, group]).then_inc(s_rn, 1)
                dve.wait_ge(s_rn, g + 1)
                for t in tiles_of(GROUPS[g])[0::2]:
                    nc.vector.tensor_scalar(on[:, t, :], go[:, t, :], rn[:, t:t + 1], None, ALU.mult)\
                      .then_inc(s_onv, 1)

            def largest(b):
                for t in range(b * TPB, (b + 1) * TPB):
                    dve.wait_ge(s_sim, t + 1)
                    nc.vector.tensor_reduce(seq[:, t:t + 1], psM[t % TPB][:, 1:(t % TPB + 1) * P], AX, ALU.max)\
                      .then_inc(s_seq, 1)
                    nc.vector.tensor_copy(em[:, t:t + 1], psM[t % TPB][:, 0:1]).then_inc(s_max, 1)

            link = Chain(dve, s_vec)

            def familiar(h):
                c = halves[h]
                dve.wait_ge(s_seq, NT // 2 * (h + 1))
                dve.wait_ge(s_max, NT // 2 * (h + 1))
                link(nc.vector.tensor_tensor(fam[:, c], em[:, c], k.FIRST[:, c], ALU.add))
                link(nc.vector.tensor_tensor(seq[:, c], seq[:, c], fam[:, c], ALU.max))
                link(nc.vector.tensor_scalar(ems[:, c], em[:, c], k.SCAL[:, 4:5], None, ALU.mult))
                link(nc.vector.scalar_tensor_tensor(out=fam[:, c], in0=seq[:, c], scalar=k.SCAL[:, 2:3],
                                                    in1=ems[:, c], op0=ALU.mult, op1=ALU.add))

            def attended(h):
                c = halves[h]
                dve.wait_ge(s_nov, h + 1)
                link(nc.vector.tensor_scalar(att[:, c], att[:, c], k.SCAL[:, 1:2], k.SCAL[:, 3:4], ALU.mult, ALU.add))

            def add(t):
                nc.vector.scalar_tensor_tensor(out=k.X[:, t, :], in0=go[:, t, :], scalar=att[:, t:t + 1],
                                               in1=k.X[:, t, :], op0=ALU.mult, op1=ALU.add).then_inc(s_x, 1)

            for u in range(2):
                nc.vector.tensor_copy(ont[u][:, 0:1], k.EMA[:, 0:1]).then_inc(s_ema, 1)
            norm.moments(dve, 0)
            norm.moments(dve, 1)
            norm.even_tiles(dve, 0)
            norm.even_tiles(dve, 1)
            norm.moments(dve, 2)
            norm.moments(dve, 3)
            unit(0)
            unit(1)
            norm.even_tiles(dve, 2)
            norm.even_tiles(dve, 3)
            largest(0)
            largest(1)
            unit(2)
            largest(2)
            for b in range(3, B):
                largest(b)
                if b == 3:
                    unit(3)
                if b == B // 2 - 1:
                    familiar(0)
                if b == B // 2:
                    attended(0)
                if b >= B // 2 and b < B - 1:
                    for t in range((b - B // 2) * 6, min((b - B // 2 + 1) * 6, NT // 2)):
                        add(t)
            familiar(1)
            attended(1)
            for t in range(NT // 2, NT):
                add(t)

        @block.scalar
        def _(act):
            def gelu(b):
                norm.wait_quad(act, b)
                nc.scalar.activation(go[:, b * TPB:(b + 1) * TPB, :], xn[:, b * TPB:(b + 1) * TPB, :],
                                     ACT.Gelu_apprx_tanh).then_inc(s_go, 1)

            def length(b):
                act.wait_ge(s_go, b + 1)
                for t in range(b * TPB, (b + 1) * TPB):
                    if t >= 2:
                        act.wait_ge(s_ss, t - 1)
                    nc.scalar.activation(sq[:, t % 2, :], go[:, t, :], ACT.Square, accum_out=ss[:, t:t + 1])\
                      .then_inc(s_ss, 1)

            def unit(g):
                act.wait_ge(s_rn, g + 1)
                for t in tiles_of(GROUPS[g])[1::2]:
                    nc.scalar.activation(on[:, t, :], go[:, t, :], ACT.Identity, scale=rn[:, t:t + 1])\
                      .then_inc(s_ona, 1)

            def turned(b):
                if b >= 2:
                    act.wait_ge(s_sim, (b - 1) * TPB)
                act.wait_ge(s_tr, b + 1)
                nc.scalar.copy(ont[b % 2][:, 1:1 + T], psT[b % 2][:, :]).then_inc(s_ot, 1)

            def novelty(h):
                act.wait_ge(s_vec, STEPS * (h + 1) - 1)
                nc.scalar.activation(att[:, halves[h]], fam[:, halves[h]], ACT.Exp, scale=k.SCAL[:, 0:1])\
                  .then_inc(s_nov, 1)

            norm.root(act, 0)
            norm.root(act, 1)
            norm.odd_tiles(act, 0)
            gelu(0)
            gelu(1)
            norm.odd_tiles(act, 1)
            length(0)
            length(1)
            gelu(2)
            gelu(3)
            length(2)
            length(3)
            unit(0)
            turned(0)
            turned(1)
            unit(1)
            norm.odd_tiles(act, 2)
            gelu(4)
            gelu(5)
            turned(2)
            length(4)
            length(5)
            turned(3)
            norm.odd_tiles(act, 3)
            gelu(6)
            gelu(7)
            unit(2)
            turned(4)
            length(6)
            length(7)
            unit(3)
            turned(5)
            novelty(0)
            turned(6)
            turned(7)
            novelty(1)

        @block.tensor
        def _(pe):
            def turn(b):
                pe.wait_ge(s_onv, TPB // 2 * (b + 1))
                pe.wait_ge(s_ona, TPB // 2 * (b + 1))
                if b >= 2:
                    pe.wait_ge(s_ot, b - 1)
                for j in range(TPB):
                    last = nc.tensor.transpose(psT[b % 2][:, j * P:(j + 1) * P], on[:, b * TPB + j, :],
                                               k.IDENT[:, :])
                last.then_inc(s_tr, 1)

            turn(0)
            pe.wait_ge(s_ema, 2)
            for b in range(B):
                if b + 1 < B:
                    turn(b + 1)
                pe.wait_ge(s_ot, b + 1)
                for j in range(TPB):
                    t, n = b * TPB + j, (j + 1) * P
                    if b >= 1:
                        pe.wait_ge(s_max, t - TPB + 1)
                    mine = ont[b % 2][:, 1 + j * P:1 + (j + 1) * P]
                    nc.tensor.matmul(psM[j][:, 0:n], mine, ont[b % 2][:, 0:n], start=True, stop=False)
                    nc.tensor.matmul(psM[j][:, n - P + 1:n], k.IDENTB[:, :], k.PAST[:, 0:P - 1], start=False,
                                     stop=True).then_inc(s_sim, 1)


W1_LOADS = 6 * 16


def load_weights1(sp, k, dram, e):
    for w, full, rest in ((dram.w0k, COL_W0, COL_REST), (dram.w1k, COL_W1, COL_REST + P // 2)):
        of = w[bass.ds(e, 1), :, :].rearrange("a d f -> (a d) f")
        sp.dma_start(k.RAW[:, full:full + FULL1], of[:, 0:FULL1]).then_inc(k.s_w1, 16)
        sp.dma_start(k.RAW[:, rest:rest + HREST], of[:, FULL1:H1]).then_inc(k.s_w1, 16)
    sp.dma_start(k.RAW[:, COL_WO:COL_WO + FULL1].rearrange("p (c d) -> p c d", c=HC1 - 1),
                 dram.wok[bass.ds(e, 1), 0:FULL1, :].rearrange("a (c p) d -> p (a c) d", p=P)).then_inc(k.s_w1, 16)
    sp.dma_start(k.RAW[0:HREST, COL_WO + FULL1:COLS1],
                 dram.wok[bass.ds(e, 1), FULL1:H1, :].rearrange("a p d -> (a p) d")).then_inc(k.s_w1, 16)


def route1(nc, st, k, dram):
    w = Work(st)
    mask = st.sb("mask", [P, 2, NT, E], BF16)
    cnt = st.sb("cnt", [P, B, E])
    pos = st.sb("pos", [P, 2, NT])
    rank = st.sb("rank", [P, 2, NT])
    val = st.sb("val", [P, 2, NT])
    kb = st.sb("kb", [P, 2, NT])
    gt = st.sb("gt", [P, 2, NT])
    slot = st.sb("slot", [P, 2, NT])
    rec = st.sb("rec", [P, 2, NT, 6, E], BF16)
    parts = st.sb("parts", [P, 2, NT, 3], BF16)
    part = st.sb("part", [P, 2, NT])
    hot = st.sb("hot", [P, 2, NT, CAP1], BF16)
    got = st.sb("got", [P, B, 6, E])
    row = st.sb("row", [P, 2, B * E])
    psM = st.ps("psM", [P, 512])
    s_hot = st.sem("hot")
    s_rec = st.sem("rec")
    s_zero = st.sem("zero")
    s_use = st.sem("use")
    psC = st.ps("psC", [P, 2, NT * E])
    psN = st.ps("psN", [P, 512])
    s_vec = st.sem("vec")
    s_exp = st.sem("exp")
    s_cnt = st.sem("cnt")

    def clear():
        nc.gpsimd.memset(k.RAW[:, :], 0.0).then_inc(s_zero, 1)

    def gpsimd(pool):
        pool.wait_ge(s_vec, 34)
        for c in range(2):
            nc.gpsimd.tensor_tensor(rec[:, c, :, 0:3, :],
                                    mask[:, c, :, :].unsqueeze(2).to_broadcast([P, NT, 3, E]),
                                    k.IDS[:, :, :].unsqueeze(3).to_broadcast([P, NT, 3, E]), ALU.mult)\
              .then_inc(s_rec, 1)

        for n in range(3):
            pool.wait_ge(k.s_wh, n + 1)
            nc.gpsimd.tensor_tensor(k.wl[0][:, PIECES1[n]], k.RAW[:, PIECES1[n]],
                                    k.wh[0][:, PIECES1[n]].bitcast(F32), ALU.subtract).then_inc(k.s_wl, 1)

    def sync(sp):
        sp.wait_ge(s_zero, 1)
        load_weights1(sp, k, dram, 0)
        sp.wait_ge(k.s_rows, 16 * B)

    def exponent(act, h):
        act.wait_ge(s_vec, 17 * h + 2)
        nc.scalar.activation(w.q[:, HALVES[h], :], w.p[:, HALVES[h], :], ACT.Exp).then_inc(s_exp, 1)

    def scalar(act):
        act.wait_ge(k.s_w1, W1_LOADS)
        for n in range(3):
            nc.scalar.copy(k.wh[0][:, PIECES1[n]], k.RAW[:, PIECES1[n]]).then_inc(k.s_wh, 1)

    def vector(dve):
        link = Chain(dve, s_vec)
        for h in range(2):
            c = HALVES[h]
            dve.wait_ge(k.s_lg, B // 2 * (h + 1))
            softmax_over_experts(nc, dve, link, k, w, h, s_exp)
            first_largest(nc, link, k, w, h, w.p, val[:, 0, :], rank[:, 0, :], mask[:, 0, :, :])
            link(nc.vector.tensor_tensor(w.s[:, c, :], w.q[:, c, :], over_experts(rank[:, 0, :], c), ALU.not_equal))
            link(nc.vector.tensor_tensor(w.s[:, c, :], w.s[:, c, :], w.p[:, c, :], ALU.mult))
            first_largest(nc, link, k, w, h, w.s, val[:, 1, :], rank[:, 1, :], mask[:, 1, :, :])
        assert link.n == 34
        dve.wait_ge(s_cnt, 1)
        link(nc.vector.tensor_scalar(cnt[:, :, :], psN[:, 0:B * E].rearrange("p (g e) -> p g e", e=E),
                                     float(CAP1), None, ALU.min))
        link(nc.vector.tensor_tensor(w.q[:, :, :], psC[:, 0, :].rearrange("p (t e) -> p t e", e=E),
                                     mask[:, 0, :, :], ALU.mult))
        link(nc.vector.tensor_reduce(pos[:, 0, :], w.q[:, :, :], AX, ALU.add))
        link(nc.vector.tensor_tensor(w.q[:, :, :].rearrange("p (g j) e -> p g j e", j=TPB),
                                     psC[:, 1, :].rearrange("p (g j e) -> p g j e", j=TPB, e=E),
                                     cnt[:, :, :].unsqueeze(2).to_broadcast([P, B, TPB, E]), ALU.add))
        link(nc.vector.tensor_tensor(w.q[:, :, :], w.q[:, :, :], mask[:, 1, :, :], ALU.mult))
        link(nc.vector.tensor_reduce(pos[:, 1, :], w.q[:, :, :], AX, ALU.add))
        link(nc.vector.tensor_scalar(kb[:, :, :], pos[:, :, :], CAP1 + 0.5, 0.5, ALU.is_le, ALU.mult))
        link(nc.vector.tensor_tensor(gt[:, :, :], kb[:, :, :], val[:, :, :], ALU.mult))
        link(nc.vector.tensor_scalar(kb[:, :, :], gt[:, :, :], 0.0, float(SKIP), ALU.is_equal, ALU.mult))
        link(nc.vector.scalar_tensor_tensor(out=flat(slot[:, :, :]), in0=flat(kb[:, :, :]), scalar=-1.0,
                                            in1=flat(pos[:, :, :]), op0=ALU.add, op1=ALU.add))
        link(nc.vector.tensor_copy(parts[:, :, :, 0], gt[:, :, :]))
        link(nc.vector.tensor_tensor(part[:, :, :], gt[:, :, :], parts[:, :, :, 0], ALU.subtract))
        link(nc.vector.tensor_copy(parts[:, :, :, 1], part[:, :, :]))
        link(nc.vector.tensor_tensor(part[:, :, :], part[:, :, :], parts[:, :, :, 1], ALU.subtract))
        link(nc.vector.tensor_copy(parts[:, :, :, 2], part[:, :, :]))
        for c in range(2):
            nc.vector.tensor_tensor(rec[:, c, :, 3:6, :],
                                    mask[:, c, :, :].unsqueeze(2).to_broadcast([P, NT, 3, E]),
                                    parts[:, c, :, :].unsqueeze(3).to_broadcast([P, NT, 3, E]), ALU.mult)\
              .then_inc(s_rec, 1)
        for t in range(NT):
            for c in range(2):
                nc.vector.tensor_scalar(hot[:, c, t, :], k.IOTA[:, :], slot[:, c, t:t + 1], None,
                                        ALU.is_equal).then_inc(s_hot, 1)
        dve.wait_ge(s_use, 1)
        link(nc.vector.tensor_copy(got[:, :, :, :].rearrange("p g a e -> p (g a e)"), psM[:, 0:6 * B * E]))
        field = lambda a: got[:, :, a, :]
        by_group = lambda v: v.rearrange("p (g e) -> p g e", e=E)
        link(nc.vector.scalar_tensor_tensor(out=by_group(row[:, 0, :]), in0=field(0), scalar=float(P),
                                            in1=field(1), op0=ALU.mult, op1=ALU.add))
        link(nc.vector.tensor_scalar(by_group(row[:, 1, :]), field(2), -float(SKIP), float(SKIP),
                                     ALU.mult, ALU.add))
        link(nc.vector.tensor_tensor(row[:, 1, :], row[:, 1, :], row[:, 0, :], ALU.add))
        link(nc.vector.tensor_copy(k.SRC_ROW[:, :], row[:, 0, :]))
        link(nc.vector.tensor_copy(k.DST_ROW[:, :], row[:, 1, :]))
        link(nc.vector.tensor_tensor(by_group(k.SGATE[:, :]), field(3), field(4), ALU.add))
        link(nc.vector.tensor_tensor(by_group(k.SGATE[:, :]), by_group(k.SGATE[:, :]), field(5), ALU.add))

    def tensor(pe):
        pe.wait_ge(s_vec, 34)
        for c in range(2):
            out = psC[:, c, :].rearrange("p (g j e) -> p g j e", j=TPB, e=E)
            m = mask[:, c, :, :].rearrange("p (g j) e -> p g j e", j=TPB)
            nc.tensor.matmul(psC[:, c, :], k.TRIU[:, :], mask[:, c, :, :].rearrange("p t e -> p (t e)"),
                             start=True, stop=False, skip_group_check=True)
            for s in range(1, TPB):
                nc.tensor.matmul(out[:, :, s:TPB, :], k.ONESB[:, :], m[:, :, 0:TPB - s, :], start=False,
                                 stop=(s == TPB - 1), skip_group_check=True)
        for j in range(TPB):
            last = nc.tensor.matmul(psN[:, 0:B * E], k.ONESB[:, :],
                                    mask[:, 0, :, :].rearrange("p (g j) e -> p g j e", j=TPB)[:, :, j, :],
                                    start=(j == 0), stop=(j == TPB - 1), skip_group_check=True)
        last.then_inc(s_cnt, 1)
        pe.wait_ge(s_rec, 4)
        for t in range(NT):
            g = t // TPB
            for c in range(2):
                n = 2 * t + c
                pe.wait_ge(s_hot, n + 1)
                last = nc.tensor.matmul(psM[:, g * 6 * E:(g + 1) * 6 * E], hot[:, c, t, :],
                                        rec[:, c, t, :, :].rearrange("p a e -> p (a e)"),
                                        start=(n % (2 * TPB) == 0), stop=(n % (2 * TPB) == 2 * TPB - 1),
                                        skip_group_check=True)
        last.then_inc(s_use, 1)

    r = Names()
    r.exponent, r.clear, r.scalar, r.vector, r.gpsimd, r.sync, r.tensor = (
        exponent, clear, scalar, vector, gpsimd, sync, tensor)
    return r


def experts1(nc, name, k, dram, delta):
    with ExitStack() as ctx:
        st = Stage(nc, ctx, name)
        raw, wh, wl = k.RAW, k.wh, k.wl
        xe = [st.sb(f"xe{h}", [P, HALF, D]) for h in range(2)]
        xh = [st.sb(f"xh{h}", [P, 512], F32R) for h in range(2)]
        xl = [st.sb(f"xl{h}", [P, 512], F32R) for h in range(2)]
        ge = [st.sb(f"ge{c}", [P, 512]) for c in range(2)]
        hid = [st.sb(f"hid{c}", [P, 512]) for c in range(2)]
        hh = [st.sb(f"hh{c}", [P, 512], F32R) for c in range(3)]
        hl = [st.sb(f"hl{c}", [P, 512], F32R) for c in range(3)]
        eot = st.sb("eot", [P, 512])
        eo = [st.sb(f"eo{h}", [P, HALF, D]) for h in range(2)]
        psA = [st.ps(f"psA{c}", [P, 512]) for c in range(2)]
        psB = [st.ps(f"psB{c}", [P, 512]) for c in range(2)]
        psY = [st.ps(f"psY{h}", [P, 512]) for h in range(2)]
        psX = st.ps("psX", [P, 512])
        psO = st.ps("psO", [P, 512])
        s_wh, s_wl = k.s_wh, k.s_wl
        s_xe = [st.sem(f"xe{h}") for h in range(2)]
        s_tr = st.sem("tr")
        s_xh = st.sem("xh")
        s_xl = st.sem("xl")
        s_ua = st.sem("ua")
        s_ub = st.sem("ub")
        s_ge = st.sem("ge")
        s_hid = st.sem("hid")
        s_hh = st.sem("hh")
        s_hl = st.sem("hl")
        s_dn = st.sem("dn")
        s_et = st.sem("et")
        s_op = st.sem("op")
        s_eo = st.sem("eo")
        s_sc = [st.sem(f"sc{h}") for h in range(2)]
        block = st.block()
        f32 = lambda ap: ap.bitcast(F32)

        def rounds(eng, body, drain):
            def one(q):
                for u in range(2):
                    for h in range(2):
                        body(4 * q + 2 * u + h, 2 * q + u, u, h,
                             isinstance(q, int) and q == E // 2 - 1 and u == 1 and h == 1)
            one(0)
            with eng.Fori(1, E // 2 - 1) as q:
                one(q)
            one(E // 2 - 1)
            drain()

        @block.sync
        def _(sp):
            with sp.Fori(1, E) as e:
                sp.wait_ge(s_wl, 3 * e)
                load_weights1(sp, k, dram, e)

        @block.gpsimd
        def _(pool):
            def gather(n):
                e, h = n // 2, n % 2
                if n >= 2:
                    pool.wait_ge(s_tr, n - 1)
                for g in range(HALF):
                    col = (h * HALF + g) * E + e
                    nc.gpsimd.indirect_dma_start(
                        out=xe[h][:, g, :], out_offset=None, in_=dram.normed[:, :],
                        in_offset=bass.IndirectOffsetOnAxis(ap=k.SRC_ROW[:, col:col + 1], axis=0))\
                      .then_inc(s_xe[h], 16)

            def scatter(n):
                e, h = n // 2, n % 2
                if n == 0 and k.s_base is not None:
                    pool.wait_ge(k.s_base, 16 * len(GROUPS))
                if e >= 1:
                    pool.wait_ge(s_sc[h], 16 * HALF * e)
                for g in range(HALF):
                    col = (h * HALF + g) * E + e
                    pool.wait_ge(s_eo, HALF * n + g + 1)
                    nc.gpsimd.indirect_dma_start(
                        out=delta[:, :], out_offset=bass.IndirectOffsetOnAxis(ap=k.DST_ROW[:, col:col + 1], axis=0),
                        in_=eo[h][:, g, :], in_offset=None, bounds_check=B * T - 1, oob_is_err=False,
                        compute_op=ALU.add).then_inc(s_sc[h], 16)

            AHEAD = 4
            pool.wait_ge(k.s_rows, 16 * B)
            for n in range(AHEAD):
                gather(n)
            for n in range(2 * E):
                if n + AHEAD < 2 * E:
                    gather(n + AHEAD)
                scatter(n)
            for h in range(2):
                pool.wait_ge(s_sc[h], 16 * HALF * E)

        @block.tensor
        def _(pe):
            def turn(n, e, h):
                pe.wait_ge(s_xe[h], 16 * HALF * (e + 1))
                after(pe, s_xl, n)
                for g in range(HALF):
                    last = nc.tensor.transpose(psX[:, g * CAP1:(g + 1) * CAP1], xe[h][:, g, :], k.IDENT[:, :])
                last.then_inc(s_tr, 1)

            def three(out, col, u, mh, ml, rows=P, first=True, last=True):
                cs = slice(col, col + P)
                nc.tensor.matmul(out, wh[u][0:rows, cs], mh, start=first, stop=False)
                nc.tensor.matmul(out, wh[u][0:rows, cs], ml, start=False, stop=False)
                return nc.tensor.matmul(out, wl[u][0:rows, cs], mh, start=False, stop=last)

            def down(n, c, u, h):
                rows = P if c < HC1 - 1 else P // 2
                pe.wait_ge(s_hl, HC1 * n + c + 1)
                if c == 0:
                    after(pe, s_et, n - 1)
                three(psY[h][:, :], COL_WO + c * P, u, hh[c % 3][0:rows, :], hl[c % 3][0:rows, :], rows,
                      c == 0, c == HC1 - 1).then_inc(s_dn, 1)

            def turn_back(n):
                pe.wait_ge(s_et, n + 1)
                after(pe, s_eo, HALF * n)
                for g in range(HALF):
                    last = nc.tensor.transpose(psO[:, g * P:(g + 1) * P], eot[:, g * CAP1:(g + 1) * CAP1],
                                               k.IDENT[:, :])
                last.then_inc(s_op, 1)

            def unit(n, e, u, h, last):
                pe.wait_ge(s_xl, n + 1)
                pe.wait_ge(s_wl, 3 * e + 3)
                for c in range(HC1):
                    after(pe, s_hid, HC1 * n + c - 1)
                    col = c * P if c < HC1 - 1 else COL_REST
                    three(psA[c % 2][:, :], col, u, xh[h][:, :], xl[h][:, :]).then_inc(s_ua, 1)
                    if c < HC1 - 1:
                        three(psB[c % 2][:, :], COL_W1 + c * P, u, xh[h][:, :], xl[h][:, :]).then_inc(s_ub, 1)
                    if c >= 2:
                        down(n, c - 2, u, h)
                    elif not (isinstance(n, int) and n == 0):
                        down(n - 1, HC1 - 2 + c, u if h else 1 - u, 1 - h)
                    if c == 2 and not last:
                        turn(n + 1, e + h, 1 - h)
                    if c == 4 and not (isinstance(n, int) and n == 0):
                        turn_back(n - 1)

            def drain():
                n = 2 * E - 1
                down(n, HC1 - 2, 1, 1)
                down(n, HC1 - 1, 1, 1)
                turn_back(n)

            turn(0, 0, 0)
            rounds(pe, unit, drain)

        @block.scalar
        def _(act):
            def weight(e, n, u):
                if n == 0:
                    act.wait_ge(k.s_w1, W1_LOADS * (e + 1))
                    after(act, s_dn, HC1 * 2 * (e - 1))
                nc.scalar.copy(wh[u][:, PIECES1[n]], raw[:, PIECES1[n]]).then_inc(s_wh, 1)

            def turned(n, h):
                after(act, s_ua, HC1 * (n - 1))
                act.wait_ge(s_tr, n + 1)
                nc.scalar.copy(xh[h][:, :], psX[:, :]).then_inc(s_xh, 1)

            def high(n, c):
                act.wait_ge(s_hid, HC1 * n + c + 1)
                after(act, s_dn, HC1 * n + c - 2)
                rows = P if c < HC1 - 1 else P // 2
                nc.scalar.copy(hh[c % 3][0:rows, :], hid[c % 2][0:rows, :]).then_inc(s_hh, 1)

            def result(n, h):
                act.wait_ge(s_dn, HC1 * (n + 1))
                after(act, s_op, n)
                nc.scalar.copy(eot[:, :], psY[h][:, :]).then_inc(s_et, 1)

            def gated(n, e, h):
                act.wait_ge(s_op, n + 1)
                after(act, s_sc[h], 16 * HALF * e)
                for g in range(HALF):
                    col = (h * HALF + g) * E + e
                    nc.scalar.activation(eo[h][:, g, :], psO[:, g * P:(g + 1) * P], ACT.Identity,
                                         scale=k.SGATE[:, bass.ds(col, 1)]).then_inc(s_eo, 1)

            def unit(n, e, u, h, last):
                first = isinstance(n, int) and n == 0
                for c in range(HC1):
                    rows = P if c < HC1 - 1 else P // 2
                    act.wait_ge(s_ua, HC1 * n + c + 1)
                    after(act, s_hid, HC1 * n + c - 1)
                    nc.scalar.activation(ge[c % 2][0:rows, :], psA[c % 2][0:rows, :], ACT.Gelu_apprx_tanh)\
                      .then_inc(s_ge, 1)
                    if c >= 1:
                        high(n, c - 1)
                    elif not first:
                        high(n - 1, HC1 - 1)
                    if c == 2 and not first:
                        result(n - 1, 1 - h)
                    if c == 3 and not last:
                        turned(n + 1, 1 - h)
                    if c == 5 and not first:
                        gated(n - 1, e + h - 1, 1 - h)
                    if not (isinstance(e, int) and e == E - 1):
                        if h == 0 and c == 4:
                            weight(e + 1, 0, 1 - u)
                        if h == 1 and c in (1, 4):
                            weight(e + 1, 1 + c // 4, 1 - u)

            def drain():
                high(2 * E - 1, HC1 - 1)
                result(2 * E - 1, 1)
                gated(2 * E - 1, E - 1, 1)

            turned(0, 0)
            rounds(act, unit, drain)

        @block.vector
        def _(dve):
            def weight(e, n, u):
                dve.wait_ge(s_wh, 3 * e + n + 1)
                nc.vector.tensor_tensor(wl[u][:, PIECES1[n]], raw[:, PIECES1[n]], f32(wh[u][:, PIECES1[n]]),
                                        ALU.subtract).then_inc(s_wl, 1)

            def turned(n, h):
                dve.wait_ge(s_xh, n + 1)
                nc.vector.tensor_tensor(xl[h][:, :], psX[:, :], f32(xh[h][:, :]), ALU.subtract).then_inc(s_xl, 1)

            def low(n, c):
                dve.wait_ge(s_hh, HC1 * n + c + 1)
                rows = slice(0, P if c < HC1 - 1 else P // 2)
                nc.vector.tensor_tensor(hl[c % 3][rows, :], hid[c % 2][rows, :], f32(hh[c % 3][rows, :]),
                                        ALU.subtract).then_inc(s_hl, 1)

            def unit(n, e, u, h, last):
                first = isinstance(n, int) and n == 0
                for c in range(HC1):
                    after(dve, s_hl, HC1 * n + c - 1)
                    dve.wait_ge(s_ge, HC1 * n + c + 1)
                    if c < HC1 - 1:
                        dve.wait_ge(s_ub, (HC1 - 1) * n + c + 1)
                        nc.vector.tensor_tensor(hid[c % 2][:, :], ge[c % 2][:, :], psB[c % 2][:, :], ALU.mult)\
                          .then_inc(s_hid, 1)
                    else:
                        half = P // 2
                        nc.vector.tensor_tensor(hid[c % 2][0:half, :], ge[c % 2][0:half, :], psA[c % 2][half:P, :],
                                                ALU.mult).then_inc(s_hid, 1)
                    if c >= 1:
                        low(n, c - 1)
                    elif not first:
                        low(n - 1, HC1 - 1)
                    if c == 3 and not last:
                        turned(n + 1, 1 - h)
                    if not (isinstance(e, int) and e == E - 1):
                        if h == 0 and c == 4:
                            weight(e + 1, 0, 1 - u)
                        if h == 1 and c in (1, 4):
                            weight(e + 1, 1 + c // 4, 1 - u)

            def drain():
                low(2 * E - 1, HC1 - 1)

            turned(0, 0)
            rounds(dve, unit, drain)


def attention1(nc, name, k, delta):
    with ExitStack() as ctx:
        st = Stage(nc, ctx, name)
        groups = [slice(ch, NT, TPB) for ch in range(NCH)]
        xn = st.sb("xn", [P, NT, D])
        XT = st.sb("XT", [P, NCH, B, CH])
        D0 = [st.sb(f"D0{u}", [P, CH + 1, B, 3]) for u in range(2)]
        D1 = [st.sb(f"D1{u}", [P, CH + 1, B, 3]) for u in range(2)]
        Z = [st.sb(f"Z{u}", [P, CH + 1, B]) for u in range(2)]
        R = st.sb("R", [P, CH, B])
        S = [st.sb(f"S{u}", [P, CH + 1, B, 3]) for u in range(2)]
        HB = B // 2
        psG = [[st.ps(f"ps{n}{q}", [P, 512]) for q in range(2)] for n in "czr"]
        psO = [st.ps(f"psO{q}", [P, 512]) for q in range(2)]
        s_y = [st.sem(f"y{g}") for g in range(NCH)]
        s_f = st.sem("f")
        s_bn = st.sem("bn")
        s_mv = st.sem("mv")
        s_var = st.sem("var")
        s_std = st.sem("std")
        s_rs = st.sem("rs")
        s_nb = st.sem("nb")
        s_xv = st.sem("xv")
        s_xn = st.sem("xn")
        s_xtr = st.sem("xtr")
        s_xt = st.sem("xt")
        s_init = st.sem("init")
        s_pj = st.sem("pj")
        s_ev = st.sem("ev")
        s_c = st.sem("c")
        s_ru = st.sem("ru")
        s_a = st.sem("a")
        s_hy = st.sem("hy")
        s_tr = st.sem("tr")
        s_x = st.sem("x")
        y = st.sb("y", [P, NT, D])
        block = st.block()
        STEPS = CH + 1

        def gate_piece(act, ch, n, b):
            u = ch % 2
            src = psG[n][b // HB][:, (b % HB) * CH:(b % HB + 1) * CH]
            bias = k.COLS[:, 3 + n:4 + n]
            if n == 0:
                out, func = D1[u][:, 0:CH, b, 2], ACT.Identity
            elif n == 1:
                out, func = Z[u][:, 0:CH, b], ACT.Sigmoid
            else:
                out, func = R[:, :, b], ACT.Sigmoid
            nc.scalar.activation(out, src, func, bias=bias).then_inc(s_ev, 1)

        PIECES = [(n, b) for n in (1, 2, 0) for b in range(B)]

        @block.sync
        def _(sp):
            for g, group in enumerate(groups):
                sp.dma_start(y[:, group, :], delta.rearrange("(t p) d -> p t d", p=P)[:, group, :])\
                  .then_inc(s_y[g], 16)

        @block.gpsimd
        def _(pool):
            ts = nc.gpsimd.tensor_scalar
            link = Chain(pool, s_mv)
            for g, group in enumerate(groups):
                pool.wait_ge(s_bn, B * (g + 1))
                mean_and_variance(nc, k, link, group, s_var)
                if g == 0:
                    pool.wait_ge(s_rs, 1)
                else:
                    pool.wait_ge(s_var, g + 1)
                    inverse_root(nc.gpsimd, link, k.RSTD[:, group], k.VAR[:, group], k.STD[:, group], k.DIF[:, group], False)
                nc.gpsimd.tensor_tensor(k.NBIAS[:, group], k.BOTH[:, group], k.RSTD[:, group], ALU.mult)\
                  .then_inc(s_nb, 1)
                if g >= 1:
                    u = g % 2
                    pool.wait_ge(s_ev, len(PIECES) * g + B)
                    ts(D1[u][:, 1:CH + 1, :, 0], Z[u][:, 0:CH, :], -1.0, 1.0, ALU.mult, ALU.add).then_inc(s_ru, 1)
                    ts(D0[u][:, 0:CH, :, 2], R[:, :, :], k.COLS[:, 0:1], None, ALU.mult).then_inc(s_ru, 1)

        @block.tensor
        def _(pe):
            def turn(g):
                if g >= 1:
                    pe.wait_ge(s_c, B)
                    pe.wait_ge(s_ev, len(PIECES) * g - B)
                pe.wait_ge(s_xv, HB)
                pe.wait_ge(s_xn, B * g + HB)
                for q in range(2):
                    for j in range(HB):
                        t = (q * HB + j) * TPB + g
                        last = nc.tensor.transpose(psG[0][q][:, j * P:(j + 1) * P], xn[:, t, :], k.IDENT[:, :])
                    last.then_inc(s_xtr, 1)

            def project(g):
                pe.wait_ge(s_xt, 2 * (g + 1))
                for n in (1, 2, 0):
                    for q in range(2):
                        last = nc.tensor.matmul(psG[n][q][:, :], k.WT[:, n * P:(n + 1) * P],
                                                XT[:, g, q * HB:(q + 1) * HB, :], start=True, stop=True)
                    last.then_inc(s_pj, 1)

            turn(0)
            project(0)
            for ch in range(NCH):
                if ch + 1 < NCH:
                    turn(ch + 1)
                    project(ch + 1)
                pe.wait_ge(s_a, (ch + 1) * STEPS)
                if ch >= 1:
                    pe.wait_ge(s_x, B * ch)
                for b in range(B):
                    last = nc.tensor.transpose(psO[b // HB][:, (b % HB) * P:(b % HB + 1) * P],
                                               S[ch % 2][:, 1:CH + 1, b, 1], k.IDENT[:, :])
                last.then_inc(s_tr, 1)

        @block.scalar
        def _(act):
            def normed(g, b):
                if b == 0:
                    act.wait_ge(s_nb, g + 1)
                t = b * TPB + g
                nc.scalar.activation(xn[:, t, :], k.X[:, t, :], ACT.Identity, scale=k.RSTD[:, t:t + 1],
                                     bias=k.NBIAS[:, t:t + 1]).then_inc(s_xn, 1)

            def turned(g, q):
                act.wait_ge(s_xtr, 2 * g + q + 1)
                nc.scalar.activation(XT[:, g, q * HB:(q + 1) * HB, :],
                                     psG[0][q][:, :].rearrange("p (b t) -> p b t", b=HB), ACT.Identity,
                                     bias=k.COLS[:, 2:3], scale=k.COLS[:, 1:2]).then_inc(s_xt, 1)

            def gates(g, i):
                if i % B == 0:
                    act.wait_ge(s_pj, 3 * g + i // B + 1)
                if i == 0 and g >= 1:
                    act.wait_ge(s_ru, 2 * g)
                gate_piece(act, g, *PIECES[i])

            def aside(g, r):
                if 32 <= r < 40:
                    normed(g, r - 32)
                elif r in (48, 50):
                    turned(g, (r - 48) // 2)
                elif 64 <= r < 112 and r % 2 == 0:
                    gates(g, (r - 64) // 2)

            act.wait_ge(s_var, 1)
            nc.scalar.activation(k.STD[:, groups[0]], k.VAR[:, groups[0]], ACT.Sqrt).then_inc(s_std, 1)
            for b in range(0, HB):
                normed(0, b)
            for q in range(2):
                turned(0, q)
            act.wait_ge(s_init, 1)
            for i in range(2 * B):
                gates(0, i)
            for ch in range(NCH):
                u = ch % 2
                for r in range(CH):
                    act.wait_ge(s_a, ch * STEPS + r + 1)
                    nc.scalar.activation(D0[u][:, r + 1, :, 1], S[u][:, r, :, 2], ACT.Tanh).then_inc(s_hy, 1)
                    if ch + 1 < NCH:
                        aside(ch + 1, r)

        @block.vector
        def _(dve):
            def fold(g, b):
                if b == 0:
                    dve.wait_ge(s_y[g], 16)
                t = b * TPB + g
                nc.vector.tensor_tensor(k.X[:, t, :], k.X[:, t, :], y[:, t, :], ALU.add).then_inc(s_f, 1)

            def moments(g, b):
                t = b * TPB + g
                dve.wait_ge(s_f, B * g + b + 1)
                nc.vector.bn_stats(k.BN[:, t, :], k.X[:, t, :]).then_inc(s_bn, 1)

            def add_piece(ch, b):
                t = b * TPB + ch
                nc.vector.tensor_tensor(k.X[:, t, :], k.X[:, t, :], psO[b // HB][:, (b % HB) * P:(b % HB + 1) * P],
                                        ALU.add).then_inc(s_x, 1)

            def aside(ch, r):
                if ch + 1 < NCH and 2 <= r < 10:
                    fold(ch + 1, r - 2)
                elif ch + 1 < NCH and 10 <= r < 18:
                    moments(ch + 1, r - 10)
                elif ch >= 1 and 24 <= r < 24 + 8 * B and r % 8 == 0:
                    if r == 24:
                        dve.wait_ge(s_tr, ch)
                    add_piece(ch - 1, (r - 24) // 8)

            for u in range(2):
                nc.vector.memset(D0[u][:, :, :, 0], 0.0)
                nc.vector.memset(D0[u][:, 0, :, 1], 0.0)
                nc.vector.memset(D0[u][:, CH, :, 2], 0.0)
                nc.vector.memset(D1[u][:, 0, :, 0], 0.0)
                nc.vector.memset(D1[u][:, CH, :, 2], 0.0)
            nc.vector.memset(S[1][:, CH, :, 1], 0.0).then_inc(s_init, 1)
            for b in range(B):
                fold(0, b)
            for b in range(B):
                moments(0, b)
            dve.wait_ge(s_std, 1)
            nc.vector.reciprocal(k.RSTD[:, groups[0]], k.STD[:, groups[0]]).then_inc(s_rs, 1)
            dve.wait_ge(s_rs, 1)
            for b in range(HB, B):
                t = b * TPB
                nc.vector.tensor_scalar(xn[:, t, :], k.X[:, t, :], k.MEAN[:, t:t + 1], k.RSTD[:, t:t + 1],
                                        ALU.subtract, ALU.mult).then_inc(s_xv, 1)
            dve.wait_ge(s_ev, B)
            nc.vector.tensor_scalar(D1[0][:, 1:CH + 1, :, 0], Z[0][:, 0:CH, :], -1.0, 1.0, ALU.mult, ALU.add)\
              .then_inc(s_ru, 1)
            dve.wait_ge(s_pj, 3)
            for b in range(B):
                nc.vector.tensor_scalar(D1[0][:, 0:CH, b, 2], psG[0][b // HB][:, (b % HB) * CH:(b % HB + 1) * CH],
                                        k.COLS[:, 3:4], None, ALU.add).then_inc(s_c, 1)
            dve.wait_ge(s_ev, 2 * B)
            nc.vector.tensor_scalar(D0[0][:, 0:CH, :, 2], R[:, :, :], k.COLS[:, 0:1], None, ALU.mult)\
              .then_inc(s_ru, 1)
            dve.wait_ge(s_init, 1)
            for ch in range(NCH):
                u = ch % 2
                if ch == 0:
                    dve.wait_ge(s_c, B)
                dve.wait_ge(s_ev, len(PIECES) * (ch + 1) - B)
                dve.wait_ge(s_ru, 2 * (ch + 1))
                if ch >= 1:
                    dve.wait_ge(s_a, ch * STEPS)
                nc.vector.tensor_copy(D1[u][:, 0, :, 1], S[1 - u][:, CH, :, 1]).then_inc(s_hy, 1)
                for r in range(STEPS):
                    dve.wait_ge(s_hy, ch * (2 * CH + 1) + 2 * r + 1)
                    nc.vector.tensor_tensor_scan(S[u][:, r, :, :].rearrange("p b a -> p (b a)"),
                                                 D0[u][:, r, :, :].rearrange("p b a -> p (b a)"),
                                                 D1[u][:, r, :, :].rearrange("p b a -> p (b a)"), 0.0,
                                                 ALU.mult, ALU.add).then_inc(s_a, 1)
                    if r == CH:
                        break
                    dve.wait_ge(s_a, ch * STEPS + r + 1)
                    nc.vector.tensor_tensor(D1[u][:, r + 1, :, 1], Z[u][:, r, :], S[u][:, r, :, 1], ALU.mult)\
                      .then_inc(s_hy, 1)
                    aside(ch, r)
            dve.wait_ge(s_tr, NCH)
            for b in range(B):
                add_piece(NCH - 1, b)


def macaron(nc, x, ema, log_tau, log_blend, logit_blend_seq, gate_w, gate_b, w1, b1, w2, b2,
            u, W, b, gamma, beta, router_w, w0k, w1k, wok, out):
    dram = Names()
    dram.x, dram.ema, dram.log_tau, dram.log_blend, dram.logit_blend_seq = x, ema, log_tau, log_blend, logit_blend_seq
    dram.gate_w, dram.gate_b, dram.w1, dram.b1, dram.w2, dram.b2 = gate_w, gate_b, w1, b1, w2, b2
    dram.u, dram.W, dram.b, dram.gamma, dram.beta = u, W, b, gamma, beta
    dram.router_w, dram.w0k, dram.w1k, dram.wok = router_w, w0k, w1k, wok
    dram.normed = nc.dram_tensor("normed", (B * T, D), F32).ap()
    dram.delta0 = [nc.dram_tensor(f"delta{n}", (B * T, D), F32).ap() for n in range(2)]
    dram.delta1 = [nc.dram_tensor("delta_b0", (B * T, D), F32).ap()]
    with ExitStack() as ctx:
        st = Stage(nc, ctx, "k")
        k = Names()
        k.X = st.sb("X", [P, NT, D])
        k.ZEROS = st.sb("ZEROS", [P, 16 * D])
        k.BN = st.sb("BN", [P, NT, 6])
        k.MEAN, k.DIF, k.VAR, k.BOTH, k.STD, k.RSTD, k.NBIAS = (
            st.sb(n, [P, NT]) for n in ("MEAN", "DIF", "VAR", "BOTH", "STD", "RSTD", "NBIAS"))
        k.IDENT = st.sb("IDENT", [P, P])
        k.IDENTB = st.sb("IDENTB", [P, P], BF16)
        k.TRIU = st.sb("TRIU", [P, P], BF16)
        k.ONESB = st.sb("ONESB", [P, P], BF16)
        k.ONES = st.sb("ONES", [P, P])
        k.PAST = st.sb("PAST", [P, P], BF16)
        k.FIRST = st.sb("FIRST", [P, NT])
        k.RESET = st.sb("RESET", [P, E * NT])
        k.IOTA = st.sb("IOTA", [P, CAP1], F16)
        k.IDS = st.sb("IDS", [P, NT, 3], BF16)
        k.RANK = st.sb("RANK", [P, E])
        k.GW0 = st.sb("GW0", [P, E])
        k.GB0 = st.sb("GB0", [1, NT, E])
        k.RW1 = st.sb("RW1", [P, E])
        k.B1T = st.sb("B1T", [P, E * FC0])
        k.WT = st.sb("WT", [P, 3 * D])
        k.COLS = st.sb("COLS", [P, 8])
        k.SCAL = st.sb("SCAL", [P, 8])
        k.EMA = st.sb("EMA", [P, 2])
        k.GATE0 = st.sb("GATE0", [P, NT])
        k.SLOT_ROW = st.sb("SLOT_ROW", [P, 2, E], U32)
        k.SRC_ROW = st.sb("SRC_ROW", [P, B * E], U32)
        k.DST_ROW = st.sb("DST_ROW", [P, B * E], U32)
        k.SGATE = st.sb("SGATE", [P, B * E])

        def ffn0(n, **kw):
            with ExitStack() as own:
                held = Stage(nc, own, f"f0{n}")
                k.s_rows = held.sem("rows")
                with ExitStack() as routing:
                    k.psL = [Stage(nc, routing, f"l0{n}").ps(f"psL{h}", [P, 512]) for h in range(2)]
                    k.xn = held.sb("xn", [P, NT, D])
                    normalize(nc, f"n0{n}", k, dram, route0, weights=k.GW0[:, :], rows=dram.normed,
                              bias=flat(k.GB0[0:1, :, :]), **kw)
                experts0(nc, f"e0{n}", k, dram, dram.delta0[n], 32 if n == 0 else 32 * 3)

        def ffn1(n, target, base=None, **kw):
            with ExitStack() as own:
                held = Stage(nc, own, f"f1{n}")
                k.s_rows = held.sem("rows")
                k.s_base = held.sem("base") if base is not None else None
                k.RAW = held.sb("RAW", [P, COLS1])
                k.wh, k.wl = ([held.sb(f"w{x}{u}", [P, COLS1], F32R) for u in range(2)] for x in "hl")
                k.s_w1 = held.sem("w1")
                k.s_wh = held.sem("wh")
                k.s_wl = held.sem("wl")
                with ExitStack() as routing:
                    k.psL = [Stage(nc, routing, f"l1{n}").ps(f"psL{h}", [P, 512]) for h in range(2)]
                    k.xn = Stage(nc, routing, f"x1{n}").sb("xn", [P, NT, D])
                    normalize(nc, f"n1{n}", k, dram, route1, weights=k.RW1[:, :], rows=dram.normed, base=base, **kw)
                experts1(nc, f"e1{n}", k, dram, target)

        d0, d1, g0 = dram.delta0, dram.delta1, k.GATE0
        stages = [
            lambda: ffn0(0, arrive=k.s_x),
            lambda: attention0(nc, "a0", k, d0[0], g0, [d0[1]] + d1),
            lambda: ffn0(1),
            lambda: ffn1(0, d1[0], delta=d0[1], gate=g0),
            lambda: attention1(nc, "a1", k, d1[0]),
            lambda: ffn1(1, out.rearrange("b t d -> (b t) d"), base=out),
        ]
        Stage.used.clear()
        early = ctx.enter_context(ExitStack())
        held = Stage(nc, early, "w")
        k.W1 = held.sb("W1", [P, E, F0])
        k.W2 = held.sb("W2", [P, E * FC0, D])
        k.B2 = held.sb("B2", [P, E, D])
        setup(nc, k, dram)
        for n, s in enumerate(stages):
            if n == 3:
                early.close()
                recycle(nc)
            s()


_INS = ['L0_attn_x', 'L0_attn_ema_out', 'L0_attn_log_tau', 'L0_attn_log_blend', 'L0_attn_logit_blend_seq',
        'L0_ffn_gate_w', 'L0_ffn_gate_b', 'L0_ffn_w1', 'L0_ffn_b1', 'L0_ffn_w2', 'L0_ffn_b2',
        'L1_attn_u', 'L1_attn_W', 'L1_attn_b', 'L1_attn_gamma', 'L1_attn_beta',
        'L1_ffn_router_w', 'L1_ffn_w0_kernel', 'L1_ffn_w1_kernel', 'L1_ffn_wo_kernel']
_OUT = (B, T, D)


def kernel(**inputs):
    import numpy as _np
    import concourse.bacc as _bacc
    from concourse import mybir as _mybir
    from concourse.bass_utils import run_bass_kernel_spmd as _run

    nc = _bacc.Bacc("TRN2", target_bir_lowering=False, num_devices=1)
    arrays, args = {}, []
    for name in _INS:
        a = _np.ascontiguousarray(inputs[name])
        arrays[f"in_{name}_dram"] = a
        args.append(nc.dram_tensor(f"in_{name}_dram", a.shape, _mybir.dt.from_np(a.dtype), kind="ExternalInput").ap())
    out = nc.dram_tensor("out_0_dram", _OUT, _mybir.dt.float32, kind="ExternalOutput").ap()
    macaron(nc, *args, out)
    r = _run(nc, [arrays], core_ids=[0])
    return r.results[0]["out_0_dram"]
```
